# Optimizing a Trainium2 kernel written in Bass

```python
import numpy as np
import jax
import jax.numpy as jnp

def _softmax(x, axis=-1):
    return jax.nn.softmax(x, axis=axis)

def _gelu(x):
    return jax.nn.gelu(x, approximate=True)

def _silu(x):
    return jax.nn.silu(x)

def _sigmoid(x):
    return jax.nn.sigmoid(x)

def _layernorm(x, axis=-1, eps=1e-05):
    m = jnp.mean(x, axis=axis, keepdims=True)
    v = jnp.var(x, axis=axis, keepdims=True)
    return (x - m) / jnp.sqrt(v + eps)

def _scatter_add(tgt, idx, src, axis=0):
    return tgt.at[idx].add(src)

def _segment_sum(src, seg, n):
    return jax.ops.segment_sum(src, seg, n)
kernel_name = 'mk_lm_tower_d2_tok_ids1024_r4_42d23b'

def setup_inputs(seed: int=0):
    np.random.seed(seed)
    _w = jnp.asarray

    def _rec_inputs():
        import jax
        import jax.numpy as jnp
        _rk = jax.random.key(seed)
        x = jax.random.randint(jax.random.fold_in(_rk, 1), (8, 512), 0, 24991, jnp.int32)
        return x
    x = _rec_inputs()

    def _L0_tok_setup():
        import jax, jax.numpy as jnp
        import numpy as np
        V, R, D = (25000, 64, 256)
        B, S = (8, 512)
        key = jax.random.key(seed)
        k1, k2, k3, k4 = jax.random.split(key, 4)
        input_ids = jax.random.randint(k1, (B, S), 0, V, dtype=jnp.int64 if jax.config.jax_enable_x64 else jnp.int32)
        U = jax.random.normal(k2, (V, R), dtype=jnp.float32)
        s = jax.random.uniform(k3, (R,), dtype=jnp.float32)
        Vt = jax.random.normal(k4, (R, D), dtype=jnp.float32)
        return {'input': input_ids, 'U': U, 's': s, 'Vt': Vt}
    _L0_tok_all = _L0_tok_setup()
    _L0_tok_in = {k: v for k, v in _L0_tok_all.items() if k in ('U', 's', 'Vt')}
    del _L0_tok_all

    def _L0_attn_setup():
        import jax, jax.numpy as jnp
        import numpy as np
        B, T, D, H = (2, 512, 256, 16)
        key = jax.random.key(seed)
        ks = jax.random.split(key, 5)
        s = 0.02
        return {'x': jax.random.normal(ks[0], (B, T, D), dtype=jnp.float32), 'W_qkv': jax.random.normal(ks[1], (3 * D, D), dtype=jnp.float32) * s, 'b_qkv': jnp.zeros((3 * D,), dtype=jnp.float32), 'W_out': jax.random.normal(ks[2], (D, D), dtype=jnp.float32) * s, 'b_out': jnp.zeros((D,), dtype=jnp.float32)}
    _L0_attn_all = _L0_attn_setup()
    _L0_attn_in = {k: v for k, v in _L0_attn_all.items() if k in ('W_qkv', 'b_qkv', 'W_out', 'b_out')}
    del _L0_attn_all

    def _L0_ffn_setup():
        import jax, jax.numpy as jnp
        import numpy as np
        D = 256
        H = 512
        E = 8
        TOP_K = 2
        N_SHARED = 1
        B, S = (2, 256)
        key = jax.random.key(seed)
        ks = jax.random.split(key, 12)
        sc = 0.02
        return {'hidden': jax.random.normal(ks[0], (B, S, D), jnp.float32), 'router_w': jax.random.normal(ks[1], (D, E), jnp.float32) * sc, 'router_b': jnp.zeros((E,), jnp.float32), 'sw1': jax.random.normal(ks[2], (D, H), jnp.float32) * sc, 'sb1': jnp.zeros((H,), jnp.float32), 'sw2': jax.random.normal(ks[3], (H, D), jnp.float32) * sc, 'sb2': jnp.zeros((D,), jnp.float32), 'rw1': jax.random.normal(ks[4], (E, D, H), jnp.float32) * sc, 'rb1': jnp.zeros((E, H), jnp.float32), 'rw2': jax.random.normal(ks[5], (E, H, D), jnp.float32) * sc, 'rb2': jnp.zeros((E, D), jnp.float32)}
    _L0_ffn_all = _L0_ffn_setup()
    _L0_ffn_in = {k: v for k, v in _L0_ffn_all.items() if k in ('router_w', 'router_b', 'sw1', 'sb1', 'sw2', 'sb2', 'rw1', 'rb1', 'rw2', 'rb2')}
    del _L0_ffn_all

    def _L1_attn_setup():
        import jax, jax.numpy as jnp
        import numpy as np

        def _phm(x, A, S, b):
            f = A.shape[0]
            din = f * S.shape[1]
            dout = f * S.shape[2]
            W = jnp.einsum('nij,nkl->ikjl', A, S).reshape(din, dout)
            return x @ W + b

        def _ln(x, g, b, eps=1e-05):
            mu = jnp.mean(x, axis=-1, keepdims=True)
            var = jnp.mean((x - mu) ** 2, axis=-1, keepdims=True)
            return (x - mu) * jax.lax.rsqrt(var + eps) * g + b
        key = jax.random.key(seed)
        ks = jax.random.split(key, 10)
        L, N, E, f = (512, 4, 256, 4)
        p = lambda k, sh: jax.random.normal(k, sh, jnp.float32) * 0.02
        return {'query': jax.random.normal(ks[0], (L, N, E), jnp.float32), 'qA': p(ks[1], (f, f, f)), 'qS': p(ks[2], (f, E // f, E // f)), 'qb': jnp.zeros((E,), jnp.float32), 'kA': p(ks[3], (f, f, f)), 'kS': p(ks[4], (f, E // f, E // f)), 'kb': jnp.zeros((E,), jnp.float32), 'vA': p(ks[5], (f, f, f)), 'vS': p(ks[6], (f, E // f, E // f)), 'vb': jnp.zeros((E,), jnp.float32), 'oA': p(ks[7], (f, f, f)), 'oS': p(ks[8], (f, E // f, E // f)), 'ob': jnp.zeros((E,), jnp.float32), 'g1': jnp.ones((E,), jnp.float32), 'b1': jnp.zeros((E,), jnp.float32), 'g2': jnp.ones((E,), jnp.float32), 'b2': jnp.zeros((E,), jnp.float32)}
    _L1_attn_all = _L1_attn_setup()
    _L1_attn_in = {k: v for k, v in _L1_attn_all.items() if k in ('qA', 'qS', 'qb', 'kA', 'kS', 'kb', 'vA', 'vS', 'vb', 'oA', 'oS', 'ob', 'g1', 'b1', 'g2', 'b2')}
    del _L1_attn_all

    def _L1_ffn_setup():
        import jax, jax.numpy as jnp
        import numpy as np
        IN_F, OUT_F, BLOCK, NBLK = (256, 1024, 64, 16)
        TOPK = NBLK // 4
        key = jax.random.key(seed)
        ks = jax.random.split(key, 7)
        s = 1.0 / np.sqrt(IN_F)
        s2 = 1.0 / np.sqrt(OUT_F)
        return {'x': jax.random.normal(ks[0], (4, 1024, IN_F), jnp.float32), 'router_w': jax.random.uniform(ks[1], (NBLK, IN_F), jnp.float32, -s, s), 'router_b': jax.random.uniform(ks[2], (NBLK,), jnp.float32, -s, s), 'w1': jax.random.uniform(ks[3], (OUT_F, IN_F), jnp.float32, -s, s), 'b1': jax.random.uniform(ks[4], (OUT_F,), jnp.float32, -s, s), 'w2': jax.random.uniform(ks[5], (IN_F, OUT_F), jnp.float32, -s2, s2), 'b2': jax.random.uniform(ks[6], (IN_F,), jnp.float32, -s2, s2)}
    _L1_ffn_all = _L1_ffn_setup()
    _L1_ffn_in = {k: v for k, v in _L1_ffn_all.items() if k in ('router_w', 'router_b', 'w1', 'b1', 'w2', 'b2')}
    del _L1_ffn_all
    return {'x': x, 'L0_tok_U': _L0_tok_in['U'], 'L0_tok_s': _L0_tok_in['s'], 'L0_tok_Vt': _L0_tok_in['Vt'], 'L0_attn_W_qkv': _L0_attn_in['W_qkv'], 'L0_attn_b_qkv': _L0_attn_in['b_qkv'], 'L0_attn_W_out': _L0_attn_in['W_out'], 'L0_attn_b_out': _L0_attn_in['b_out'], 'L0_ffn_router_w': _L0_ffn_in['router_w'], 'L0_ffn_router_b': _L0_ffn_in['router_b'], 'L0_ffn_sw1': _L0_ffn_in['sw1'], 'L0_ffn_sb1': _L0_ffn_in['sb1'], 'L0_ffn_sw2': _L0_ffn_in['sw2'], 'L0_ffn_sb2': _L0_ffn_in['sb2'], 'L0_ffn_rw1': _L0_ffn_in['rw1'], 'L0_ffn_rb1': _L0_ffn_in['rb1'], 'L0_ffn_rw2': _L0_ffn_in['rw2'], 'L0_ffn_rb2': _L0_ffn_in['rb2'], 'L1_attn_qA': _L1_attn_in['qA'], 'L1_attn_qS': _L1_attn_in['qS'], 'L1_attn_qb': _L1_attn_in['qb'], 'L1_attn_kA': _L1_attn_in['kA'], 'L1_attn_kS': _L1_attn_in['kS'], 'L1_attn_kb': _L1_attn_in['kb'], 'L1_attn_vA': _L1_attn_in['vA'], 'L1_attn_vS': _L1_attn_in['vS'], 'L1_attn_vb': _L1_attn_in['vb'], 'L1_attn_oA': _L1_attn_in['oA'], 'L1_attn_oS': _L1_attn_in['oS'], 'L1_attn_ob': _L1_attn_in['ob'], 'L1_attn_g1': _L1_attn_in['g1'], 'L1_attn_b1': _L1_attn_in['b1'], 'L1_attn_g2': _L1_attn_in['g2'], 'L1_attn_b2': _L1_attn_in['b2'], 'L1_ffn_router_w': _L1_ffn_in['router_w'], 'L1_ffn_router_b': _L1_ffn_in['router_b'], 'L1_ffn_w1': _L1_ffn_in['w1'], 'L1_ffn_b1': _L1_ffn_in['b1'], 'L1_ffn_w2': _L1_ffn_in['w2'], 'L1_ffn_b2': _L1_ffn_in['b2']}

def reference(x, L0_tok_U, L0_tok_s, L0_tok_Vt, L0_attn_W_qkv, L0_attn_b_qkv, L0_attn_W_out, L0_attn_b_out, L0_ffn_router_w, L0_ffn_router_b, L0_ffn_sw1, L0_ffn_sb1, L0_ffn_sw2, L0_ffn_sb2, L0_ffn_rw1, L0_ffn_rb1, L0_ffn_rw2, L0_ffn_rb2, L1_attn_qA, L1_attn_qS, L1_attn_qb, L1_attn_kA, L1_attn_kS, L1_attn_kb, L1_attn_vA, L1_attn_vS, L1_attn_vb, L1_attn_oA, L1_attn_oS, L1_attn_ob, L1_attn_g1, L1_attn_b1, L1_attn_g2, L1_attn_b2, L1_ffn_router_w, L1_ffn_router_b, L1_ffn_w1, L1_ffn_b1, L1_ffn_w2, L1_ffn_b2):
    import jax
    import jax.numpy as jnp

    def _L0_tok_ref(input, U, s, Vt):
        import jax, jax.numpy as jnp
        import numpy as np
        V, R, D = (25000, 64, 256)
        B, S = (8, 512)
        weight = U * s @ Vt
        return weight[input]

    def _L0_attn_ref(x, W_qkv, b_qkv, W_out, b_out):
        import jax, jax.numpy as jnp
        import numpy as np
        B, T, D, H = (2, 512, 256, 16)
        Bx, Tx, Dx = x.shape
        Hh = H
        hd = Dx // Hh
        topk = max(1, int(Tx * 0.3))
        scale = Dx ** (-0.5)
        qkv = x @ W_qkv.T + b_qkv
        qkv = qkv.reshape(Bx, Tx, 3, Hh, hd)
        q = jnp.transpose(qkv[:, :, 0], (0, 2, 1, 3))
        k = jnp.transpose(qkv[:, :, 1], (0, 2, 1, 3))
        v = jnp.transpose(qkv[:, :, 2], (0, 2, 1, 3))
        scores = jnp.einsum('bhid,bhjd->bhij', q, k) * scale
        topk_scores, indices = jax.lax.top_k(scores, topk)
        bi = jnp.arange(Bx)[:, None, None, None]
        hi = jnp.arange(Hh)[None, :, None, None]
        ti = jnp.arange(Tx)[None, None, :, None]
        masked = jnp.full_like(scores, -jnp.inf)
        masked = masked.at[bi, hi, ti, indices].set(topk_scores)
        attn = jax.nn.softmax(masked, axis=-1)
        out = jnp.einsum('bhij,bhjd->bhid', attn, v)
        out = jnp.transpose(out, (0, 2, 1, 3)).reshape(Bx, Tx, Dx)
        return out @ W_out.T + b_out

    def _L0_ffn_ref(hidden, router_w, router_b, sw1, sb1, sw2, sb2, rw1, rb1, rw2, rb2):
        import jax, jax.numpy as jnp
        import numpy as np
        D = 256
        H = 512
        E = 8
        TOP_K = 2
        N_SHARED = 1
        B, S = (2, 256)
        b, s, d = hidden.shape
        T = b * s
        flat = hidden.reshape(T, d)
        router_logits = flat @ router_w + router_b
        router_probs = jax.nn.softmax(router_logits, axis=-1)
        topk_probs, topk_idx = jax.lax.top_k(router_probs, TOP_K)
        weights = jnp.zeros_like(router_probs).at[jnp.arange(T)[:, None], topk_idx].add(topk_probs)
        sh = jax.nn.gelu(flat @ sw1 + sb1, approximate=False)
        shared_out = (sh @ sw2 + sb2) / N_SHARED
        h1 = jax.nn.gelu(jnp.einsum('td,edh->teh', flat, rw1) + rb1[None], approximate=False)
        expert_out = jnp.einsum('teh,ehd->ted', h1, rw2) + rb2[None]
        mixed = jnp.einsum('ted,te->td', expert_out, weights)
        return (shared_out + mixed).reshape(b, s, d)

    def _L1_attn_ref(query, qA, qS, qb, kA, kS, kb, vA, vS, vb, oA, oS, ob, g1, b1, g2, b2):
        import jax, jax.numpy as jnp
        import numpy as np

        def _phm(x, A, S, b):
            f = A.shape[0]
            din = f * S.shape[1]
            dout = f * S.shape[2]
            W = jnp.einsum('nij,nkl->ikjl', A, S).reshape(din, dout)
            return x @ W + b

        def _ln(x, g, b, eps=1e-05):
            mu = jnp.mean(x, axis=-1, keepdims=True)
            var = jnp.mean((x - mu) ** 2, axis=-1, keepdims=True)
            return (x - mu) * jax.lax.rsqrt(var + eps) * g + b
        L, N, E = query.shape
        H = 16
        D = E // H
        eps = 1e-06
        key_raw = query
        val_raw = query
        qn = _ln(query, g1, b1)
        q = jax.nn.relu(_phm(qn, qA, qS, qb))
        k = jax.nn.relu(_phm(key_raw, kA, kS, kb))
        v = _phm(val_raw, vA, vS, vb)
        resh = lambda t: t.reshape(L, N * H, D).transpose(1, 0, 2)
        q, k, v = (resh(q), resh(k), resh(v))
        idx = np.pi / 2 * jnp.arange(1, L + 1, dtype=query.dtype)[None, :, None] / L
        s, c = (jnp.sin(idx), jnp.cos(idx))
        q_ = jnp.concatenate([q * s, q * c], axis=-1)
        k_ = jnp.concatenate([k * s, k * c], axis=-1)
        kv = jnp.einsum('nld,nlm->ndm', k_, v)
        z = 1.0 / jnp.maximum(jnp.einsum('nld,nd->nl', q_, k_.sum(axis=1)), eps)
        attn = jnp.einsum('nld,ndm->nlm', q_, kv) * z[..., None]
        attn = attn.transpose(1, 0, 2).reshape(L, N, E)
        attn = attn + qn
        out = _ln(attn, g2, b2)
        return _phm(out, oA, oS, ob) + out

    def _L1_ffn_ref(x, router_w, router_b, w1, b1, w2, b2):
        import jax, jax.numpy as jnp
        import numpy as np
        IN_F, OUT_F, BLOCK, NBLK = (256, 1024, 64, 16)
        TOPK = NBLK // 4
        x_shape = x.shape
        xf = x.reshape(-1, IN_F)
        n = xf.shape[0]
        prob = jax.nn.softmax(xf @ router_w.T + router_b, axis=-1)
        _, idx = jax.lax.top_k(prob, TOPK)
        mask = jnp.zeros((n, NBLK), bool).at[jnp.arange(n)[:, None], idx].set(True)
        w1b = w1.reshape(NBLK, BLOCK, IN_F)
        b1b = b1.reshape(NBLK, BLOCK)
        h = jnp.einsum('nd,ibd->nib', xf, w1b) + b1b
        h = jnp.where(mask[:, :, None], h, jnp.zeros((), h.dtype))
        h = jax.nn.relu(h)
        w2b = w2.reshape(IN_F, NBLK, BLOCK)
        y = jnp.einsum('nib,dib->nd', jnp.where(mask[:, :, None], h, 0.0), w2b) + b2
        return y.reshape(x_shape)
    h = _L0_tok_ref(x, L0_tok_U, L0_tok_s, L0_tok_Vt)
    h = h + _L0_attn_ref(_layernorm(h, axis=-1), L0_attn_W_qkv, L0_attn_b_qkv, L0_attn_W_out, L0_attn_b_out)
    h = h + _L0_ffn_ref(_layernorm(h, axis=-1), L0_ffn_router_w, L0_ffn_router_b, L0_ffn_sw1, L0_ffn_sb1, L0_ffn_sw2, L0_ffn_sb2, L0_ffn_rw1, L0_ffn_rb1, L0_ffn_rw2, L0_ffn_rb2)
    h = h + _L1_attn_ref(_layernorm(h, axis=-1), L1_attn_qA, L1_attn_qS, L1_attn_qb, L1_attn_kA, L1_attn_kS, L1_attn_kb, L1_attn_vA, L1_attn_vS, L1_attn_vb, L1_attn_oA, L1_attn_oS, L1_attn_ob, L1_attn_g1, L1_attn_b1, L1_attn_g2, L1_attn_b2)
    h = h + _L1_ffn_ref(_layernorm(h, axis=-1), L1_ffn_router_w, L1_ffn_router_b, L1_ffn_w1, L1_ffn_b1, L1_ffn_w2, L1_ffn_b2)
    return h

_drawn_inputs = setup_inputs


def setup_inputs(seed=0):
    import zlib

    import numpy as np

    out = dict(_drawn_inputs(seed))
    spreads = {'L0_attn_b_qkv': (0.0, 0.8),
     'L0_attn_b_out': (0.0, 0.392),
     'L0_ffn_router_b': (0.0, 0.8),
     'L0_ffn_sb1': (0.0, 0.8),
     'L0_ffn_sb2': (0.0, 0.35),
     'L0_ffn_rb1': (0.0, 0.8),
     'L0_ffn_rb2': (0.0, 0.8),
     'L1_attn_qb': (0.0, 2.0),
     'L1_attn_kb': (0.0, 2.0),
     'L1_attn_vb': (0.0, 0.48),
     'L1_attn_ob': (0.0, 0.48),
     'L1_attn_g1': (1.0, 0.2),
     'L1_attn_b1': (0.0, 0.46),
     'L1_attn_g2': (1.0, 0.2),
     'L1_attn_b2': (0.0, 0.461)}
    factors = {'L0_attn_W_qkv': 8.0,
     'L0_attn_W_out': 6.926,
     'L0_ffn_router_w': 8.0,
     'L0_ffn_sw1': 3.417,
     'L0_ffn_sw2': 3.181,
     'L0_ffn_rw1': 8.0,
     'L0_ffn_rw2': 8.0,
     'L1_attn_qA': 113.523,
     'L1_attn_qS': 115.785,
     'L1_attn_kA': 25.213,
     'L1_attn_kS': 26.609,
     'L1_attn_vA': 8.0,
     'L1_attn_vS': 8.0,
     'L1_attn_oA': 8.0,
     'L1_attn_oS': 8.0,
     'L1_ffn_router_w': 2.882,
     'L1_ffn_router_b': 22.977,
     'L1_ffn_w1': 3.12,
     'L1_ffn_b1': 64.0,
     'L1_ffn_b2': 25.329}
    for name, (base, spread) in spreads.items():
        noise = np.random.default_rng([zlib.crc32(name.encode()), seed]).standard_normal(out[name].shape)
        drawn = base * np.exp(spread * noise) if base else spread * noise
        out[name] = jnp.asarray(drawn.astype(out[name].dtype))
    for name, factor in factors.items():
        out[name] = (out[name] * factor).astype(out[name].dtype)
    return out
```

```python
from contextlib import ExitStack

import numpy as np

import concourse.bass as bass
from concourse import mybir

ALU = mybir.AluOpType
ACT = mybir.ActivationFunctionType
AX = mybir.AxisListType
F32 = mybir.dt.float32
BF16 = mybir.dt.bfloat16
I32 = mybir.dt.int32

P = 128
BATCH, SEQ, D = 8, 512, 256
TOKENS = BATCH * SEQ
TILES = TOKENS // P
SEQ_TILES = SEQ // P
DC = D // P
RANK = 64
HEADS, HD = 16, 16
HALF = HEADS // 2
BH = BATCH * HEADS
KEEP = int(SEQ * 0.3)
QK_SCALE = D ** -0.5
PARTS_Q = (0, 0, 0, 1, 1, 1, 2, 2)
PARTS_K = (0, 1, 2, 0, 1, 2, 0, 1)
SLOTS = len(PARTS_Q)
BIG = 2.0 ** 100
WINDOW = 8
LN_EPS = 1e-5
EXPERTS, TOP_E, EH = 8, 2, 512
BLOCKS, BLOCK, TOP_B, OUTF = 16, 64, 4, 1024
PHM = 4


def bc(ap, shape):
    return ap.to_broadcast(shape)


def load_constants(nc, t, m, sems):
    loaded = sems("const_loaded")
    with nc.Block() as block:
        @block.sync
        def _(sp):
            pairs = [(m.ident[:], t["ident"]), (m.ids[:], t["ids"]), (m.s_col[:], t["s_col"]),
                     (m.vt[:], t["Vt"]), (m.qk_bias[:], t["qk_bias"]), (m.half_mask[:], t["half_mask"]),
                     (m.rank8[:], t["rank8"].to_broadcast((P, 8)))]
            for dst, src in pairs:
                sp.dma_start(dst, src).then_inc(loaded, 16)
            sp.wait_ge(loaded, 16 * len(pairs))

        @block.vector
        def _(v):
            nc.vector.memset(m.eps[:], LN_EPS)
            nc.vector.memset(m.ones[:], 1.0)
            v.wait_ge(loaded, 16 * 7)
            nc.vector.tensor_scalar(m.qk_bias[:, 0:DC], m.qk_bias[:, 0:DC], QK_SCALE, None, ALU.mult)


def embed(nc, t, m, sems):
    gathered = [sems(f"gathered{g}") for g in range(4)]
    turned, scaled, made, kept = sems("u_turned"), sems("u_scaled"), sems("rows_made"), sems("rows_kept")
    with ExitStack() as c:
        rows = c.enter_context(nc.sbuf_tensor("u_rows", [P, TILES, RANK], F32))
        uT = c.enter_context(nc.sbuf_tensor("uT", [RANK, 2, SEQ], F32))
        psT = c.enter_context(nc.psum_tensor("psT_emb", [P, 2, 512], F32))
        psH = c.enter_context(nc.psum_tensor("psH_emb", [P, 4, 512], F32))
        block = c.enter_context(nc.Block())

        @block.gpsimd
        def _(pool):
            for i in range(TILES):
                pool.indirect_dma_start(
                    out=rows[:, i, :], out_offset=None, in_=t["U"],
                    in_offset=bass.IndirectOffsetOnAxis(ap=m.ids[:, i:i + 1], axis=0),
                ).then_inc(gathered[i // 8], 16)

        @block.tensor
        def _(pe):
            for g in range(BATCH):
                if g % 2 == 0:
                    pe.wait_ge(gathered[g // 2], 16 * 8)
                if g >= 2:
                    pe.wait_ge(scaled, g - 1)
                for j in range(4):
                    tr = nc.tensor.transpose(psT[0:RANK, g % 2, j * P:(j + 1) * P], rows[:, 4 * g + j, :], m.ident[:])
                tr.then_inc(turned, 1)
                pe.wait_ge(scaled, g + 1)
                if g >= 2:
                    pe.wait_ge(kept, 2 * (g - 1))
                for j in range(4):
                    nc.tensor.matmul(psH[:, 2 * (g % 2) + j // 2, (j % 2) * D:(j % 2 + 1) * D],
                                     uT[:, g % 2, j * P:(j + 1) * P], m.vt[:],
                                     start=True, stop=True, skip_group_check=True).then_inc(made, 1)

        @block.vector
        def _(v):
            for g in range(BATCH):
                v.wait_ge(turned, g + 1)
                if g >= 2:
                    v.wait_ge(made, 4 * (g - 1))
                nc.vector.tensor_scalar(uT[:, g % 2, :], psT[0:RANK, g % 2, :], m.s_col[:], None, ALU.mult).then_inc(scaled, 1)

        @block.scalar
        def _(act):
            for i in range(0, TILES, 2):
                act.wait_ge(made, i + 2)
                nc.scalar.copy(m.resid[:, i:i + 2, :], psH[:, (i // 2) % 4, :].rearrange("p (n d) -> p n d", n=2)).then_inc(kept, 1)


def norm_stats(nc, v, st, src, mean, var, n=TILES):
    with v.Fori(0, n) as i:
        nc.vector.bn_stats(st[:, bass.ds(i, 1), :], src[:, bass.ds(i, 1), :])
    v.drain()
    even, odd = st[:, :, 1:2].rearrange("p n a -> p (n a)"), st[:, :, 4:5].rearrange("p n a -> p (n a)")
    m2e, m2o = st[:, :, 2:3].rearrange("p n a -> p (n a)"), st[:, :, 5:6].rearrange("p n a -> p (n a)")
    nc.vector.tensor_tensor(mean, even, odd, ALU.add)
    nc.vector.tensor_tensor(var, even, odd, ALU.subtract)
    v.drain()
    nc.vector.tensor_scalar(mean, mean, 0.5, None, ALU.mult)
    nc.vector.tensor_tensor(var, var, var, ALU.mult)
    nc.vector.tensor_tensor(m2e, m2e, m2o, ALU.add)
    v.drain()
    nc.vector.tensor_scalar(var, var, 0.25, None, ALU.mult)
    nc.vector.tensor_scalar(m2e, m2e, 1.0 / D, None, ALU.mult)
    v.drain()
    nc.vector.tensor_tensor(var, var, m2e, ALU.add)


def norm_turn(nc, m, sems, tag, src, keep, xT, gain=None, shift=None):
    vars_ready, root, rows_ready = sems("vars_ready" + tag), sems("root" + tag), sems("xhat_ready" + tag)
    turned, moved = sems("x_turned" + tag), sems("x_moved" + tag)
    G = 2
    STEPS = TILES // G
    WIDE = 8
    with ExitStack() as c:
        st = c.enter_context(nc.sbuf_tensor("ln_st" + tag, [P, TILES, 6], F32))
        mean = c.enter_context(nc.sbuf_tensor("ln_mean" + tag, [P, TILES], F32))
        var = c.enter_context(nc.sbuf_tensor("ln_var" + tag, [P, TILES], F32))
        rstd = c.enter_context(nc.sbuf_tensor("ln_rstd" + tag, [P, TILES], F32))
        ring = None
        if keep is None:
            ring = c.enter_context(nc.sbuf_tensor("xhat" + tag, [P, 2 * G, D], F32))
        ps = c.enter_context(nc.psum_tensor("psN" + tag, [P, 2, 512], F32))
        block = c.enter_context(nc.Block())
        row = (lambda i: ring[:, i % (2 * G), :]) if keep is None else (lambda i: keep[:, i, :])

        @block.vector
        def _(v):
            norm_stats(nc, v, st, src, mean[:], var[:])
            v.drain().then_inc(vars_ready, 1)
            v.wait_ge(root, 1)
            nc.vector.reciprocal(rstd[:], rstd[:])
            v.drain()
            for i in range(TILES):
                step = i // G
                if keep is None and i % G == 0 and step >= 2:
                    v.wait_ge(turned, step - 1)
                op = nc.vector.tensor_scalar(row(i), src[:, i, :], mean[:, i:i + 1], rstd[:, i:i + 1], ALU.subtract, ALU.mult)
                if i % G == G - 1 and gain is None:
                    op.then_inc(rows_ready, 1)
                if gain is not None and i % WIDE == WIDE - 1:
                    v.drain()
                    part = keep[:, i - WIDE + 1:i + 1, :]
                    for other, how in ((gain, ALU.mult), (shift, ALU.add)):
                        nc.vector.tensor_tensor(part, part, other.rearrange("p (o d) -> p o d", o=1).to_broadcast((P, WIDE, D)), how)
                        last = v.drain()
                    last.then_inc(rows_ready, WIDE // G)

        @block.tensor
        def _(pe):
            for s in range(STEPS):
                pe.wait_ge(rows_ready, s + 1)
                if s >= 2:
                    pe.wait_ge(moved, s - 1)
                for ch in range(DC):
                    for j in range(G):
                        tr = nc.tensor.transpose(ps[:, s % 2, (ch * G + j) * P:(ch * G + j + 1) * P],
                                                 row(s * G + j)[:, ch * P:(ch + 1) * P], m.ident[:])
                tr.then_inc(turned, 1)

        @block.scalar
        def _(act):
            act.wait_ge(vars_ready, 1)
            nc.scalar.activation(rstd[:], var[:], ACT.Sqrt, bias=m.eps[:]).then_inc(root, 1)
            for s in range(STEPS):
                act.wait_ge(turned, s + 1)
                nc.scalar.copy(xT[:, :, s * G * P:(s + 1) * G * P],
                               ps[:, s % 2, :].rearrange("p (c n) -> p c n", c=DC)).then_inc(moved, 1)


def qkv(nc, t, m, sems):
    w_loaded = sems("w_qkv_loaded")
    s = {k: sems("qkv_" + k) for k in (
        "proj", "biased", "part1", "rest1", "part2", "part3", "stored", "squares", "kstats", "guess", "guess_kept", "v_made", "v_kept", "sd", "ones")}
    NCH = 2 * DC
    with ExitStack() as c:
        sb = lambda n, sh, dt=F32: c.enter_context(nc.sbuf_tensor(n, sh, dt))
        w = sb("w_qkv", [P, DC, 3 * D])
        vb = sb("v_bias", [P, D])
        qk = sb("qk", [P, NCH, SEQ])
        rest = sb("rest", [P, NCH, SEQ])
        parts = sb("parts", [P, NCH, 3, SEQ], BF16)
        sq = sb("q_sq", [P, DC, SEQ])
        kst = sb("k_st", [P, DC, 6])
        kmv = sb("k_mv", [P, DC, 2])
        kdiag = sb("k_diag", [P, DC, 2, HALF])
        psQ = c.enter_context(nc.psum_tensor("psQ_qkv", [P, NCH, 512], F32))
        psV = c.enter_context(nc.psum_tensor("psV_qkv", [P, 2, 512], F32))
        psG = c.enter_context(nc.psum_tensor("psG_qkv", [P, 512], F32))
        guess = psG[:, 0:SEQ_TILES * DC * 2 * HALF].rearrange("p (i c a h) -> p i c a h", i=SEQ_TILES, c=DC, a=2)
        block = c.enter_context(nc.Block())

        @block.sync
        def _(sp):
            sp.dma_start(w[:], t["W_qkvT"].rearrange("(c p) e -> p c e", p=P)).then_inc(w_loaded, 16)
            sp.dma_start(vb[:], t["v_bias"].to_broadcast((P, D))).then_inc(w_loaded, 16)
            with sp.Fori(0, BATCH) as b:
                for j in range(NCH):
                    which, ch = j // DC, j % DC
                    sp.wait_ge(s["part3"], b * NCH + (j + 1))
                    dst = m.parts_dram[which][bass.ds(b, 1), :, ch * P:(ch + 1) * P, :].rearrange("o a p n -> p (o a) n")
                    sp.dma_start(dst, parts[:, j, :, :]).then_inc(s["stored"], 16)
            sp.wait_ge(s["stored"], 16 * BATCH * NCH)

        @block.tensor
        def _(pe):
            pe.wait_ge(w_loaded, 32)
            for b in range(BATCH):
                pe.wait_ge(s["biased"], b * NCH)
                for j in range(NCH):
                    for ch in range(DC):
                        mm = nc.tensor.matmul(psQ[:, j, :], w[:, ch, j * P:(j + 1) * P],
                                              m.xT[:, ch, bass.ds(b * SEQ, SEQ)], start=(ch == 0), stop=(ch == DC - 1))
                    mm.then_inc(s["proj"], 1)
                pe.wait_ge(s["v_kept"], b * SEQ_TILES)
                for i in range(SEQ_TILES):
                    for ch in range(DC):
                        mm = nc.tensor.matmul(psV[:, i // 2, (i % 2) * D:(i % 2 + 1) * D],
                                              m.xT[:, ch, bass.ds(b * SEQ + i * P, P)], w[:, ch, 2 * D:3 * D],
                                              start=(ch == 0), stop=(ch == DC - 1), skip_group_check=True)
                    mm.then_inc(s["v_made"], 1)
                pe.wait_ge(s["squares"], (b + 1) * DC)
                pe.wait_ge(s["kstats"], b + 1)
                pe.wait_ge(s["guess_kept"], b)
                for i in range(SEQ_TILES):
                    for ch in range(DC):
                        nc.tensor.matmul(guess[:, i, ch, 0, :], qk[:, ch, i * P:(i + 1) * P], kdiag[:, ch, 0, :],
                                         start=True, stop=True, skip_group_check=True)
                        mm = nc.tensor.matmul(guess[:, i, ch, 1, :], sq[:, ch, i * P:(i + 1) * P], kdiag[:, ch, 1, :],
                                              start=True, stop=True, skip_group_check=True)
                mm.then_inc(s["guess"], 1)

        @block.scalar
        def _(act):
            with act.Fori(0, BATCH) as b:
                act.wait_ge(s["guess"], b)
                act.wait_ge(s["rest1"], b * NCH)
                for j in range(NCH):
                    act.wait_ge(s["proj"], b * NCH + (j + 1))
                    nc.scalar.activation(qk[:, j, :], psQ[:, j, :], ACT.Identity, bias=m.qk_bias[:, j:j + 1],
                                         scale=QK_SCALE if j < DC else 1.0).then_inc(s["biased"], 1)
                for ch in range(DC):
                    act.wait_ge(s["biased"], b * NCH + (ch + 1))
                    nc.scalar.activation(sq[:, ch, :], qk[:, ch, :], ACT.Square).then_inc(s["squares"], 1)
                for j in range(NCH):
                    act.wait_ge(s["rest1"], b * NCH + (j + 1))
                    nc.scalar.copy(parts[:, j, 1, :], rest[:, j, :]).then_inc(s["part2"], 1)
            act.wait_ge(s["guess_kept"], BATCH)
            nc.scalar.activation(m.step[:], m.step[:], ACT.Sqrt).then_inc(s["sd"], 1)

        @block.gpsimd
        def _(pool):
            with pool.Fori(0, BATCH) as b:
                for j in range(NCH):
                    pool.wait_ge(s["part2"], b * NCH + (j + 1))
                    nc.gpsimd.tensor_tensor(parts[:, j, 2, :], rest[:, j, :], parts[:, j, 1, :], ALU.subtract).then_inc(s["part3"], 1)

        @block.vector
        def _(v):
            nc.vector.memset(m.v_aug[:, :, :, HD:HD + 1], 1.0).then_inc(s["ones"], 1)
            v.wait_ge(w_loaded, 32)
            with v.Fori(0, BATCH) as b:
                v.wait_ge(s["stored"], 16 * NCH * b)
                v.wait_ge(s["guess"], b)
                for j in range(NCH):
                    v.wait_ge(s["biased"], b * NCH + (j + 1))
                    nc.vector.tensor_copy(parts[:, j, 0, :], qk[:, j, :]).then_inc(s["part1"], 1)
                    if j >= DC:
                        nc.vector.bn_stats(kst[:, j - DC, :], qk[:, j, :])
                    v.wait_ge(s["part1"], b * NCH + (j + 1))
                    nc.vector.tensor_tensor(rest[:, j, :], qk[:, j, :], parts[:, j, 0, :], ALU.subtract).then_inc(s["rest1"], 1)
                v.drain()
                for ch in range(DC):
                    nc.vector.bn_aggr(kmv[:, ch, :], kst[:, ch, :])
                v.drain()
                for ch in range(DC):
                    for a in range(2):
                        op = nc.vector.tensor_scalar(kdiag[:, ch, a, :], m.half_mask[:], kmv[:, ch, a:a + 1], None, ALU.mult)
                op.then_inc(s["kstats"], 1)
                for i in range(SEQ_TILES):
                    v.wait_ge(s["v_made"], b * SEQ_TILES + (i // 2 * 2 + 2))
                    nc.vector.tensor_tensor(m.v_aug[:, bass.ds(b * HEADS, HEADS), i, 0:HD],
                                            psV[:, i // 2, (i % 2) * D:(i % 2 + 1) * D].rearrange("p (h d) -> p h d", h=HEADS),
                                            vb[:].rearrange("p (h d) -> p h d", h=HEADS), ALU.add).then_inc(s["v_kept"], 1)
                v.wait_ge(s["guess"], b + 1)
                for ch in range(DC):
                    nc.vector.tensor_copy(m.thr0[:, bass.ds(b * HEADS + ch * HALF, HALF), :],
                                          guess[:, :, ch, 0, :].rearrange("p i h -> p h i"))
                    op = nc.vector.tensor_copy(m.step[:, bass.ds(b * HEADS + ch * HALF, HALF), :],
                                               guess[:, :, ch, 1, :].rearrange("p i h -> p h i"))
                v.drain().then_inc(s["guess_kept"], 1)
            v.wait_ge(s["sd"], 1)
            nc.vector.scalar_tensor_tensor(m.thr0[:], m.step[:], -0.545, m.thr0[:], ALU.mult, ALU.subtract)
            v.drain()
            nc.vector.tensor_scalar(m.step[:], m.step[:], 0.5 / (SEQ * 0.344), None, ALU.mult)


def attend(nc, t, m, sems):
    names = ("half0_loaded", "half1_loaded", "scores", "copied", "count0", "count1", "count2", "thr1", "thr2", "thr3", "masked",
             "pushed", "best8", "replaced", "over", "picked", "exps", "probs", "turned", "moved", "pv", "normed", "own", "needs", "over_read")
    s = {k: sems("at_" + k) for k in names}
    ST = SEQ_TILES
    HB = 2 * BATCH
    with ExitStack() as c:
        sb = lambda n, sh, dt=F32: c.enter_context(nc.sbuf_tensor(n, sh, dt))
        ring = [sb(n, [P, HEADS, SEQ], BF16) for n in ("q_ring", "k_ring")]
        X = sb("X", [P, 2, ST, SEQ])
        E = sb("E", [P, 2, ST, SEQ])
        sgn = sb("sgn", [P, 2, ST, SEQ], BF16)
        M = sb("M", [P, ST, SEQ], BF16)
        Z = sb("Z", [P, ST, SEQ])
        M2 = sb("M2", [P, ST, SEQ], BF16)
        PT = sb("PT", [P, ST, SEQ])
        push = sb("push", [P, P], BF16)
        nmax = sb("nmax", [P, 2, ST])
        cnt = sb("cnt", [P, 3, ST])
        dist = sb("dist", [P, 4, ST])
        nthr = sb("nthr", [P, 4, ST])
        thr = sb("thr", [P, ST])
        w1 = sb("upd_a", [P, ST]); w2 = sb("upd_b", [P, ST]); w3 = sb("upd_c", [P, ST]); moved_by = sb("upd_m", [P, ST])
        slope = sb("upd_s", [P, ST])
        c3 = sb("c3", [P, ST])
        need = sb("need", [P, ST])
        lim = sb("lim", [P, ST, 8])
        best = sb("best", [P, ST, 8])
        overs = sb("overs", [P, 2, ST])
        code = sb("code", [1, 4], I32)
        codef = sb("codef", [1, 4])
        rz = sb("rz", [P, ST, 1])
        psS = c.enter_context(nc.psum_tensor("psS_at", [P, ST, 512], F32))
        psT = c.enter_context(nc.psum_tensor("psPT_at", [P, 3, 512], F32))
        psO = c.enter_context(nc.psum_tensor("psO_at", [P, 512], F32))
        O = psO[:, 0:ST * (HD + 1)].rearrange("p (i d) -> p i d", i=ST)
        over_ps = psO[0:1, 256:256 + 2 * ST]
        block = c.enter_context(nc.Block())

        @block.sync
        def _(sp):
            def load(hb_of, half):
                for which, parts in ((0, PARTS_Q), (1, PARTS_K)):
                    for slot in range(SLOTS):
                        src = m.parts_dram[which][bass.ds(hb_of, 1), parts[slot], half * P:(half + 1) * P, :]
                        sp.dma_start(ring[which][slot * HD:(slot + 1) * HD, half * HALF:(half + 1) * HALF, :],
                                     src.rearrange("o (h d) n -> d (o h) n", d=HD)).then_inc(s[f"half{half}_loaded"], 16)
            load(0, 0)
            load(0, 1)
            with sp.Fori(1, BATCH) as b:
                for half in range(2):
                    sp.wait_ge(s["pushed"], ST * (HEADS * (b - 1) + (half + 1) * HALF))
                    load(b, half)

        @block.tensor
        def _(pe):
            def ring_ready(h):
                load = 2 * SLOTS * 16
                pe.wait_ge(s["half0_loaded"], load * (h // HEADS + 1))
                pe.wait_ge(s["half1_loaded"], load * ((h + HALF) // HEADS))

            def scores(h, i):
                r = h % HEADS
                return nc.tensor.matmul(psS[:, i, :], ring[0][:, bass.ds(r, 1), i * P:(i + 1) * P].rearrange("p o n -> p (o n)"),
                                        ring[1][:, bass.ds(r, 1), :].rearrange("p o n -> p (o n)"), start=True, stop=True)

            def first_scores(h):
                ring_ready(h)
                for i in range(ST):
                    scores(h, i).then_inc(s["scores"], 1)

            def push_selected(h):
                r = h % HEADS
                for i in range(ST):
                    pe.wait_ge(s["masked"], ST * h + (i + 1))
                    nc.tensor.matmul(psS[:, i, :], ring[0][:, bass.ds(r, 1), i * P:(i + 1) * P].rearrange("p o n -> p (o n)"),
                                     ring[1][:, bass.ds(r, 1), :].rearrange("p o n -> p (o n)"), start=True, stop=False)
                    nc.tensor.matmul(psS[:, i, :], push[:], M[:, i, :], start=False, stop=True).then_inc(s["pushed"], 1)

            def next_scores(h):
                ring_ready(h)
                for i in range(ST):
                    pe.wait_ge(s["replaced"], ST * (h - 2) + (i + 1))
                    scores(h, i).then_inc(s["scores"], 1)

            def count_over(h):
                pe.wait_ge(s["needs"], h + 1)
                if not (isinstance(h, int) and h < 2):
                    pe.wait_ge(s["normed"], h - 1)
                nc.tensor.matmul(over_ps, m.ones[:, 0:1], overs[:].rearrange("p a i -> p (a i)"),
                                 start=True, stop=True, skip_group_check=True).then_inc(s["over"], 1)

            def values(h):
                pe.wait_ge(s["moved"], ST * (h + 1))
                pe.wait_ge(s["over_read"], BH if isinstance(h, int) and h >= BH - 2 else h + 2)
                if not (isinstance(h, int) and h == 0):
                    pe.wait_ge(s["normed"], h)
                for i in range(ST):
                    for j in range(ST):
                        mm = nc.tensor.matmul(O[:, i, :], PT[:, i, j * P:(j + 1) * P],
                                              m.v_aug[:, bass.ds(h, 1), j, :].rearrange("p o d -> p (o d)"),
                                              start=(j == 0), stop=(j == ST - 1), skip_group_check=True)
                mm.then_inc(s["pv"], 1)

            def turn(h, par, tiles):
                for i in tiles:
                    pe.wait_ge(s["moved"], ST * h + (1 if i == 3 else 0))
                    pe.wait_ge(s["probs"], ST * h + (i + 1))
                    for j in range(ST):
                        tr = nc.tensor.transpose(psT[:, i % 3, j * P:(j + 1) * P], E[:, par, i, j * P:(j + 1) * P], m.ident[:])
                    tr.then_inc(s["turned"], 1)

            def slot(sl, par, prev=True, nxt=True):
                turn(sl - 2, par, (0, 1, 2))
                if prev:
                    push_selected(sl - 1)
                    count_over(sl - 1)
                turn(sl - 2, par, (3,))
                if nxt:
                    next_scores(sl + 1)
                values(sl - 2)

            first_scores(0)
            for i in range(ST):
                pe.wait_ge(s["copied"], i + 1)
                if i == 0:
                    ring_ready(1)
                scores(1, i).then_inc(s["scores"], 1)
            push_selected(0)
            count_over(0)
            next_scores(2)
            with pe.Fori(1, BH // 2 - 1) as pair:
                s0 = pair * 2
                slot(s0, 0)
                slot(s0 + 1, 1)
            slot(BH - 2, 0)
            slot(BH - 1, 1, nxt=False)
            slot(BH, 0, nxt=False)
            slot(BH + 1, 1, prev=False, nxt=False)

        @block.scalar
        def _(act):
            def count(h, par, which):
                if which == 0:
                    act.wait_ge(s["copied"], ST * (h + 1))
                else:
                    act.wait_ge(s[f"thr{which}"], h + 1)
                for i in range(ST):
                    bias = m.thr0[:, bass.ds(h, 1), i:i + 1].rearrange("p o i -> p (o i)") if which == 0 else nthr[:, which, i:i + 1]
                    nc.scalar.activation(sgn[:, 1 if which else 0, i, :], X[:, par, i, :], ACT.Sign, bias=bias,
                                         accum_out=cnt[:, which, i:i + 1]).then_inc(s[f"count{which}"], 1)

            def exps(h, par, first=False):
                if not first:
                    act.wait_ge(s["turned"], ST * (h - 1))
                for i in range(ST):
                    nc.scalar.activation(E[:, par, i, :], X[:, par, i, :], ACT.Exp, bias=nmax[:, par, i:i + 1]).then_inc(s["exps"], 1)

            def move(h):
                act.wait_ge(s["pv"], h)
                for i in range(ST):
                    act.wait_ge(s["turned"], ST * h + (i + 1))
                    nc.scalar.copy(PT[:, i, :], psT[:, i % 3, :]).then_inc(s["moved"], 1)

            def slot(sl, par, old, early=False):
                count(sl, par, 0)
                if old:
                    move(sl - 2)
                count(sl, par, 1)
                exps(sl, par, early)
                count(sl, par, 2)

            slot(0, 0, False, True)
            slot(1, 1, False, True)
            with act.Fori(1, BH // 2) as pair:
                s0 = pair * 2
                slot(s0, 0, True)
                slot(s0 + 1, 1, True)
            move(BH - 2)
            move(BH - 1)

        @block.gpsimd
        def _(pool):
            with pool.Fori(0, BH // 2) as pair:
                h0 = pair * 2
                for k in range(2):
                    h = h0 + k
                    pool.wait_ge(s["exps"], ST * (h + 1))
                    for i in range(ST):
                        pool.wait_ge(s["picked"], ST * h + (i + 1))
                        nc.gpsimd.tensor_tensor(E[:, k, i, :], E[:, k, i, :], M2[:, i, :], ALU.mult).then_inc(s["probs"], 1)

        @block.vector
        def _(v):
            TARGET = 2 * (KEEP - WINDOW // 2) - SEQ
            OUT2 = (WINDOW + 0.5) ** 2

            def update(h, which):
                k = which - 1
                v.wait_ge(s[f"count{k}"], ST * (h + 1))
                step = m.step[:, bass.ds(h, 1), :].rearrange("p o i -> p (o i)")
                old = m.thr0[:, bass.ds(h, 1), :].rearrange("p o i -> p (o i)") if k == 0 else nthr[:, k, :]
                nc.vector.tensor_scalar(dist[:, k, :], cnt[:, k, :], float(-TARGET), None, ALU.add)
                v.drain()
                if k == 0:
                    nc.vector.tensor_copy(slope[:], step)
                else:
                    nc.vector.tensor_tensor(w1[:], dist[:, k - 1, :], dist[:, k, :], ALU.subtract)
                    v.drain()
                    nc.vector.tensor_tensor(w2[:], moved_by[:], w1[:], ALU.mult)
                    nc.vector.tensor_tensor(w3[:], w1[:], w1[:], ALU.mult)
                    v.drain()
                    nc.vector.tensor_scalar(w3[:], w3[:], 1e-3, None, ALU.add)
                    v.drain()
                    nc.vector.reciprocal(w3[:], w3[:])
                    v.drain()
                    nc.vector.tensor_tensor(w2[:], w2[:], w3[:], ALU.mult)
                    v.drain()
                    nc.vector.scalar_tensor_tensor(w2[:], step, 0.4, w2[:], ALU.mult, ALU.max)
                    v.drain()
                    nc.vector.scalar_tensor_tensor(slope[:], step, 2.5, w2[:], ALU.mult, ALU.min)
                v.drain()
                nc.vector.tensor_tensor(w2[:], dist[:, k, :], dist[:, k, :], ALU.mult)
                if which == 3:
                    nc.vector.scalar_tensor_tensor(w3[:], dist[:, k, :], 6.0, slope[:], ALU.add, ALU.mult)
                else:
                    nc.vector.tensor_tensor(w3[:], dist[:, k, :], slope[:], ALU.mult)
                v.drain()
                nc.vector.scalar_tensor_tensor(moved_by[:], w2[:], OUT2, w3[:], ALU.is_gt, ALU.mult)
                v.drain()
                if which == 3:
                    nc.vector.tensor_tensor(thr[:], moved_by[:], old, ALU.subtract)
                else:
                    nc.vector.tensor_tensor(nthr[:, which, :], old, moved_by[:], ALU.subtract)
                v.drain().then_inc(s[f"thr{which}"], 1)

            def copy_scores(h, par):
                for i in range(ST):
                    v.wait_ge(s["scores"], ST * h + (i + 1))
                    nc.vector.tensor_scalar(X[:, par, i, :], psS[:, i, :], 1.0, None, ALU.mult, ALU.max,
                                            accum_out=nmax[:, par, i:i + 1]).then_inc(s["own"], 1)
                v.drain()
                nc.vector.tensor_scalar(nmax[:, par, :], nmax[:, par, :], -1.0, None, ALU.mult)
                v.drain().then_inc(s["copied"], ST)

            def mask(h, par):
                for i in range(ST):
                    nc.vector.tensor_scalar(M[:, i, :], X[:, par, i, :], thr[:, i:i + 1], None, ALU.is_gt, ALU.add,
                                            accum_out=c3[:, i:i + 1]).then_inc(s["masked"], 1)
                v.drain()

            def fix_counts(h):
                nc.vector.tensor_scalar(need[:], c3[:], -1.0, float(KEEP), ALU.mult, ALU.add)
                v.drain()
                nc.vector.tensor_scalar(overs[:, 0, :], need[:], float(WINDOW), None, ALU.is_gt)
                nc.vector.tensor_scalar(overs[:, 1, :], need[:], 2.0 * WINDOW, None, ALU.is_gt)
                nc.vector.tensor_scalar(w1[:], need[:], 0.0, 1000.0, ALU.is_lt, ALU.mult)
                v.drain()
                nc.vector.tensor_tensor(overs[:, 1, :], overs[:, 1, :], w1[:], ALU.add)
                v.drain().then_inc(s["needs"], 1)

            def limits():
                nc.vector.tensor_tensor(lim[:], m.rank8[:].rearrange("p (o e) -> p o e", o=1).to_broadcast((P, ST, 8)),
                                        need[:].rearrange("p (i o) -> p i o", o=1).to_broadcast((P, ST, 8)), ALU.is_lt)
                v.drain()
                nc.vector.tensor_scalar(lim[:], lim[:], 2 * BIG, -BIG, ALU.mult, ALU.add)

            def add_best(h):
                v.wait_ge(s["pushed"], ST * (h + 1))
                limits()
                for i in range(ST):
                    nc.vector.max(best[:, i, :], psS[:, i, :])
                v.drain()
                nc.vector.tensor_tensor(best[:], best[:], lim[:], ALU.min)
                v.drain()
                for i in range(ST):
                    nc.vector.match_replace(Z[:, i, :], best[:, i, :], psS[:, i, :], -BIG).then_inc(s["replaced"], 1)

            def add_round():
                nc.vector.tensor_scalar(need[:], need[:], -float(WINDOW), None, ALU.add)
                v.drain()
                limits()
                for i in range(ST):
                    nc.vector.max(best[:, i, :], Z[:, i, :])
                v.drain()
                nc.vector.tensor_tensor(best[:], best[:], lim[:], ALU.min)
                v.drain()
                for i in range(ST):
                    nc.vector.match_replace(Z[:, i, :], best[:, i, :], Z[:, i, :], -BIG)
                v.drain()

            def check(h, par):
                v.wait_ge(s["over"], h + 1)
                nc.vector.tensor_reduce(codef[:, 0:2], over_ps.rearrange("p (a i) -> p a i", a=2), AX.X, ALU.add).then_inc(s["over_read"], 1)
                v.drain()
                nc.vector.tensor_copy(code[:, 0:2], codef[:, 0:2])
                v.drain()
                nc.vector.tensor_tensor(code[:, 2:3], code[:, 0:1], code[:, 1:2], ALU.add)
                v.drain()
                far = v.value_load(code[0:1, 2:3], min_val=0, max_val=2 ** 30)
                with v.If(far > 0):
                    worst = v.value_load(code[0:1, 1:2], min_val=0, max_val=2 ** 30)
                    with v.If(worst > 0):
                        nc.vector.memset(need[:], float(KEEP + WINDOW))
                        for i in range(ST):
                            nc.vector.tensor_scalar(Z[:, i, :], X[:, par, i, :], 1.0, None, ALU.mult)
                        v.drain()
                        with v.Fori(0, -(-KEEP // WINDOW) - 1):
                            add_round()
                    v.end_ifs()
                    add_round()
                v.end_ifs()

            def pick(h):
                for i in range(ST):
                    nc.vector.tensor_scalar(M2[:, i, :], Z[:, i, :], -BIG / 2, None, ALU.is_lt).then_inc(s["picked"], 1)

            def normalise(h):
                v.wait_ge(s["pv"], h + 1)
                nc.vector.reciprocal(rz[:], O[:, :, HD:HD + 1])
                v.drain()
                nc.vector.tensor_tensor(m.heads_out[:, bass.ds(h, 1), :, :].rearrange("p o i d -> p (o i) d"),
                                        O[:, :, 0:HD], rz[:].to_broadcast((P, ST, HD)), ALU.mult)
                v.drain().then_inc(s["normed"], 1)

            def slot(sl, par, prev=True, nxt=True, cur=True, old=True, first=False):
                if prev:
                    mask(sl - 1, 1 - par)
                    fix_counts(sl - 1)
                if cur:
                    update(sl, 1)
                if prev:
                    add_best(sl - 1)
                if cur:
                    update(sl, 2)
                if prev:
                    v.drain()
                    check(sl - 1, 1 - par)
                    if not first:
                        v.wait_ge(s["probs"], ST * (sl - 1))
                    pick(sl - 1)
                if nxt:
                    copy_scores(sl + 1, 1 - par)
                if cur:
                    update(sl, 3)
                if old:
                    normalise(sl - 2)

            nc.vector.tensor_scalar(push[:], m.ident[:], -BIG, None, ALU.mult)
            copy_scores(0, 0)
            slot(0, 0, prev=False, old=False)
            slot(1, 1, old=False, first=True)
            with v.Fori(1, BH // 2 - 1) as pair:
                s0 = pair * 2
                for k in range(2):
                    slot(s0 + k, k)
            slot(BH - 2, 0)
            slot(BH - 1, 1, nxt=False)
            slot(BH, 0, nxt=False, cur=False)
            normalise(BH - 1)


def project(nc, t, m, sems):
    w_loaded, turned, moved, made, added = (sems("pr_" + k) for k in ("w_loaded", "turned", "moved", "made", "added"))
    with ExitStack() as c:
        sb = lambda n, sh, dt=F32: c.enter_context(nc.sbuf_tensor(n, sh, dt))
        w = sb("w_out", [P, DC, D])
        bias = sb("b_out", [P, D])
        aT = sb("attnT", [P, 2, DC, P])
        flat = sb("attn_rows", [P, 2, D])
        psA = c.enter_context(nc.psum_tensor("psA_pr", [P, 2, 512], F32))
        psP = c.enter_context(nc.psum_tensor("psP_pr", [P, 2, 512], F32))
        rows, gathered = flat, sems("pr_rows")
        block = c.enter_context(nc.Block())

        @block.sync
        def _(sp):
            sp.dma_start(w[:], t["W_outT"].rearrange("(c p) e -> p c e", p=P)).then_inc(w_loaded, 16)
            sp.dma_start(bias[:], t["b_out"].to_broadcast((P, D))).then_inc(w_loaded, 16)

        @block.gpsimd
        def _(pool):
            for n in range(TILES):
                b, i = n // SEQ_TILES, n % SEQ_TILES
                if n >= 2:
                    pool.wait_ge(turned, n - 1)
                nc.gpsimd.tensor_copy(rows[:, n % 2, :].rearrange("p (h d) -> p h d", h=HEADS),
                                      m.heads_out[:, b * HEADS:(b + 1) * HEADS, i, :]).then_inc(gathered, 1)

        @block.tensor
        def _(pe):
            pe.wait_ge(w_loaded, 32)
            for n in range(TILES):
                pe.wait_ge(gathered, n + 1)
                if n >= 2:
                    pe.wait_ge(moved, n - 1)
                    pe.wait_ge(added, n - 1)
                for ch in range(DC):
                    tr = nc.tensor.transpose(psA[:, n % 2, ch * P:(ch + 1) * P], rows[:, n % 2, ch * P:(ch + 1) * P], m.ident[:])
                tr.then_inc(turned, 1)
                pe.wait_ge(moved, n + 1)
                for ch in range(DC):
                    mm = nc.tensor.matmul(psP[:, n % 2, 0:D], aT[:, n % 2, ch, :], w[:, ch, :], start=(ch == 0), stop=(ch == DC - 1))
                mm.then_inc(made, 1)

        @block.scalar
        def _(act):
            for n in range(TILES):
                act.wait_ge(turned, n + 1)
                if n >= 2:
                    act.wait_ge(made, n - 1)
                nc.scalar.copy(aT[:, n % 2, :, :], psA[:, n % 2, 0:D].rearrange("p (c n) -> p c n", c=DC)).then_inc(moved, 1)

        @block.vector
        def _(v):
            v.wait_ge(w_loaded, 32)
            nc.vector.tensor_tensor(m.resid[:], m.resid[:], bias[:].rearrange("p (o d) -> p o d", o=1).to_broadcast((P, TILES, D)), ALU.add)
            v.drain()
            for n in range(TILES):
                v.wait_ge(made, n + 1)
                nc.vector.tensor_tensor(m.resid[:, n, :], psP[:, n % 2, 0:D], m.resid[:, n, :], ALU.add).then_inc(added, 1)


def top_k_mask(nc, v, act_exp, logits, bias, n, top, work):
    p = work.probs[:, :, 0:n]
    one = lambda ap: ap.rearrange("p (t o) -> p t o", o=1).to_broadcast((P, TILES, n))
    nc.vector.tensor_tensor(p, logits, bias.rearrange("p (o e) -> p o e", o=1).to_broadcast((P, TILES, n)), ALU.add)
    nc.vector.memset(work.probs[:, :, n:n + 8], -2.0)
    v.drain()
    nc.vector.tensor_reduce(work.row[:], p, AX.X, ALU.max)
    v.drain()
    nc.vector.tensor_tensor(p, p, one(work.row[:]), ALU.subtract)
    act_exp()
    nc.vector.tensor_reduce(work.row[:], p, AX.X, ALU.add)
    v.drain()
    nc.vector.reciprocal(work.row[:], work.row[:])
    v.drain()
    nc.vector.tensor_tensor(p, p, one(work.row[:]), ALU.mult)
    v.drain()
    for i in range(TILES):
        nc.vector.max(work.best[:, i, :], work.probs[:, i, 0:n])
    v.drain()
    nc.vector.memset(work.best[:, :, top:8], -2.0)
    v.drain()
    for i in range(TILES):
        nc.vector.match_replace(work.found[:, i, :], work.best[:, i, :], work.probs[:, i, :], -1.0)
    v.drain()


class RouteWork:

    def __init__(self, sb, tag, n):
        self.probs = sb("probs" + tag, [P, TILES, n + 8])
        self.found = sb("found" + tag, [P, TILES, n + 8])
        self.best = sb("best" + tag, [P, TILES, 8])
        self.row = sb("row" + tag, [P, TILES])


def moe(nc, t, m, sems):
    s = {k: sems("moe_" + k) for k in ("small", "logits", "shifted", "exped", "weights", "wT_made", "wT_kept", "bias_made", "bias_added",
                                       "w_loaded0", "w_loaded1", "hidden", "active", "made", "h_unused", "y_free")}
    ALL = EXPERTS + 1
    HC = EH // P
    CH = BATCH
    with ExitStack() as c:
        sb = lambda n, sh, dt=F32: c.enter_context(nc.sbuf_tensor(n, sh, dt))
        w1 = sb("w1", [P, 2, DC, EH])
        w2 = sb("w2", [P, 2, HC, D])
        b1 = sb("b1", [P, ALL * HC])
        b1_now = sb("b1_now", [P, HC])
        rw = sb("router_w", [P, DC, EXPERTS])
        rb = sb("router_b", [P, EXPERTS])
        b2s = sb("b2_shared", [P, D])
        b2r = sb("b2_routed", [EXPERTS, D])
        work = RouteWork(sb, "_moe", EXPERTS)
        wt = sb("expert_weights", [P, TILES, ALL])
        wT = sb("weightsT", [EXPERTS, 2, P])
        H = sb("hidden", [P, 2, HC, SEQ])
        psH = c.enter_context(nc.psum_tensor("psH_moe", [P, HC, 512], F32))
        psY = c.enter_context(nc.psum_tensor("psY_moe", [P, 4, 512], F32))

        with nc.Block() as block:
            @block.sync
            def _(sp):
                for dst, src in ((rw[:], t["router_w"].rearrange("(c p) e -> p c e", p=P)), (rb[:], t["router_b"].to_broadcast((P, EXPERTS))),
                                 (b2s[:], t["sb2"].to_broadcast((P, D))), (b2r[:], t["rb2"]), (b1[:], t["b1_all"])):
                    sp.dma_start(dst, src).then_inc(s["small"], 16)

            @block.tensor
            def _(pe):
                pe.wait_ge(s["small"], 16 * 5)
                for i in range(TILES):
                    for ch in range(DC):
                        mm = nc.tensor.matmul(psH[:, 0, i * EXPERTS:(i + 1) * EXPERTS], m.xT[:, ch, i * P:(i + 1) * P], rw[:, ch, :],
                                              start=(ch == 0), stop=(ch == DC - 1), skip_group_check=True)
                mm.then_inc(s["logits"], 1)
                pe.wait_ge(s["weights"], 1)
                for i in range(TILES):
                    if i >= 2:
                        pe.wait_ge(s["wT_kept"], i - 1)
                    nc.tensor.transpose(psY[0:EXPERTS, i % 2, 0:P], wt[:, i, 1:ALL], m.ident[:]).then_inc(s["wT_made"], 1)
                    pe.wait_ge(s["wT_kept"], i + 1)
                    if i >= 2:
                        pe.wait_ge(s["bias_added"], i - 1)
                    nc.tensor.matmul(psY[:, 2 + i % 2, 0:D], wT[:, i % 2, :], b2r[:], start=True, stop=True).then_inc(s["bias_made"], 1)

            @block.scalar
            def _(act):
                act.wait_ge(s["shifted"], 1)
                nc.scalar.activation(work.probs[:, :, 0:EXPERTS], work.probs[:, :, 0:EXPERTS], ACT.Exp).then_inc(s["exped"], 1)
                for i in range(TILES):
                    act.wait_ge(s["wT_made"], i + 1)
                    if i >= 2:
                        act.wait_ge(s["bias_made"], i - 1)
                    nc.scalar.copy(wT[:, i % 2, :], psY[0:EXPERTS, i % 2, 0:P]).then_inc(s["wT_kept"], 1)

            @block.vector
            def _(v):
                def exp_on_scalar():
                    v.drain().then_inc(s["shifted"], 1)
                    v.wait_ge(s["exped"], 1)
                v.wait_ge(s["logits"], 1)
                top_k_mask(nc, v, exp_on_scalar, psH[:, 0, 0:TILES * EXPERTS].rearrange("p (t e) -> p t e", e=EXPERTS), rb[:], EXPERTS, TOP_E, work)
                nc.vector.memset(wt[:, :, 0:1], 1.0)
                nc.vector.scalar_tensor_tensor(wt[:, :, 1:ALL], work.found[:, :, 0:EXPERTS], -0.5, work.probs[:, :, 0:EXPERTS], ALU.is_lt, ALU.mult)
                v.drain().then_inc(s["weights"], 1)
                nc.vector.tensor_tensor(m.resid[:], m.resid[:], b2s[:].rearrange("p (o d) -> p o d", o=1).to_broadcast((P, TILES, D)), ALU.add)
                v.drain()
                for i in range(TILES):
                    v.wait_ge(s["bias_made"], i + 1)
                    nc.vector.tensor_tensor(m.resid[:, i, :], psY[:, 2 + i % 2, 0:D], m.resid[:, i, :], ALU.add).then_inc(s["bias_added"], 1)

        with nc.Block() as block:
            @block.sync
            def _(sp):
                def load(e, r):
                    sp.dma_start(w1[:, r, :, :], t["w1_all"][bass.ds(e, 1)].rearrange("o (c p) n -> p (o c) n", p=P)).then_inc(s[f"w_loaded{r}"], 16)
                    sp.dma_start(w2[:, r, :, :], t["w2_all"][bass.ds(e, 1)].rearrange("o (c p) n -> p (o c) n", p=P)).then_inc(s[f"w_loaded{r}"], 16)
                load(0, 0)
                load(1, 1)
                with sp.Fori(1, ALL // 2) as pair:
                    e = pair * 2
                    for r in range(2):
                        sp.wait_ge(s["made"], SEQ_TILES * CH * (e + (r - 1)))
                        load(e + r, r)
                sp.wait_ge(s["made"], SEQ_TILES * CH * (ALL - 2))
                load(ALL - 1, 0)

            @block.tensor
            def _(pe):
                def hidden(e, r, n):
                    g = e * CH + n
                    for hc in range(HC):
                        pe.wait_ge(s["active"], HC * g + (hc + 1))
                        for ch in range(DC):
                            mm = nc.tensor.matmul(psH[:, hc, :], w1[:, r, ch, hc * P:(hc + 1) * P], m.xT[:, ch, n * SEQ:(n + 1) * SEQ],
                                                  start=(ch == 0), stop=(ch == DC - 1))
                        mm.then_inc(s["hidden"], 1)

                def output(e, r, n):
                    g = e * CH + n
                    pe.wait_ge(s["active"], HC * (g + 2))
                    for i in range(SEQ_TILES):
                        pe.wait_ge(s["y_free"], SEQ_TILES * g + (i // 2 * 2 + 2))
                        for hc in range(HC):
                            mm = nc.tensor.matmul(psY[:, 2 * (n % 2) + i // 2, (i % 2) * D:(i % 2 + 1) * D],
                                                  H[:, n % 2, hc, i * P:(i + 1) * P], w2[:, r, hc, :],
                                                  start=(hc == 0), stop=(hc == HC - 1), skip_group_check=True)
                        mm.then_inc(s["made"], 1)

                def expert(e, r, last=False):
                    for n in range(CH):
                        if n < CH - 1:
                            hidden(e, r, n + 1)
                        elif not last:
                            pe.wait_ge(s[f"w_loaded{1 - r}"], e * 16 + (48 if r else 32))
                            hidden(e + 1, 1 - r, 0)
                        output(e, r, n)

                pe.wait_ge(s["w_loaded0"], 32)
                hidden(0, 0, 0)
                with pe.Fori(0, ALL // 2) as pair:
                    e = pair * 2
                    expert(e, 0)
                    expert(e + 1, 1)
                expert(ALL - 1, 0, last=True)

            @block.scalar
            def _(act):
                act.drain().then_inc(s["active"], HC)
                with act.Fori(0, ALL) as e:
                    act.drain()
                    nc.scalar.copy(b1_now[:], b1[:, bass.ds(e * HC, HC)])
                    act.drain()
                    for n in range(CH):
                        g = e * CH + n
                        act.wait_ge(s["h_unused"], g + 1)
                        for hc in range(HC):
                            act.wait_ge(s["hidden"], HC * g + (hc + 1))
                            nc.scalar.activation(H[:, n % 2, hc, :], psH[:, hc, :], ACT.Gelu, bias=b1_now[:, hc:hc + 1]).then_inc(s["active"], 1)

            @block.vector
            def _(v):
                v.drain().then_inc(s["y_free"], 2 * SEQ_TILES)
                v.drain().then_inc(s["h_unused"], 2)
                with v.Fori(0, ALL) as e:
                    for n in range(CH):
                        g = e * CH + n
                        for i in range(SEQ_TILES):
                            v.wait_ge(s["made"], SEQ_TILES * g + (i // 2 * 2 + 2))
                            T = n * SEQ_TILES + i
                            v.wait_ge(s["y_free"], SEQ_TILES * g)
                            weight = wt[:, T, bass.ds(e, 1)]
                            nc.vector.scalar_tensor_tensor(m.resid[:, T, :], psY[:, 2 * (n % 2) + i // 2, (i % 2) * D:(i % 2 + 1) * D],
                                                           weight, m.resid[:, T, :], ALU.mult, ALU.add).then_inc(s["y_free"], 1)
                        v.drain().then_inc(s["h_unused"], 1)


def cos_attention(nc, t, m, sems):
    s = {k: sems("cos_" + k) for k in ("loaded", "built", "made", "kept", "scored", "mixed", "summed", "norm", "omade", "oadded")}
    NAMES = "qkvo"
    with ExitStack() as c:
        sb = lambda n, sh, dt=F32: c.enter_context(nc.sbuf_tensor(n, sh, dt))
        W = sb("W_phm", [P, 4, DC, D])
        bias = sb("phm_bias", [1, 4, D])
        gains = sb("ln_gains", [P, 4, D])
        rows = sb("query", [P, TILES, D])
        qnT = sb("qnT", [P, DC, TOKENS])

        with ExitStack() as c2:
            A = c2.enter_context(nc.sbuf_tensor("phm_A", [P, 4, PHM, DC, PHM], F32))
            S = c2.enter_context(nc.sbuf_tensor("phm_S", [P, 4, PHM, D // PHM], F32))
            prod = c2.enter_context(nc.sbuf_tensor("phm_prod", [P, 4, DC * D], F32))
            block = c2.enter_context(nc.Block())

            @block.sync
            def _(sp):
                for x, name in enumerate(NAMES):
                    for half in range(2):
                        sp.dma_start(A[half * 64:(half + 1) * 64, x, :, :, :],
                                     t["A_" + name][half:half + 1].to_broadcast((64, PHM * DC * PHM)).rearrange("p (n c j) -> p n c j", n=PHM, c=DC)).then_inc(s["loaded"], 16)
                        sp.dma_start(S[half * 64:(half + 1) * 64, x, :, :], t["S_" + name].rearrange("n k l -> k n l")).then_inc(s["loaded"], 16)
                    sp.dma_start(bias[:, x, :], t["bias_" + name]).then_inc(s["loaded"], 16)
                for x, name in enumerate(("g1", "b1", "g2", "b2")):
                    sp.dma_start(gains[:, x, :], t[name].to_broadcast((P, D))).then_inc(s["loaded"], 16)
                sp.wait_ge(s["loaded"], 16 * (4 * 5 + 4))

            @block.vector
            def _(v):
                v.wait_ge(s["loaded"], 16 * (4 * 5 + 4))
                L = D // PHM
                for n in range(PHM):
                    for x in range(4):
                        dst = W[:, x, :, :] if n == 0 else prod[:, x, :]
                        dst = dst.rearrange("p c (j l) -> p (c j) l", l=L) if n == 0 else dst.rearrange("p (a l) -> p a l", l=L)
                        nc.vector.tensor_tensor(dst, S[:, x, n:n + 1, :].to_broadcast((P, DC * PHM, L)),
                                                A[:, x, n, :, :].rearrange("p c (j o) -> p (c j) o", o=1).to_broadcast((P, DC * PHM, L)), ALU.mult)
                    v.drain()
                    if n:
                        for x in range(4):
                            nc.vector.tensor_tensor(W[:, x, :, :], W[:, x, :, :], prod[:, x, :].rearrange("p (c e) -> p c e", c=DC), ALU.add)
                        v.drain()

        norm_turn(nc, m, sems, "_query", m.resid, rows, m.xT)
        norm_turn(nc, m, sems, "_qn", rows, rows, qnT, gains[:, 0, :], gains[:, 1, :])

        with ExitStack() as c2:
            sb2 = lambda n, sh, dt=F32: c2.enter_context(nc.sbuf_tensor(n, sh, dt))
            Q, K, V = (sb2(n, [P, BATCH, D]) for n in ("cos_q", "cos_k", "cos_v"))
            prod = sb2("cos_prod", [P, BATCH, D])
            mix = sb2("cos_mix", [P, 2, BATCH, D])
            cosines = sb2("cosines", [P, BATCH, BATCH])
            a = sb2("cos_a", [P, 2, BATCH * HEADS])
            den = sb2("cos_den", [P, HEADS])
            att = sb2("cos_att", [P, D])
            psP = c2.enter_context(nc.psum_tensor("psP_cos", [P, 6, 512], F32))
            block = c2.enter_context(nc.Block())

            @block.sync
            def _(sp):
                sp.dma_start(cosines[:].rearrange("p a b -> p (a b)"), t["cosines"].to_broadcast((P, BATCH * BATCH))).then_inc(s["norm"], 16)

            @block.tensor
            def _(pe):
                for it in range(SEQ_TILES):
                    for l in range(BATCH):
                        par = l % 2
                        if l < 2:
                            pe.wait_ge(s["kept"], 3 * (it * BATCH))
                        else:
                            pe.wait_ge(s["kept"], 3 * (it * BATCH + (l - 1)))
                        for x in range(3):
                            src = qnT if x == 0 else m.xT
                            out = psP[:, 3 * par + x, 0:D]
                            for ch in range(DC):
                                nc.tensor.matmul(out, src[:, ch, bass.ds(l * SEQ + it * P, P)], W[:, x, ch, :], start=(ch == 0), stop=False)
                            mm = nc.tensor.matmul(out, m.ones[0:1, :], bias[:, x, :], start=False, stop=True)
                        mm.then_inc(s["made"], 1)

            @block.scalar
            def _(act):
                with act.Fori(0, SEQ_TILES) as it:
                    act.wait_ge(s["summed"], it * BATCH)
                    for l in range(BATCH):
                        act.wait_ge(s["made"], it * BATCH + (l + 1))
                        for x, (dst, f) in enumerate(((Q, ACT.Relu), (K, ACT.Relu), (V, ACT.Copy))):
                            nc.scalar.activation(dst[:, l, :], psP[:, 3 * (l % 2) + x, 0:D], f).then_inc(s["kept"], 1)

            @block.gpsimd
            def _(pool):
                with pool.Fori(0, SEQ_TILES) as it:
                    for l in range(BATCH):
                        pool.wait_ge(s["scored"], it * BATCH + (l + 1))
                        if l >= 2:
                            pool.wait_ge(s["summed"], it * BATCH + (l - 1))
                        nc.gpsimd.tensor_tensor(mix[:, l % 2, :, :].rearrange("p l (h d) -> p (l h) d", d=HD),
                                                V[:].rearrange("p l (h d) -> p (l h) d", d=HD),
                                                a[:, l % 2, :].rearrange("p (x o) -> p x o", o=1).to_broadcast((P, BATCH * HEADS, HD)),
                                                ALU.mult).then_inc(s["mixed"], 1)

            @block.vector
            def _(v):
                v.wait_ge(s["norm"], 16)

                def score(it, l):
                    al = a[:, l % 2, :]
                    nc.vector.tensor_tensor(prod[:], Q[:, l:l + 1, :].to_broadcast((P, BATCH, D)), K[:], ALU.mult)
                    v.drain()
                    nc.vector.tensor_reduce(al, prod[:].rearrange("p l (h d) -> p (l h) d", d=HD), AX.X, ALU.add)
                    v.drain()
                    al3 = al.rearrange("p (l h) -> p l h", h=HEADS)
                    nc.vector.tensor_tensor(al3, al3, cosines[:, l, :].rearrange("p (l o) -> p l o", o=1).to_broadcast((P, BATCH, HEADS)), ALU.mult)
                    v.drain()
                    nc.vector.tensor_reduce(den[:], al.rearrange("p (l h) -> p h l", h=HEADS), AX.X, ALU.add)
                    v.drain()
                    nc.vector.tensor_scalar(den[:], den[:], 1e-6, None, ALU.max)
                    v.drain()
                    nc.vector.reciprocal(den[:], den[:])
                    v.drain()
                    nc.vector.tensor_tensor(al3, al3, den[:].rearrange("p (o h) -> p o h", o=1).to_broadcast((P, BATCH, HEADS)), ALU.mult)
                    v.drain().then_inc(s["scored"], 1)

                def collect(it, l):
                    v.wait_ge(s["mixed"], it * BATCH + (l + 1))
                    nc.vector.tensor_reduce(att[:], mix[:, l % 2, :, :].rearrange("p l e -> p e l"), AX.X, ALU.add)
                    v.drain()
                    row = rows[:, bass.ds(l * SEQ_TILES + it, 1), :].rearrange("p o d -> p (o d)")
                    nc.vector.tensor_tensor(row, row, att[:], ALU.add)
                    v.drain().then_inc(s["summed"], 1)

                with v.Fori(0, SEQ_TILES) as it:
                    v.wait_ge(s["kept"], 3 * BATCH * (it + 1))
                    for l in range(BATCH):
                        score(it, l)
                        if l:
                            collect(it, l - 1)
                    collect(it, BATCH - 1)

        norm_turn(nc, m, sems, "_out", rows, rows, qnT, gains[:, 2, :], gains[:, 3, :])

        with ExitStack() as c2:
            psO = c2.enter_context(nc.psum_tensor("psO_cos", [P, 4, 512], F32))
            block = c2.enter_context(nc.Block())

            @block.gpsimd
            def _(pool):
                nc.gpsimd.tensor_tensor(m.resid[:], m.resid[:], rows[:], ALU.add).then_inc(s["norm"], 1)

            @block.tensor
            def _(pe):
                for i in range(TILES):
                    if i >= 4:
                        pe.wait_ge(s["oadded"], i - 3)
                    for ch in range(DC):
                        nc.tensor.matmul(psO[:, i % 4, 0:D], qnT[:, ch, i * P:(i + 1) * P], W[:, 3, ch, :], start=(ch == 0), stop=False)
                    nc.tensor.matmul(psO[:, i % 4, 0:D], m.ones[0:1, :], bias[:, 3, :], start=False, stop=True).then_inc(s["omade"], 1)

            @block.vector
            def _(v):
                v.wait_ge(s["norm"], 16 + 1)
                for i in range(TILES):
                    v.wait_ge(s["omade"], i + 1)
                    nc.vector.tensor_tensor(m.resid[:, i, :], psO[:, i % 4, 0:D], m.resid[:, i, :], ALU.add).then_inc(s["oadded"], 1)


def block_ffn(nc, t, m, sems, out):
    s = {k: sems("ffn_" + k) for k in ("small", "w_loaded", "logits", "shifted", "exped", "mask", "mT_made", "mT_kept",
                                       "hidden", "spread", "relu", "masked", "made", "added", "stored", "h_unused")}
    MC = OUTF // P
    with ExitStack() as c:
        sb = lambda n, sh, dt=F32: c.enter_context(nc.sbuf_tensor(n, sh, dt))
        w1 = sb("ffn_w1", [P, DC, OUTF])
        w2 = sb("ffn_w2", [P, MC, D])
        b1 = sb("ffn_b1", [P, MC])
        b2 = sb("ffn_b2", [1, D])
        rw = sb("ffn_rw", [P, DC, BLOCKS])
        rb = sb("ffn_rb", [P, BLOCKS])
        spread = sb("ffn_spread", [BLOCKS, MC, P], BF16)
        spread32 = sb("ffn_spread32", [BLOCKS, MC * P])
        maskT = sb("maskT", [BLOCKS, TOKENS], BF16)
        work = RouteWork(sb, "_ffn", BLOCKS)
        chosen = sb("chosen", [P, TILES, BLOCKS])
        H = sb("ffn_hidden", [P, 2, MC, SEQ])
        psH = c.enter_context(nc.psum_tensor("psH_ffn", [P, 2, 512], F32))
        psM = c.enter_context(nc.psum_tensor("psM_ffn", [P, 2, 512], F32))
        psY = c.enter_context(nc.psum_tensor("psY_ffn", [P, 4, 512], F32))
        out_tiles = out.rearrange("(n p) d -> p n d", p=P)

        with nc.Block() as block:
            @block.sync
            def _(sp):
                for dst, src in ((rw[:], t["ffn_rwT"].rearrange("(c p) e -> p c e", p=P)), (rb[:], t["ffn_rb"].to_broadcast((P, BLOCKS))),
                                 (b1[:], t["ffn_b1"]), (b2[:], t["ffn_b2"]), (spread32[:], t["spread"])):
                    sp.dma_start(dst, src).then_inc(s["small"], 16)
                sp.dma_start(w1[:], t["ffn_w1T"].rearrange("(c p) e -> p c e", p=P)).then_inc(s["w_loaded"], 16)
                sp.dma_start(w2[:], t["ffn_w2T"].rearrange("(c p) e -> p c e", p=P)).then_inc(s["w_loaded"], 16)

            @block.tensor
            def _(pe):
                pe.wait_ge(s["small"], 16 * 5)
                for i in range(TILES):
                    for ch in range(DC):
                        mm = nc.tensor.matmul(psH[:, 0, i * BLOCKS:(i + 1) * BLOCKS], m.xT[:, ch, i * P:(i + 1) * P], rw[:, ch, :],
                                              start=(ch == 0), stop=(ch == DC - 1), skip_group_check=True)
                mm.then_inc(s["logits"], 1)
                pe.wait_ge(s["mask"], 1)
                for g in range(BATCH):
                    if g >= 2:
                        pe.wait_ge(s["mT_kept"], g - 1)
                    for j in range(SEQ_TILES):
                        tr = nc.tensor.transpose(psM[0:BLOCKS, g % 2, j * P:(j + 1) * P], chosen[:, SEQ_TILES * g + j, :], m.ident[:])
                    tr.then_inc(s["mT_made"], 1)

            @block.scalar
            def _(act):
                act.wait_ge(s["shifted"], 1)
                nc.scalar.activation(work.probs[:, :, 0:BLOCKS], work.probs[:, :, 0:BLOCKS], ACT.Exp).then_inc(s["exped"], 1)
                for g in range(BATCH):
                    act.wait_ge(s["mT_made"], g + 1)
                    nc.scalar.copy(maskT[:, g * SEQ:(g + 1) * SEQ], psM[0:BLOCKS, g % 2, :]).then_inc(s["mT_kept"], 1)

            @block.vector
            def _(v):
                def exp_on_scalar():
                    v.drain().then_inc(s["shifted"], 1)
                    v.wait_ge(s["exped"], 1)
                v.wait_ge(s["small"], 16 * 5)
                nc.vector.tensor_copy(spread[:].rearrange("b m p -> b (m p)"), spread32[:])
                v.wait_ge(s["logits"], 1)
                top_k_mask(nc, v, exp_on_scalar, psH[:, 0, :].rearrange("p (t e) -> p t e", e=BLOCKS), rb[:], BLOCKS, TOP_B, work)
                nc.vector.tensor_scalar(chosen[:], work.found[:, :, 0:BLOCKS], -0.5, None, ALU.is_lt)
                v.drain().then_inc(s["mask"], 1)

        with nc.Block() as block:
            @block.tensor
            def _(pe):
                def hidden(n):
                    for mc in range(MC):
                        k = n * MC + mc
                        if not (isinstance(n, int) and n == 0 and mc < 2):
                            pe.wait_ge(s["masked"], k - 1)
                        for ch in range(DC):
                            mm = nc.tensor.matmul(psH[:, mc % 2, :], w1[:, ch, mc * P:(mc + 1) * P], m.xT[:, ch, bass.ds(n * SEQ, SEQ)],
                                                  start=(ch == 0), stop=(ch == DC - 1))
                        mm.then_inc(s["hidden"], 1)
                        nc.tensor.matmul(psM[:, mc % 2, :], spread[:, mc, :], maskT[:, bass.ds(n * SEQ, SEQ)], start=True, stop=True).then_inc(s["spread"], 1)

                def output(n, par):
                    pe.wait_ge(s["masked"], (n + 1) * MC)
                    for i in range(SEQ_TILES):
                        if not (isinstance(n, int) and n == 0):
                            pe.wait_ge(s["added"], SEQ_TILES * (n - 1) + (i + 1))
                        for mc in range(MC):
                            nc.tensor.matmul(psY[:, i, 0:D], H[:, par, mc, i * P:(i + 1) * P], w2[:, mc, :], start=(mc == 0), stop=False)
                        nc.tensor.matmul(psY[:, i, 0:D], m.ones[0:1, :], b2[:], start=False, stop=True).then_inc(s["made"], 1)

                pe.wait_ge(s["w_loaded"], 32)
                hidden(0)
                hidden(1)
                output(0, 0)
                with pe.Fori(0, BATCH // 2 - 1) as pair:
                    n = pair * 2 + 1
                    hidden(n + 1)
                    output(n, 1)
                    hidden(n + 2)
                    output(n + 1, 0)
                output(BATCH - 1, 1)

            @block.scalar
            def _(act):
                with act.Fori(0, BATCH // 2) as pair:
                    n0 = pair * 2
                    for k in range(2):
                        n = n0 + k
                        for mc in range(MC):
                            act.wait_ge(s["hidden"], n * MC + (mc + 1))
                            if mc == 0:
                                act.wait_ge(s["h_unused"], n + 1)
                            nc.scalar.activation(H[:, k, mc, :], psH[:, mc % 2, :], ACT.Relu, bias=b1[:, mc:mc + 1]).then_inc(s["relu"], 1)

            @block.vector
            def _(v):
                def mask_hidden(n, k):
                    for mc in range(MC):
                        v.wait_ge(s["relu"], n * MC + (mc + 1))
                        v.wait_ge(s["spread"], n * MC + (mc + 1))
                        nc.vector.tensor_tensor(H[:, k, mc, :], psM[:, mc % 2, :], H[:, k, mc, :], ALU.mult).then_inc(s["masked"], 1)

                def add_output(n):
                    for i in range(SEQ_TILES):
                        v.wait_ge(s["made"], SEQ_TILES * n + (i + 1))
                        row = m.resid[:, bass.ds(n * SEQ_TILES + i, 1), :].rearrange("p o d -> p (o d)")
                        nc.vector.tensor_tensor(row, psY[:, i, 0:D], row, ALU.add).then_inc(s["added"], 1)
                    v.drain().then_inc(s["h_unused"], 1)

                v.drain().then_inc(s["h_unused"], 2)
                mask_hidden(0, 0)
                with v.Fori(0, BATCH // 2 - 1) as pair:
                    n = pair * 2
                    mask_hidden(n + 1, 1)
                    add_output(n)
                    mask_hidden(n + 2, 0)
                    add_output(n + 1)
                mask_hidden(BATCH - 1, 1)
                add_output(BATCH - 2)
                add_output(BATCH - 1)

            @block.sync
            def _(sp):
                with sp.Fori(0, BATCH) as n:
                    sp.wait_ge(s["added"], SEQ_TILES * (n + 1))
                    sp.dma_start(out_tiles[:, bass.ds(n * SEQ_TILES, SEQ_TILES), :], m.resid[:, bass.ds(n * SEQ_TILES, SEQ_TILES), :]).then_inc(s["stored"], 16)
                sp.wait_ge(s["stored"], 16 * BATCH)


class Memory:
    pass


def lm_tower(nc, t, out, stop=None):
    m = Memory()
    m.parts_dram = [nc.dram_tensor(n, (BATCH, 3, D, SEQ), BF16, kind="Internal").ap() for n in ("q_parts", "k_parts")]
    out = out.rearrange("b s d -> (b s) d")

    def dump(sems):
        with nc.Block() as block:
            @block.sync
            def _(sp):
                d = sems("dumped")
                sp.dma_start(out.rearrange("(n p) d -> p n d", p=P), m.resid[:]).then_inc(d, 16)
                sp.wait_ge(d, 16)

    with ExitStack() as c:
        sems = lambda n: c.enter_context(nc.semaphore(n))
        sb = lambda st, n, sh, dt=F32: st.enter_context(nc.sbuf_tensor(n, sh, dt))
        m.ident = sb(c, "ident", [P, P])
        m.ids = sb(c, "ids", [P, TILES], I32)
        m.s_col = sb(c, "s_col", [RANK, 1])
        m.vt = sb(c, "vt", [RANK, D])
        m.qk_bias = sb(c, "qk_bias", [P, 2 * DC])
        m.half_mask = sb(c, "half_mask", [P, HALF])
        m.rank8 = sb(c, "rank8", [P, 8])
        m.eps = sb(c, "eps", [P, 1])
        m.ones = sb(c, "ones", [P, P])
        m.resid = sb(c, "resid", [P, TILES, D])
        load_constants(nc, t, m, sems)
        embed(nc, t, m, sems)
        if stop == "embed":
            return dump(sems)
        with ExitStack() as c0:
            m.v_aug = sb(c0, "v_aug", [P, BH, SEQ_TILES, HD + 1])
            m.thr0 = sb(c0, "thr0", [P, BH, SEQ_TILES])
            m.step = sb(c0, "step", [P, BH, SEQ_TILES])
            with ExitStack() as c1:
                m.xT = sb(c1, "xT", [P, DC, TOKENS])
                norm_turn(nc, m, sems, "_0", m.resid, None, m.xT)
                qkv(nc, t, m, sems)
            m.heads_out = sb(c0, "heads_out", [P, BH, SEQ_TILES, HD])
            attend(nc, t, m, sems)
            project(nc, t, m, sems)
        if stop == "attn":
            return dump(sems)
        m.xT = sb(c, "xT1", [P, DC, TOKENS])
        norm_turn(nc, m, sems, "_1", m.resid, None, m.xT)
        moe(nc, t, m, sems)
        if stop == "moe":
            return dump(sems)
        cos_attention(nc, t, m, sems)
        if stop == "cos":
            return dump(sems)
        norm_turn(nc, m, sems, "_2", m.resid, None, m.xT)
        block_ffn(nc, t, m, sems, out)


def layouts(i):
    r = {}
    a = {k: np.asarray(v) for k, v in i.items()}
    r["ids"] = a["x"].reshape(TILES, P).T
    r["U"], r["s_col"], r["Vt"] = a["L0_tok_U"], a["L0_tok_s"].reshape(RANK, 1), a["L0_tok_Vt"]
    r["W_qkvT"] = a["L0_attn_W_qkv"].T
    r["qk_bias"] = a["L0_attn_b_qkv"][:2 * D].reshape(2 * DC, P).T
    r["v_bias"] = a["L0_attn_b_qkv"][2 * D:].reshape(1, D)
    r["W_outT"], r["b_out"] = a["L0_attn_W_out"].T, a["L0_attn_b_out"].reshape(1, D)
    r["router_w"], r["router_b"] = a["L0_ffn_router_w"], a["L0_ffn_router_b"].reshape(1, EXPERTS)
    r["w1_all"] = np.concatenate([a["L0_ffn_sw1"][None], a["L0_ffn_rw1"]])
    r["w2_all"] = np.concatenate([a["L0_ffn_sw2"][None], a["L0_ffn_rw2"]])
    r["b1_all"] = np.concatenate([a["L0_ffn_sb1"][None], a["L0_ffn_rb1"]]).reshape(-1, P).T
    r["sb2"], r["rb2"] = a["L0_ffn_sb2"].reshape(1, D), a["L0_ffn_rb2"]
    for x in "qkvo":
        r["A_" + x] = a[f"L1_attn_{x}A"].reshape(PHM, DC, 2, PHM).transpose(2, 0, 1, 3).reshape(2, -1)
        r["S_" + x], r["bias_" + x] = a[f"L1_attn_{x}S"], a[f"L1_attn_{x}b"].reshape(1, D)
    for x in ("g1", "b1", "g2", "b2"):
        r[x] = a["L1_attn_" + x].reshape(1, D)
    r["ffn_rwT"], r["ffn_rb"] = a["L1_ffn_router_w"].T, a["L1_ffn_router_b"].reshape(1, BLOCKS)
    r["ffn_w1T"], r["ffn_w2T"] = a["L1_ffn_w1"].T, a["L1_ffn_w2"].T
    r["ffn_b1"], r["ffn_b2"] = a["L1_ffn_b1"].reshape(-1, P).T, a["L1_ffn_b2"].reshape(1, D)
    r["ident"] = np.eye(P, dtype=np.float32)
    r["half_mask"] = np.repeat(np.eye(HALF, dtype=np.float32), HD, axis=0)
    r["rank8"] = np.arange(8, dtype=np.float32).reshape(1, 8)
    angle = (np.pi / 2) * np.arange(1, BATCH + 1) / BATCH
    r["cosines"] = np.cos(angle[:, None] - angle[None, :]).astype(np.float32).reshape(1, -1)
    r["spread"] = np.repeat(np.eye(BLOCKS, dtype=np.float32), BLOCK, axis=1)
    return {k: np.ascontiguousarray(v) for k, v in r.items()}


def kernel(**inputs):
    import concourse.bacc as bacc
    from concourse.bass_utils import run_bass_kernel_spmd

    nc = bacc.Bacc("TRN2", target_bir_lowering=False, num_devices=1)
    arrays = {f"in_{k}": v for k, v in layouts(inputs).items()}
    t = {k[3:]: nc.dram_tensor(k, v.shape, mybir.dt.from_np(v.dtype), kind="ExternalInput").ap() for k, v in arrays.items()}
    out = nc.dram_tensor("out_0", (BATCH, SEQ, D), F32, kind="ExternalOutput").ap()
    lm_tower(nc, t, out)
    r = run_bass_kernel_spmd(nc, [arrays], core_ids=[0])
    return r.results[0]["out_0"]
```

```python
from contextlib import ExitStack

import numpy as np

import concourse.bass as bass
from concourse import mybir

ALU = mybir.AluOpType
ACT = mybir.ActivationFunctionType
AX = mybir.AxisListType
F32 = mybir.dt.float32
BF16 = mybir.dt.bfloat16
I32 = mybir.dt.int32

P = 128
BATCH, SEQ, D = 8, 512, 256
TOKENS = BATCH * SEQ
TILES = TOKENS // P
SEQ_TILES = SEQ // P
DC = D // P
RANK = 64
HEADS, HD = 16, 16
HALF = HEADS // 2
BH = BATCH * HEADS
KEEP = int(SEQ * 0.3)
QK_SCALE = D ** -0.5
PARTS_Q = (0, 0, 0, 1, 1, 1, 2, 2)
PARTS_K = (0, 1, 2, 0, 1, 2, 0, 1)
SLOTS = len(PARTS_Q)
BIG = 2.0 ** 100
WINDOW = 8
LN_EPS = 1e-5
EXPERTS, TOP_E, EH = 8, 2, 512
BLOCKS, BLOCK, TOP_B, OUTF = 16, 64, 4, 1024
FULL_SLOT = 42
PHM = 4


START = 1


STAGE_SEMAPHORES = {'qkv': ['proj', 'biased', 'part1', 'rest1', 'part2', 'part3', 'stored', 'squares', 'kstats', 'guess', 'guess_kept', 'v_made',
         'v_kept', 'sd', 'ones'],
 'attend': ['half0_loaded', 'half1_loaded', 'scores', 'copied', 'count0', 'count1', 'count2', 'thr1', 'thr2', 'masked', 'pushed',
            'best8', 'replaced', 'over', 'picked', 'exps', 'probs', 'turned', 'moved', 'pv', 'normed', 'needs', 'over_read',
            'small', 'nmaxed', 'kept'],
 'moe': ['small', 'logits', 'shifted', 'exped', 'weights', 'wT_made', 'wT_kept', 'bias_made', 'bias_added', 'w_loaded0',
         'w_loaded1', 'hidden', 'active', 'made', 'h_unused', 'y_free'],
 'cos': ['loaded', 'built', 'made', 'kept', 'scored', 'mixed', 'summed', 'norm', 'omade', 'oadded'],
 'ffn': ['small', 'w_loaded', 'logits', 'shifted', 'exped', 'mask', 'mT_made', 'mT_kept', 'hidden', 'spread', 'relu', 'masked',
         'made', 'added', 'stored', 'h_unused']}


class Steps:

    def __init__(self, engine, semaphore, base):
        self.engine, self.semaphore, self.base, self.number = engine, semaphore, base, {}

    def did(self, name, operation):
        operation.then_inc(self.semaphore, 1)
        self.number[name] = len(self.number) + 1

    def after(self, name):
        self.engine.wait_ge(self.semaphore, self.base + self.number[name])

    def end(self):
        return self.base + len(self.number)


def load_constants(nc, t, m, sems):
    loaded = sems("const_loaded")
    with nc.Block() as block:
        @block.sync
        def _(sp):
            pairs = [(m.ident[:], t["ident"]), (m.ids[:], t["ids"]), (m.s_col[:], t["s_col"]),
                     (m.vt[:], t["Vt"]), (m.qk_bias[:], t["qk_bias"]), (m.half_mask[:], t["half_mask"]),
                     (m.rank8[:], t["rank8"].to_broadcast((P, 8)))]
            for dst, src in pairs:
                sp.dma_start(dst, src).then_inc(loaded, 16)
            sp.wait_ge(loaded, 16 * len(pairs))

            for stage in m.sem.values():
                for semaphore in stage.values():
                    sp.sem_inc(semaphore, START)

        @block.vector
        def _(v):
            nc.vector.memset(m.eps[:], LN_EPS)
            nc.vector.memset(m.ones[:], 1.0)
            v.wait_ge(loaded, 16 * 7)
            nc.vector.tensor_scalar(m.qk_bias[:, 0:DC], m.qk_bias[:, 0:DC], QK_SCALE, None, ALU.mult)


def embed(nc, t, m, sems):
    gathered = [sems(f"gathered{g}") for g in range(4)]
    turned, scaled, made, kept = sems("u_turned"), sems("u_scaled"), sems("rows_made"), sems("rows_kept")
    with ExitStack() as c:
        rows = c.enter_context(nc.sbuf_tensor("u_rows", [P, TILES, RANK], F32))
        uT = c.enter_context(nc.sbuf_tensor("uT", [RANK, 2, SEQ], F32))
        psT = c.enter_context(nc.psum_tensor("psT_emb", [P, 2, 512], F32))
        psH = c.enter_context(nc.psum_tensor("psH_emb", [P, 4, 512], F32))
        block = c.enter_context(nc.Block())

        @block.gpsimd
        def _(pool):
            for i in range(TILES):
                pool.indirect_dma_start(
                    out=rows[:, i, :], out_offset=None, in_=t["U"],
                    in_offset=bass.IndirectOffsetOnAxis(ap=m.ids[:, i:i + 1], axis=0),
                ).then_inc(gathered[i // 8], 16)

        @block.tensor
        def _(pe):
            for g in range(BATCH):
                if g % 2 == 0:
                    pe.wait_ge(gathered[g // 2], 16 * 8)
                if g >= 2:
                    pe.wait_ge(scaled, g - 1)
                for j in range(4):
                    tr = nc.tensor.transpose(psT[0:RANK, g % 2, j * P:(j + 1) * P], rows[:, 4 * g + j, :], m.ident[:])
                tr.then_inc(turned, 1)
                pe.wait_ge(scaled, g + 1)
                if g >= 2:
                    pe.wait_ge(kept, 2 * (g - 1))
                for j in range(4):
                    nc.tensor.matmul(psH[:, 2 * (g % 2) + j // 2, (j % 2) * D:(j % 2 + 1) * D],
                                     uT[:, g % 2, j * P:(j + 1) * P], m.vt[:],
                                     start=True, stop=True, skip_group_check=True).then_inc(made, 1)

        @block.vector
        def _(v):
            for g in range(BATCH):
                v.wait_ge(turned, g + 1)
                if g >= 2:
                    v.wait_ge(made, 4 * (g - 1))
                nc.vector.tensor_scalar(uT[:, g % 2, :], psT[0:RANK, g % 2, :], m.s_col[:], None, ALU.mult).then_inc(scaled, 1)

        @block.scalar
        def _(act):
            for i in range(0, TILES, 2):
                act.wait_ge(made, i + 2)
                nc.scalar.copy(m.resid[:, i:i + 2, :], psH[:, (i // 2) % 4, :].rearrange("p (n d) -> p n d", n=2)).then_inc(kept, 1)


def norm_stats(nc, v, st, src, mean, var, n=TILES):
    with v.Fori(0, n) as i:
        nc.vector.bn_stats(st[:, bass.ds(i, 1), :], src[:, bass.ds(i, 1), :])
    v.drain()
    even, odd = st[:, :, 1:2].rearrange("p n a -> p (n a)"), st[:, :, 4:5].rearrange("p n a -> p (n a)")
    m2e, m2o = st[:, :, 2:3].rearrange("p n a -> p (n a)"), st[:, :, 5:6].rearrange("p n a -> p (n a)")
    nc.vector.tensor_tensor(mean, even, odd, ALU.add)
    nc.vector.tensor_tensor(var, even, odd, ALU.subtract)
    v.drain()
    nc.vector.tensor_scalar(mean, mean, 0.5, None, ALU.mult)
    nc.vector.tensor_tensor(var, var, var, ALU.mult)
    nc.vector.tensor_tensor(m2e, m2e, m2o, ALU.add)
    v.drain()
    nc.vector.tensor_scalar(var, var, 0.25, None, ALU.mult)
    nc.vector.tensor_scalar(m2e, m2e, 1.0 / D, None, ALU.mult)
    v.drain()
    nc.vector.tensor_tensor(var, var, m2e, ALU.add)


def norm_turn(nc, m, sems, tag, src, keep, xT, gain=None, shift=None):
    vars_ready, root, rows_ready = sems("vars_ready" + tag), sems("root" + tag), sems("xhat_ready" + tag)
    turned, moved = sems("x_turned" + tag), sems("x_moved" + tag)
    G = 2
    STEPS = TILES // G
    WIDE = 8
    with ExitStack() as c:
        st = c.enter_context(nc.sbuf_tensor("ln_st" + tag, [P, TILES, 6], F32))
        mean = c.enter_context(nc.sbuf_tensor("ln_mean" + tag, [P, TILES], F32))
        var = c.enter_context(nc.sbuf_tensor("ln_var" + tag, [P, TILES], F32))
        rstd = c.enter_context(nc.sbuf_tensor("ln_rstd" + tag, [P, TILES], F32))
        ring = None
        if keep is None:
            ring = c.enter_context(nc.sbuf_tensor("xhat" + tag, [P, 2 * G, D], F32))
        ps = c.enter_context(nc.psum_tensor("psN" + tag, [P, 2, 512], F32))
        block = c.enter_context(nc.Block())
        row = (lambda i: ring[:, i % (2 * G), :]) if keep is None else (lambda i: keep[:, i, :])

        @block.vector
        def _(v):
            norm_stats(nc, v, st, src, mean[:], var[:])
            v.drain().then_inc(vars_ready, 1)
            v.wait_ge(root, 1)
            nc.vector.reciprocal(rstd[:], rstd[:])
            v.drain()
            for i in range(TILES):
                step = i // G
                if keep is None and i % G == 0 and step >= 2:
                    v.wait_ge(turned, step - 1)
                op = nc.vector.tensor_scalar(row(i), src[:, i, :], mean[:, i:i + 1], rstd[:, i:i + 1], ALU.subtract, ALU.mult)
                if i % G == G - 1 and gain is None:
                    op.then_inc(rows_ready, 1)
                if gain is not None and i % WIDE == WIDE - 1:
                    v.drain()
                    part = keep[:, i - WIDE + 1:i + 1, :]
                    for other, how in ((gain, ALU.mult), (shift, ALU.add)):
                        nc.vector.tensor_tensor(part, part, other.rearrange("p (o d) -> p o d", o=1).to_broadcast((P, WIDE, D)), how)
                        last = v.drain()
                    last.then_inc(rows_ready, WIDE // G)

        @block.tensor
        def _(pe):
            for s in range(STEPS):
                pe.wait_ge(rows_ready, s + 1)
                if s >= 2:
                    pe.wait_ge(moved, s - 1)
                for ch in range(DC):
                    for j in range(G):
                        tr = nc.tensor.transpose(ps[:, s % 2, (ch * G + j) * P:(ch * G + j + 1) * P],
                                                 row(s * G + j)[:, ch * P:(ch + 1) * P], m.ident[:])
                tr.then_inc(turned, 1)

        @block.scalar
        def _(act):
            act.wait_ge(vars_ready, 1)
            nc.scalar.activation(rstd[:], var[:], ACT.Sqrt, bias=m.eps[:]).then_inc(root, 1)
            for s in range(STEPS):
                act.wait_ge(turned, s + 1)
                nc.scalar.copy(xT[:, :, s * G * P:(s + 1) * G * P],
                               ps[:, s % 2, :].rearrange("p (c n) -> p c n", c=DC)).then_inc(moved, 1)


def qkv(nc, t, m, sems):
    w_loaded = sems("w_qkv_loaded")
    s = m.sem["qkv"]
    NCH = 2 * DC
    with ExitStack() as c:
        sb = lambda n, sh, dt=F32: c.enter_context(nc.sbuf_tensor(n, sh, dt))
        w = sb("w_qkv", [P, DC, 3 * D])
        vb = sb("v_bias", [P, D])
        qk = sb("qk", [P, NCH, SEQ])
        rest = sb("rest", [P, NCH, SEQ])
        parts = sb("parts", [P, NCH, 3, SEQ], BF16)
        sq = sb("q_sq", [P, DC, SEQ])
        kst = sb("k_st", [P, DC, 6])
        kmv = sb("k_mv", [P, DC, 2])
        kdiag = sb("k_diag", [P, DC, 2, HALF])
        psQ = c.enter_context(nc.psum_tensor("psQ_qkv", [P, NCH, 512], F32))
        psV = c.enter_context(nc.psum_tensor("psV_qkv", [P, 2, 512], F32))
        psG = c.enter_context(nc.psum_tensor("psG_qkv", [P, 512], F32))
        guess = psG[:, 0:SEQ_TILES * DC * 2 * HALF].rearrange("p (i c a h) -> p i c a h", i=SEQ_TILES, c=DC, a=2)
        block = c.enter_context(nc.Block())

        @block.sync
        def _(sp):
            sp.dma_start(w[:], t["W_qkvT"].rearrange("(c p) e -> p c e", p=P)).then_inc(w_loaded, 16)
            sp.dma_start(vb[:], t["v_bias"].to_broadcast((P, D))).then_inc(w_loaded, 16)
            with sp.Fori(0, BATCH) as b:
                for j in range(NCH):
                    which, ch = j // DC, j % DC
                    sp.wait_ge(s["part3"], START + b * NCH + (j + 1))
                    dst = m.parts_dram[which][bass.ds(b, 1), :, ch * P:(ch + 1) * P, :].rearrange("o a p n -> p (o a) n")
                    sp.dma_start(dst, parts[:, j, :, :]).then_inc(s["stored"], 16)
            sp.wait_ge(s["stored"], START + 16 * BATCH * NCH)

        @block.tensor
        def _(pe):
            pe.wait_ge(w_loaded, 32)
            for b in range(BATCH):
                pe.wait_ge(s["biased"], START + b * NCH)
                for j in range(NCH):
                    for ch in range(DC):
                        mm = nc.tensor.matmul(psQ[:, j, :], w[:, ch, j * P:(j + 1) * P],
                                              m.xT[:, ch, bass.ds(b * SEQ, SEQ)], start=(ch == 0), stop=(ch == DC - 1))
                    mm.then_inc(s["proj"], 1)
                pe.wait_ge(s["v_kept"], START + b * SEQ_TILES)
                for i in range(SEQ_TILES):
                    for ch in range(DC):
                        mm = nc.tensor.matmul(psV[:, i // 2, (i % 2) * D:(i % 2 + 1) * D],
                                              m.xT[:, ch, bass.ds(b * SEQ + i * P, P)], w[:, ch, 2 * D:3 * D],
                                              start=(ch == 0), stop=(ch == DC - 1), skip_group_check=True)
                    mm.then_inc(s["v_made"], 1)
                pe.wait_ge(s["squares"], START + (b + 1) * DC)
                pe.wait_ge(s["kstats"], START + b + 1)
                pe.wait_ge(s["guess_kept"], START + b)
                for i in range(SEQ_TILES):
                    for ch in range(DC):
                        nc.tensor.matmul(guess[:, i, ch, 0, :], qk[:, ch, i * P:(i + 1) * P], kdiag[:, ch, 0, :],
                                         start=True, stop=True, skip_group_check=True)
                        mm = nc.tensor.matmul(guess[:, i, ch, 1, :], sq[:, ch, i * P:(i + 1) * P], kdiag[:, ch, 1, :],
                                              start=True, stop=True, skip_group_check=True)
                mm.then_inc(s["guess"], 1)

        @block.scalar
        def _(act):
            with act.Fori(0, BATCH) as b:
                act.wait_ge(s["guess"], START + b)
                act.wait_ge(s["rest1"], START + b * NCH)
                for j in range(NCH):
                    act.wait_ge(s["proj"], START + b * NCH + (j + 1))
                    nc.scalar.activation(qk[:, j, :], psQ[:, j, :], ACT.Identity, bias=m.qk_bias[:, j:j + 1],
                                         scale=QK_SCALE if j < DC else 1.0).then_inc(s["biased"], 1)
                for ch in range(DC):
                    act.wait_ge(s["biased"], START + b * NCH + (ch + 1))
                    nc.scalar.activation(sq[:, ch, :], qk[:, ch, :], ACT.Square).then_inc(s["squares"], 1)
                for j in range(NCH):
                    act.wait_ge(s["rest1"], START + b * NCH + (j + 1))
                    nc.scalar.copy(parts[:, j, 1, :], rest[:, j, :]).then_inc(s["part2"], 1)
            act.wait_ge(s["guess_kept"], START + BATCH)
            nc.scalar.activation(m.step[:], m.step[:], ACT.Sqrt).then_inc(s["sd"], 1)

        @block.gpsimd
        def _(pool):
            with pool.Fori(0, BATCH) as b:
                for j in range(NCH):
                    pool.wait_ge(s["part2"], START + b * NCH + (j + 1))
                    nc.gpsimd.tensor_tensor(parts[:, j, 2, :], rest[:, j, :], parts[:, j, 1, :], ALU.subtract).then_inc(s["part3"], 1)

        @block.vector
        def _(v):
            nc.vector.memset(m.v_aug[:, :, :, HD:HD + 1], 1.0).then_inc(s["ones"], 1)
            v.wait_ge(w_loaded, 32)
            with v.Fori(0, BATCH) as b:
                v.wait_ge(s["stored"], START + 16 * NCH * b)
                v.wait_ge(s["guess"], START + b)
                for j in range(NCH):
                    v.wait_ge(s["biased"], START + b * NCH + (j + 1))
                    nc.vector.tensor_copy(parts[:, j, 0, :], qk[:, j, :]).then_inc(s["part1"], 1)
                    if j >= DC:
                        nc.vector.bn_stats(kst[:, j - DC, :], qk[:, j, :])
                    v.wait_ge(s["part1"], START + b * NCH + (j + 1))
                    nc.vector.tensor_tensor(rest[:, j, :], qk[:, j, :], parts[:, j, 0, :], ALU.subtract).then_inc(s["rest1"], 1)
                v.drain()
                for ch in range(DC):
                    nc.vector.bn_aggr(kmv[:, ch, :], kst[:, ch, :])
                v.drain()
                for ch in range(DC):
                    for a in range(2):
                        op = nc.vector.tensor_scalar(kdiag[:, ch, a, :], m.half_mask[:], kmv[:, ch, a:a + 1], None, ALU.mult)
                op.then_inc(s["kstats"], 1)
                for i in range(SEQ_TILES):
                    v.wait_ge(s["v_made"], START + b * SEQ_TILES + (i // 2 * 2 + 2))
                    nc.vector.tensor_tensor(m.v_aug[:, bass.ds(b * HEADS, HEADS), i, 0:HD],
                                            psV[:, i // 2, (i % 2) * D:(i % 2 + 1) * D].rearrange("p (h d) -> p h d", h=HEADS),
                                            vb[:].rearrange("p (h d) -> p h d", h=HEADS), ALU.add).then_inc(s["v_kept"], 1)
                v.wait_ge(s["guess"], START + b + 1)
                for ch in range(DC):
                    nc.vector.tensor_copy(m.thr0[:, bass.ds(b * HEADS + ch * HALF, HALF), :],
                                          guess[:, :, ch, 0, :].rearrange("p i h -> p h i"))
                    op = nc.vector.tensor_copy(m.step[:, bass.ds(b * HEADS + ch * HALF, HALF), :],
                                               guess[:, :, ch, 1, :].rearrange("p i h -> p h i"))
                v.drain().then_inc(s["guess_kept"], 1)
            v.wait_ge(s["sd"], START + 1)
            nc.vector.scalar_tensor_tensor(m.thr0[:], m.step[:], -0.545, m.thr0[:], ALU.mult, ALU.subtract)
            v.drain()
            nc.vector.tensor_scalar(m.step[:], m.step[:], 0.5 / (SEQ * 0.313), None, ALU.mult)


def attend(nc, t, m, sems):
    s = m.sem["attend"]
    ST = SEQ_TILES
    HB = 2 * BATCH
    with ExitStack() as c:
        sb = lambda n, sh, dt=F32: c.enter_context(nc.sbuf_tensor(n, sh, dt))
        ring = [sb(n, [P, HEADS, SEQ], BF16) for n in ("q_ring", "k_ring")]
        X = sb("X", [P, 2, ST, SEQ])
        E = sb("E", [P, 2, ST, SEQ])
        sgn = sb("sgn", [P, 2, ST, SEQ], BF16)
        M = sb("M", [P, ST, SEQ], BF16)
        Z = sb("Z", [P, ST, SEQ])
        kept = sb("kept", [P, ST, SEQ], BF16)
        gate = sb("gate", [P, 1])
        PT = sb("PT", [P, ST, SEQ])
        push = sb("push", [P, P], BF16)
        nmax = sb("nmax", [P, 2, ST])
        cnt = sb("cnt", [P, 3, ST])
        dist = sb("dist", [P, 4, ST])
        nthr = sb("nthr", [P, 4, ST])
        thr = sb("thr", [P, ST])
        top = sb("top", [P, ST])
        slope, wish, sq_d, gap, partner = (sb("upd_" + n, [P, ST]) for n in ("slope", "wish", "sq", "gap", "partner"))
        mv = sb("upd_moves", [P, 3, ST])
        flip = sb("upd_flips", [P, 3, ST], I32)
        c3 = sb("c3", [P, ST])
        need = sb("need", [P, ST])
        lim = sb("lim", [P, ST, 8])
        best = sb("best", [P, ST, 8])
        overs = sb("overs", [P, 3, ST])
        code = sb("code", [1, 1], I32)
        flags = sb("flags", [1, 3 * ST])
        flag_weights = sb("flag_weights", [1, 3 * ST])
        rz = sb("rz", [P, ST, 1])
        psS = c.enter_context(nc.psum_tensor("psS_at", [P, ST, 512], F32))
        psT = c.enter_context(nc.psum_tensor("psPT_at", [P, 3, 512], F32))
        psO = c.enter_context(nc.psum_tensor("psO_at", [P, 512], F32))
        O = psO[:, 0:ST * (HD + 1)].rearrange("p (i d) -> p i d", i=ST)
        over_ps = psO[0:1, 256:256 + 3 * ST]
        block = c.enter_context(nc.Block())

        @block.sync
        def _(sp):
            def load(hb_of, half):
                for which, parts in ((0, PARTS_Q), (1, PARTS_K)):
                    for slot in range(SLOTS):
                        src = m.parts_dram[which][bass.ds(hb_of, 1), parts[slot], half * P:(half + 1) * P, :]
                        sp.dma_start(ring[which][slot * HD:(slot + 1) * HD, half * HALF:(half + 1) * HALF, :],
                                     src.rearrange("o (h d) n -> d (o h) n", d=HD)).then_inc(s[f"half{half}_loaded"], 16)
            load(0, 0)
            load(0, 1)
            with sp.Fori(1, BATCH) as b:
                for half in range(2):
                    sp.wait_ge(s["pushed"], START + ST * (HEADS * (b - 1) + (half + 1) * HALF))
                    load(b, half)

        @block.tensor
        def _(pe):
            def ring_ready(h):
                load = 2 * SLOTS * 16
                pe.wait_ge(s["half0_loaded"], START + load * (h // HEADS + 1))
                pe.wait_ge(s["half1_loaded"], START + load * ((h + HALF) // HEADS))

            def scores(h, i):
                r = h % HEADS
                return nc.tensor.matmul(psS[:, i, :], ring[0][:, bass.ds(r, 1), i * P:(i + 1) * P].rearrange("p o n -> p (o n)"),
                                        ring[1][:, bass.ds(r, 1), :].rearrange("p o n -> p (o n)"), start=True, stop=True)

            def first_scores(h):
                ring_ready(h)
                for i in range(ST):
                    scores(h, i).then_inc(s["scores"], 1)

            def push_selected(h):
                r = h % HEADS
                for i in range(ST):
                    pe.wait_ge(s["masked"], START + ST * h + (i + 1))
                    nc.tensor.matmul(psS[:, i, :], ring[0][:, bass.ds(r, 1), i * P:(i + 1) * P].rearrange("p o n -> p (o n)"),
                                     ring[1][:, bass.ds(r, 1), :].rearrange("p o n -> p (o n)"), start=True, stop=False)
                    nc.tensor.matmul(psS[:, i, :], push[:], M[:, i, :], start=False, stop=True).then_inc(s["pushed"], 1)

            def next_scores(h):
                ring_ready(h)
                for i in range(ST):
                    pe.wait_ge(s["replaced"], START + ST * (h - 2) + (i + 1))
                    scores(h, i).then_inc(s["scores"], 1)

            def count_over(h):
                pe.wait_ge(s["needs"], START + h + 1)
                if not (isinstance(h, int) and h < 2):
                    pe.wait_ge(s["normed"], START + h - 1)
                nc.tensor.matmul(over_ps, m.ones[:, 0:1], overs[:].rearrange("p a i -> p (a i)"),
                                 start=True, stop=True, skip_group_check=True).then_inc(s["over"], 1)

            def values(h):
                pe.wait_ge(s["moved"], START + ST * (h + 1))
                pe.wait_ge(s["over_read"], START + (BH if isinstance(h, int) and h >= BH - 2 else h + 2))
                if not (isinstance(h, int) and h == 0):
                    pe.wait_ge(s["normed"], START + h)
                for i in range(ST):
                    for j in range(ST):
                        mm = nc.tensor.matmul(O[:, i, :], PT[:, i, j * P:(j + 1) * P],
                                              m.v_aug[:, bass.ds(h, 1), j, :].rearrange("p o d -> p (o d)"),
                                              start=(j == 0), stop=(j == ST - 1), skip_group_check=True)
                mm.then_inc(s["pv"], 1)

            def turn(h, par, tiles):
                for i in tiles:
                    pe.wait_ge(s["moved"], START + ST * h + (1 if i == 3 else 0))
                    pe.wait_ge(s["probs"], START + ST * h + (i + 1))
                    for j in range(ST):
                        tr = nc.tensor.transpose(psT[:, i % 3, j * P:(j + 1) * P], E[:, par, i, j * P:(j + 1) * P], m.ident[:])
                    tr.then_inc(s["turned"], 1)

            def slot(sl, par, prev=True, nxt=True):
                if prev:
                    push_selected(sl - 1)
                    count_over(sl - 1)
                turn(sl - 2, par, range(ST))
                if nxt:
                    next_scores(sl + 1)
                values(sl - 2)

            first_scores(0)
            for i in range(ST):
                pe.wait_ge(s["copied"], START + i + 1)
                if i == 0:
                    ring_ready(1)
                scores(1, i).then_inc(s["scores"], 1)
            push_selected(0)
            count_over(0)
            next_scores(2)
            with pe.Fori(1, BH // 2 - 1) as pair:
                s0 = pair * 2
                slot(s0, 0)
                slot(s0 + 1, 1)
            slot(BH - 2, 0)
            slot(BH - 1, 1, nxt=False)
            slot(BH, 0, nxt=False)
            slot(BH + 1, 1, prev=False, nxt=False)

        @block.scalar
        def _(act):
            def count(h, par, which):
                if which == 0:
                    pass
                else:
                    act.wait_ge(s[f"thr{which}"], START + h + 1)
                for i in range(ST):
                    if which == 0:
                        act.wait_ge(s["copied"], START + ST * h + (i + 1))
                    bias = m.thr0[:, bass.ds(h, 1), i:i + 1].rearrange("p o i -> p (o i)") if which == 0 else nthr[:, which, i:i + 1]
                    nc.scalar.activation(sgn[:, 1 if which else 0, i, :], X[:, par, i, :], ACT.Sign, bias=bias,
                                         accum_out=cnt[:, which, i:i + 1]).then_inc(s[f"count{which}"], 1)

            def exps(h, par, first=False):
                act.wait_ge(s["nmaxed"], START + h + 1)
                if not first:
                    act.wait_ge(s["turned"], START + ST * (h - 1))
                for i in range(ST):
                    nc.scalar.activation(E[:, par, i, :], X[:, par, i, :], ACT.Exp, bias=nmax[:, par, i:i + 1]).then_inc(s["exps"], 1)

            def move(h):
                act.wait_ge(s["pv"], START + h)
                for i in range(ST):
                    act.wait_ge(s["turned"], START + ST * h + (i + 1))
                    nc.scalar.copy(PT[:, i, :], psT[:, i % 3, :]).then_inc(s["moved"], 1)

            def slot(sl, par, old, early=False):
                count(sl, par, 0)
                count(sl, par, 1)
                if old:
                    move(sl - 2)
                exps(sl, par, early)
                count(sl, par, 2)

            slot(0, 0, False, True)
            slot(1, 1, False, True)
            with act.Fori(1, BH // 2) as pair:
                s0 = pair * 2
                slot(s0, 0, True)
                slot(s0 + 1, 1, True)
            move(BH - 2)
            move(BH - 1)

        @block.gpsimd
        def _(pool):
            with pool.Fori(0, BH // 2) as pair:
                h0 = pair * 2
                for k in range(2):
                    h = h0 + k
                    pool.wait_ge(s["exps"], START + ST * (h + 1))
                    pool.wait_ge(s["picked"], START + h + 1)
                    pool.wait_ge(s["probs"], START + ST * h)
                    nc.gpsimd.tensor_tensor(gate[:], m.ones[:, 0:1], m.ones[:, 0:1], ALU.mult)
                    for i in range(ST):
                        nc.gpsimd.tensor_scalar(kept[:, i, :], Z[:, i, :], -BIG / 2, None, ALU.is_lt).then_inc(s["kept"], 1)
                    for i in range(ST):
                        pool.wait_ge(s["kept"], START + ST * h + (i + 1))
                        nc.gpsimd.tensor_tensor(E[:, k, i, :], E[:, k, i, :], kept[:, i, :], ALU.mult).then_inc(s["probs"], 1)

        @block.vector
        def _(v):
            AIM = KEEP - WINDOW // 2
            OFF = (0.0, 0.25, 0.625)
            FAR2 = (WINDOW + 1.0) ** 2

            def row(ap, h):
                return ap[:, bass.ds(h, 1), :].rearrange("p o i -> p (o i)")

            def mask(h, par, i):
                nc.vector.tensor_scalar(M[:, i, :], X[:, par, i, :], thr[:, i:i + 1], None, ALU.is_gt, ALU.add,
                                        accum_out=c3[:, i:i + 1]).then_inc(s["masked"], 1)

            def copy_scores(h, par, i):
                v.wait_ge(s["scores"], START + ST * h + (i + 1))
                nc.vector.tensor_scalar(X[:, par, i, :], psS[:, i, :], 1.0, None, ALU.mult, ALU.max,
                                        accum_out=top[:, i:i + 1]).then_inc(s["copied"], 1)

            def take_best(i):
                nc.vector.match_replace(Z[:, i, :], best[:, i, :], psS[:, i, :], -BIG).then_inc(s["replaced"], 1)

            def negate_max(h, par):
                v.wait_ge(s["copied"], START + ST * (h + 1))
                nc.vector.tensor_scalar(nmax[:, par, :], top[:], -1.0, None, ALU.mult).then_inc(s["nmaxed"], 1)

            def distance(st, h, k):
                v.wait_ge(s[f"count{k}"], START + ST * (h + 1))
                st.did(f"dist{k}", nc.vector.tensor_scalar(dist[:, k, :], cnt[:, k, :], SEQ - 2.0 * AIM + OFF[k], None, ALU.add))

            def add_round(i, count):
                tiles = slice(i, i + count)
                nc.vector.tensor_scalar(need[:, tiles], need[:, tiles], -float(WINDOW), None, ALU.add)
                for k in range(i, i + count):
                    nc.vector.max(best[:, k, :], Z[:, k, :])
                v.drain()
                nc.vector.tensor_tensor(lim[:, tiles, :], ranks[:, tiles, :], needs8[:, tiles, :], ALU.is_lt)
                v.drain()
                nc.vector.tensor_scalar(lim[:, tiles, :], lim[:, tiles, :], 2 * BIG, -BIG, ALU.mult, ALU.add)
                v.drain()
                nc.vector.tensor_tensor(best[:, tiles, :], best[:, tiles, :], lim[:, tiles, :], ALU.min)
                v.drain()
                for k in range(i, i + count):
                    nc.vector.match_replace(Z[:, k, :], best[:, k, :], Z[:, k, :], -BIG)
                v.drain()

            def rare_rows(par):
                found = v.value_load(code[0:1, 0:1], min_val=0, max_val=3 * ST * SERIOUS)
                with v.If(found > 0):
                    v.drain()
                    for i in range(ST):
                        with v.If(found % 2 ** (i + 1) > 2 ** i - 1):
                            add_round(i, 1)
                        v.end_ifs()
                    with v.If(found > SERIOUS - 1):
                        nc.vector.memset(need[:], float(KEEP + WINDOW))
                        for i in range(ST):
                            nc.vector.tensor_scalar(Z[:, i, :], X[:, par, i, :], 1.0, None, ALU.mult)
                        v.drain()
                        with v.Fori(0, -(-KEEP // WINDOW)):
                            add_round(0, ST)
                    v.end_ifs()
                v.end_ifs()

            SERIOUS = 2 ** ST
            ranks = m.rank8[:].rearrange("p (o e) -> p o e", o=1).to_broadcast((P, ST, 8))
            needs8 = need[:].rearrange("p (i o) -> p i o", o=1).to_broadcast((P, ST, 8))

            def slot(sl, par, base, prev=True, nxt=True, cur=True, old=True):
                st = Steps(v, s["small"], base)
                h, other = sl - 1, 1 - par
                if prev:
                    v.wait_ge(s["small"], base)
                    mask(h, other, 0)
                    mask(h, other, 1)
                if cur:
                    distance(st, sl, 0)
                if prev:
                    mask(h, other, 2)
                if cur:
                    st.after("dist0")
                    st.did("q0", nc.vector.tensor_tensor(sq_d[:], dist[:, 0, :], dist[:, 0, :], ALU.mult))
                    st.did("x0", nc.vector.tensor_tensor(wish[:], dist[:, 0, :], row(m.step, sl), ALU.mult))
                if prev:
                    mask(h, other, 3)
                if cur:
                    st.after("x0")
                    st.did("mv1", nc.vector.scalar_tensor_tensor(mv[:, 0, :], sq_d[:], FAR2, wish[:], ALU.is_gt, ALU.mult))
                if old:
                    v.wait_ge(s["pv"], START + sl - 2)
                    st.did("sum", nc.vector.reciprocal(rz[:], O[:, :, HD:HD + 1]))
                if prev:
                    v.wait_ge(s["masked"], START + ST * (h + 1))
                    st.did("need", nc.vector.tensor_scalar(need[:], c3[:], -1.0, float(KEEP), ALU.mult, ALU.add))
                if cur:
                    st.after("mv1")
                    nc.vector.tensor_tensor(nthr[:, 1, :], row(m.thr0, sl), mv[:, 0, :], ALU.subtract).then_inc(s["thr1"], 1)
                if old:
                    st.after("sum")
                    nc.vector.tensor_tensor(m.heads_out[:, bass.ds(sl - 3, 1), :, :].rearrange("p o i d -> p (o i) d"),
                                            O[:, :, 0:HD], rz[:].to_broadcast((P, ST, HD)), ALU.mult).then_inc(s["normed"], 1)
                if prev:
                    st.after("need")
                    st.did("below", nc.vector.tensor_tensor(lim[:], ranks, needs8, ALU.is_lt))
                    st.did("over8", nc.vector.tensor_scalar(overs[:, 0, :], need[:], float(WINDOW), None, ALU.is_gt))
                    st.did("over16", nc.vector.tensor_scalar(overs[:, 1, :], need[:], 2.0 * WINDOW, None, ALU.is_gt))
                    nc.vector.tensor_scalar(overs[:, 2, :], need[:], 0.0, None, ALU.is_lt).then_inc(s["needs"], 1)
                    st.after("below")
                    st.did("lim", nc.vector.tensor_scalar(lim[:], lim[:], 2 * BIG, -BIG, ALU.mult, ALU.add))
                    st.after("lim")
                    v.wait_ge(s["pushed"], START + ST * (h + 1))
                if cur:
                    st.did("slope_1", nc.vector.tensor_scalar(slope[:], row(m.step, sl), 1.0, None, ALU.mult))
                if prev:
                    for i in range(ST - 1):
                        nc.vector.max(best[:, i, :], psS[:, i, :])
                if cur:
                    distance(st, sl, 1)
                if prev:
                    st.did("best", nc.vector.max(best[:, ST - 1, :], psS[:, ST - 1, :]))
                if cur:
                    st.after("dist1")
                    st.did("e", nc.vector.tensor_tensor(gap[:], dist[:, 0, :], dist[:, 1, :], ALU.subtract))
                    st.did("pr", nc.vector.tensor_tensor(wish[:], dist[:, 0, :], dist[:, 1, :], ALU.mult))
                    st.did("q1", nc.vector.tensor_tensor(sq_d[:], dist[:, 1, :], dist[:, 1, :], ALU.mult))
                if prev:
                    st.after("best")
                    st.did("chosen01", nc.vector.tensor_tensor(best[:, 0:2, :], best[:, 0:2, :], lim[:, 0:2, :], ALU.min))
                    v.wait_ge(s["over"], START + h + 1)
                    with nc.allow_low_precision(reason="sums of small whole numbers"):
                        nc.vector.scalar_tensor_tensor(flags[:], over_ps, 1.0, flag_weights[:], ALU.min, ALU.mult).then_inc(s["over_read"], 1)
                    v.wait_ge(s["kept"], START + ST * h)
                    st.after("chosen01")
                    st.did("chosen23", nc.vector.tensor_tensor(best[:, 2:4, :], best[:, 2:4, :], lim[:, 2:4, :], ALU.min))
                    take_best(0)
                if cur:
                    st.after("e")
                    st.did("re", nc.vector.reciprocal(gap[:], gap[:]))
                    st.after("pr")
                    st.did("flip1", nc.vector.tensor_scalar(flip[:, 0, :], wish[:], 0.0, None, ALU.is_lt))
                if prev:
                    take_best(1)
                    st.after("chosen23")
                    v.wait_ge(s["over_read"], START + h + 1)
                    with nc.allow_low_precision(reason="a sum of small whole numbers"):
                        st.did("code", nc.vector.tensor_reduce(code[:], flags[:], AX.X, ALU.add))
                if cur:
                    st.after("re")
                    st.did("r", nc.vector.tensor_tensor(gap[:], gap[:], mv[:, 0, :], ALU.mult))
                if prev:
                    take_best(2)
                if prev:
                    st.after("code")
                if cur:
                    st.after("r")
                    st.did("dp", nc.vector.tensor_copy(partner[:], dist[:, 0, :]))
                    st.did("slope1", nc.vector.copy_predicated(slope[:], flip[:, 0, :], gap[:]))
                if prev:
                    take_best(3)
                if cur:
                    st.after("slope1")
                    st.did("x1", nc.vector.tensor_tensor(wish[:], dist[:, 1, :], slope[:], ALU.mult))
                    st.after("x1")
                    st.did("mv2", nc.vector.scalar_tensor_tensor(mv[:, 1, :], sq_d[:], FAR2, wish[:], ALU.is_gt, ALU.mult))
                    st.after("mv2")
                    nc.vector.tensor_tensor(nthr[:, 2, :], nthr[:, 1, :], mv[:, 1, :], ALU.subtract).then_inc(s["thr2"], 1)
                if prev:
                    rare_rows(other)
                    v.drain().then_inc(s["picked"], 1)
                if nxt:
                    copy_scores(sl + 1, other, 0)
                    copy_scores(sl + 1, other, 1)
                if cur:
                    v.wait_ge(s["thr2"], START + sl + 1)
                    st.did("slope_2", nc.vector.tensor_scalar(slope[:], row(m.step, sl), 1.0, None, ALU.mult))
                    st.did("back0", nc.vector.tensor_tensor(mv[:, 2, :], mv[:, 0, :], mv[:, 1, :], ALU.add))
                    distance(st, sl, 2)
                    st.after("dist2")
                    st.did("pr2", nc.vector.tensor_tensor(wish[:], dist[:, 1, :], dist[:, 2, :], ALU.mult))
                    st.did("q2", nc.vector.tensor_tensor(sq_d[:], dist[:, 2, :], dist[:, 2, :], ALU.mult))
                if nxt:
                    copy_scores(sl + 1, other, 2)
                if cur:
                    st.after("pr2")
                    st.did("flip2", nc.vector.tensor_scalar(flip[:, 1, :], wish[:], 0.0, None, ALU.is_lt))
                    st.after("flip2")
                    st.did("flips", nc.vector.tensor_tensor(flip[:, 2, :], flip[:, 0, :], flip[:, 1, :], ALU.max))
                    st.did("pt", nc.vector.copy_predicated(mv[:, 2, :], flip[:, 1, :], mv[:, 1, :]))
                    st.did("pd", nc.vector.copy_predicated(partner[:], flip[:, 1, :], dist[:, 1, :]))
                if nxt:
                    copy_scores(sl + 1, other, 3)
                if cur:
                    st.after("pd")
                    st.did("e2", nc.vector.tensor_tensor(gap[:], partner[:], dist[:, 2, :], ALU.subtract))
                    st.after("e2")
                    st.did("re2", nc.vector.reciprocal(gap[:], gap[:]))
                    st.after("re2")
                    st.did("r2", nc.vector.tensor_tensor(gap[:], gap[:], mv[:, 2, :], ALU.mult))
                    st.after("r2")
                if nxt:
                    negate_max(sl + 1, other)
                if cur:
                    st.did("slope2", nc.vector.copy_predicated(slope[:], flip[:, 2, :], gap[:]))
                    st.after("slope2")
                    st.did("x2", nc.vector.scalar_tensor_tensor(wish[:], dist[:, 2, :], 3.0, slope[:], ALU.add, ALU.mult))
                    st.after("x2")
                    st.did("mv3", nc.vector.scalar_tensor_tensor(mv[:, 2, :], sq_d[:], FAR2, wish[:], ALU.is_gt, ALU.mult))
                    st.after("mv3")
                    st.did("thr", nc.vector.tensor_tensor(thr[:], mv[:, 2, :], nthr[:, 2, :], ALU.subtract))
                return st

            v.drain()
            nc.vector.tensor_scalar(push[:], m.ident[:], -BIG, None, ALU.mult)
            nc.vector.memset(flag_weights[:, ST:3 * ST], float(SERIOUS))
            for i in range(ST):
                nc.vector.memset(flag_weights[:, i:i + 1], 2.0 ** i)
            v.drain()
            for i in range(ST):
                copy_scores(0, 0, i)
            negate_max(0, 0)
            base = slot(0, 0, START, prev=False, old=False).end()
            base = slot(1, 1, base, old=False).end()
            base = slot(2, 0, base, old=False).end()
            base = slot(3, 1, base).end()
            with v.Fori(2, BH // 2 - 1) as pair:
                even = slot(pair * 2, 0, pair * (2 * FULL_SLOT) + (base - 4 * FULL_SLOT))
                odd = slot(pair * 2 + 1, 1, pair * (2 * FULL_SLOT) + (base - 3 * FULL_SLOT))
                assert len(even.number) == len(odd.number) == FULL_SLOT
            base = base + (BH // 2 - 3) * 2 * FULL_SLOT
            base = slot(BH - 2, 0, base).end()
            base = slot(BH - 1, 1, base, nxt=False).end()
            base = slot(BH, 0, base, nxt=False, cur=False).end()
            base = slot(BH + 1, 1, base, prev=False, nxt=False, cur=False).end()
            slot(BH + 2, 0, base, prev=False, nxt=False, cur=False)


def project(nc, t, m, sems):
    w_loaded, turned, moved, made, added = (sems("pr_" + k) for k in ("w_loaded", "turned", "moved", "made", "added"))
    with ExitStack() as c:
        sb = lambda n, sh, dt=F32: c.enter_context(nc.sbuf_tensor(n, sh, dt))
        w = sb("w_out", [P, DC, D])
        bias = sb("b_out", [P, D])
        aT = sb("attnT", [P, 2, DC, P])
        flat = sb("attn_rows", [P, 2, D])
        psA = c.enter_context(nc.psum_tensor("psA_pr", [P, 2, 512], F32))
        psP = c.enter_context(nc.psum_tensor("psP_pr", [P, 2, 512], F32))
        rows, gathered = flat, sems("pr_rows")
        block = c.enter_context(nc.Block())

        @block.sync
        def _(sp):
            sp.dma_start(w[:], t["W_outT"].rearrange("(c p) e -> p c e", p=P)).then_inc(w_loaded, 16)
            sp.dma_start(bias[:], t["b_out"].to_broadcast((P, D))).then_inc(w_loaded, 16)

        @block.gpsimd
        def _(pool):
            for n in range(TILES):
                b, i = n // SEQ_TILES, n % SEQ_TILES
                if n >= 2:
                    pool.wait_ge(turned, n - 1)
                nc.gpsimd.tensor_copy(rows[:, n % 2, :].rearrange("p (h d) -> p h d", h=HEADS),
                                      m.heads_out[:, b * HEADS:(b + 1) * HEADS, i, :]).then_inc(gathered, 1)

        @block.tensor
        def _(pe):
            pe.wait_ge(w_loaded, 32)
            for n in range(TILES):
                pe.wait_ge(gathered, n + 1)
                if n >= 2:
                    pe.wait_ge(moved, n - 1)
                    pe.wait_ge(added, n - 1)
                for ch in range(DC):
                    tr = nc.tensor.transpose(psA[:, n % 2, ch * P:(ch + 1) * P], rows[:, n % 2, ch * P:(ch + 1) * P], m.ident[:])
                tr.then_inc(turned, 1)
                pe.wait_ge(moved, n + 1)
                for ch in range(DC):
                    mm = nc.tensor.matmul(psP[:, n % 2, 0:D], aT[:, n % 2, ch, :], w[:, ch, :], start=(ch == 0), stop=(ch == DC - 1))
                mm.then_inc(made, 1)

        @block.scalar
        def _(act):
            for n in range(TILES):
                act.wait_ge(turned, n + 1)
                if n >= 2:
                    act.wait_ge(made, n - 1)
                nc.scalar.copy(aT[:, n % 2, :, :], psA[:, n % 2, 0:D].rearrange("p (c n) -> p c n", c=DC)).then_inc(moved, 1)

        @block.vector
        def _(v):
            v.wait_ge(w_loaded, 32)
            nc.vector.tensor_tensor(m.resid[:], m.resid[:], bias[:].rearrange("p (o d) -> p o d", o=1).to_broadcast((P, TILES, D)), ALU.add)
            v.drain()
            for n in range(TILES):
                v.wait_ge(made, n + 1)
                nc.vector.tensor_tensor(m.resid[:, n, :], psP[:, n % 2, 0:D], m.resid[:, n, :], ALU.add).then_inc(added, 1)


def top_k_mask(nc, v, act_exp, logits, bias, n, top, work):
    p = work.probs[:, :, 0:n]
    one = lambda ap: ap.rearrange("p (t o) -> p t o", o=1).to_broadcast((P, TILES, n))
    nc.vector.tensor_tensor(p, logits, bias.rearrange("p (o e) -> p o e", o=1).to_broadcast((P, TILES, n)), ALU.add)
    nc.vector.memset(work.probs[:, :, n:n + 8], -2.0)
    v.drain()
    nc.vector.tensor_reduce(work.row[:], p, AX.X, ALU.max)
    v.drain()
    nc.vector.tensor_tensor(p, p, one(work.row[:]), ALU.subtract)
    act_exp()
    nc.vector.tensor_reduce(work.row[:], p, AX.X, ALU.add)
    v.drain()
    nc.vector.reciprocal(work.row[:], work.row[:])
    v.drain()
    nc.vector.tensor_tensor(p, p, one(work.row[:]), ALU.mult)
    v.drain()
    for i in range(TILES):
        nc.vector.max(work.best[:, i, :], work.probs[:, i, 0:n])
    v.drain()
    nc.vector.memset(work.best[:, :, top:8], -2.0)
    v.drain()
    for i in range(TILES):
        nc.vector.match_replace(work.found[:, i, :], work.best[:, i, :], work.probs[:, i, :], -1.0)
    v.drain()


class RouteWork:

    def __init__(self, sb, tag, n):
        self.probs = sb("probs" + tag, [P, TILES, n + 8])
        self.found = sb("found" + tag, [P, TILES, n + 8])
        self.best = sb("best" + tag, [P, TILES, 8])
        self.row = sb("row" + tag, [P, TILES])


def moe(nc, t, m, sems):
    s = m.sem["moe"]
    ALL = EXPERTS + 1
    HC = EH // P
    CH = BATCH
    with ExitStack() as c:
        sb = lambda n, sh, dt=F32: c.enter_context(nc.sbuf_tensor(n, sh, dt))
        w1 = sb("w1", [P, 2, DC, EH])
        w2 = sb("w2", [P, 2, HC, D])
        b1 = sb("b1", [P, ALL * HC])
        b1_now = sb("b1_now", [P, HC])
        rw = sb("router_w", [P, DC, EXPERTS])
        rb = sb("router_b", [P, EXPERTS])
        b2s = sb("b2_shared", [P, D])
        b2r = sb("b2_routed", [EXPERTS, D])
        work = RouteWork(sb, "_moe", EXPERTS)
        wt = sb("expert_weights", [P, TILES, ALL])
        wT = sb("weightsT", [EXPERTS, 2, P])
        H = sb("hidden", [P, 2, HC, SEQ])
        psH = c.enter_context(nc.psum_tensor("psH_moe", [P, HC, 512], F32))
        psY = c.enter_context(nc.psum_tensor("psY_moe", [P, 4, 512], F32))

        with nc.Block() as block:
            @block.sync
            def _(sp):
                for dst, src in ((rw[:], t["router_w"].rearrange("(c p) e -> p c e", p=P)), (rb[:], t["router_b"].to_broadcast((P, EXPERTS))),
                                 (b2s[:], t["sb2"].to_broadcast((P, D))), (b2r[:], t["rb2"]), (b1[:], t["b1_all"])):
                    sp.dma_start(dst, src).then_inc(s["small"], 16)

            @block.tensor
            def _(pe):
                pe.wait_ge(s["small"], START + 16 * 5)
                for i in range(TILES):
                    for ch in range(DC):
                        mm = nc.tensor.matmul(psH[:, 0, i * EXPERTS:(i + 1) * EXPERTS], m.xT[:, ch, i * P:(i + 1) * P], rw[:, ch, :],
                                              start=(ch == 0), stop=(ch == DC - 1), skip_group_check=True)
                mm.then_inc(s["logits"], 1)
                pe.wait_ge(s["weights"], START + 1)
                for i in range(TILES):
                    if i >= 2:
                        pe.wait_ge(s["wT_kept"], START + i - 1)
                    nc.tensor.transpose(psY[0:EXPERTS, i % 2, 0:P], wt[:, i, 1:ALL], m.ident[:]).then_inc(s["wT_made"], 1)
                    pe.wait_ge(s["wT_kept"], START + i + 1)
                    if i >= 2:
                        pe.wait_ge(s["bias_added"], START + i - 1)
                    nc.tensor.matmul(psY[:, 2 + i % 2, 0:D], wT[:, i % 2, :], b2r[:], start=True, stop=True).then_inc(s["bias_made"], 1)

            @block.scalar
            def _(act):
                act.wait_ge(s["shifted"], START + 1)
                nc.scalar.activation(work.probs[:, :, 0:EXPERTS], work.probs[:, :, 0:EXPERTS], ACT.Exp).then_inc(s["exped"], 1)
                for i in range(TILES):
                    act.wait_ge(s["wT_made"], START + i + 1)
                    if i >= 2:
                        act.wait_ge(s["bias_made"], START + i - 1)
                    nc.scalar.copy(wT[:, i % 2, :], psY[0:EXPERTS, i % 2, 0:P]).then_inc(s["wT_kept"], 1)

            @block.vector
            def _(v):
                def exp_on_scalar():
                    v.drain().then_inc(s["shifted"], 1)
                    v.wait_ge(s["exped"], START + 1)
                v.wait_ge(s["logits"], START + 1)
                top_k_mask(nc, v, exp_on_scalar, psH[:, 0, 0:TILES * EXPERTS].rearrange("p (t e) -> p t e", e=EXPERTS), rb[:], EXPERTS, TOP_E, work)
                nc.vector.memset(wt[:, :, 0:1], 1.0)
                nc.vector.scalar_tensor_tensor(wt[:, :, 1:ALL], work.found[:, :, 0:EXPERTS], -0.5, work.probs[:, :, 0:EXPERTS], ALU.is_lt, ALU.mult)
                v.drain().then_inc(s["weights"], 1)
                nc.vector.tensor_tensor(m.resid[:], m.resid[:], b2s[:].rearrange("p (o d) -> p o d", o=1).to_broadcast((P, TILES, D)), ALU.add)
                v.drain()
                for i in range(TILES):
                    v.wait_ge(s["bias_made"], START + i + 1)
                    nc.vector.tensor_tensor(m.resid[:, i, :], psY[:, 2 + i % 2, 0:D], m.resid[:, i, :], ALU.add).then_inc(s["bias_added"], 1)

        with nc.Block() as block:
            @block.sync
            def _(sp):
                def load(e, r):
                    sp.dma_start(w1[:, r, :, :], t["w1_all"][bass.ds(e, 1)].rearrange("o (c p) n -> p (o c) n", p=P)).then_inc(s[f"w_loaded{r}"], 16)
                    sp.dma_start(w2[:, r, :, :], t["w2_all"][bass.ds(e, 1)].rearrange("o (c p) n -> p (o c) n", p=P)).then_inc(s[f"w_loaded{r}"], 16)
                load(0, 0)
                load(1, 1)
                with sp.Fori(1, ALL // 2) as pair:
                    e = pair * 2
                    for r in range(2):
                        sp.wait_ge(s["made"], START + SEQ_TILES * CH * (e + (r - 1)))
                        load(e + r, r)
                sp.wait_ge(s["made"], START + SEQ_TILES * CH * (ALL - 2))
                load(ALL - 1, 0)

            @block.tensor
            def _(pe):
                def hidden(e, r, n):
                    g = e * CH + n
                    for hc in range(HC):
                        pe.wait_ge(s["active"], START + HC * g + (hc + 1))
                        for ch in range(DC):
                            mm = nc.tensor.matmul(psH[:, hc, :], w1[:, r, ch, hc * P:(hc + 1) * P], m.xT[:, ch, n * SEQ:(n + 1) * SEQ],
                                                  start=(ch == 0), stop=(ch == DC - 1))
                        mm.then_inc(s["hidden"], 1)

                def output(e, r, n):
                    g = e * CH + n
                    pe.wait_ge(s["active"], START + HC * (g + 2))
                    for i in range(SEQ_TILES):
                        pe.wait_ge(s["y_free"], START + SEQ_TILES * g + (i // 2 * 2 + 2))
                        for hc in range(HC):
                            mm = nc.tensor.matmul(psY[:, 2 * (n % 2) + i // 2, (i % 2) * D:(i % 2 + 1) * D],
                                                  H[:, n % 2, hc, i * P:(i + 1) * P], w2[:, r, hc, :],
                                                  start=(hc == 0), stop=(hc == HC - 1), skip_group_check=True)
                        mm.then_inc(s["made"], 1)

                def expert(e, r, last=False):
                    for n in range(CH):
                        if n < CH - 1:
                            hidden(e, r, n + 1)
                        elif not last:
                            pe.wait_ge(s[f"w_loaded{1 - r}"], START + e * 16 + (48 if r else 32))
                            hidden(e + 1, 1 - r, 0)
                        output(e, r, n)

                pe.wait_ge(s["w_loaded0"], START + 32)
                hidden(0, 0, 0)
                with pe.Fori(0, ALL // 2) as pair:
                    e = pair * 2
                    expert(e, 0)
                    expert(e + 1, 1)
                expert(ALL - 1, 0, last=True)

            @block.scalar
            def _(act):
                act.drain().then_inc(s["active"], HC)
                with act.Fori(0, ALL) as e:
                    act.drain()
                    nc.scalar.copy(b1_now[:], b1[:, bass.ds(e * HC, HC)])
                    act.drain()
                    for n in range(CH):
                        g = e * CH + n
                        act.wait_ge(s["h_unused"], START + g + 1)
                        for hc in range(HC):
                            act.wait_ge(s["hidden"], START + HC * g + (hc + 1))
                            nc.scalar.activation(H[:, n % 2, hc, :], psH[:, hc, :], ACT.Gelu, bias=b1_now[:, hc:hc + 1]).then_inc(s["active"], 1)

            @block.vector
            def _(v):
                v.drain().then_inc(s["y_free"], 2 * SEQ_TILES)
                v.drain().then_inc(s["h_unused"], 2)
                with v.Fori(0, ALL) as e:
                    for n in range(CH):
                        g = e * CH + n
                        for i in range(SEQ_TILES):
                            v.wait_ge(s["made"], START + SEQ_TILES * g + (i // 2 * 2 + 2))
                            T = n * SEQ_TILES + i
                            v.wait_ge(s["y_free"], START + SEQ_TILES * g)
                            weight = wt[:, T, bass.ds(e, 1)]
                            nc.vector.scalar_tensor_tensor(m.resid[:, T, :], psY[:, 2 * (n % 2) + i // 2, (i % 2) * D:(i % 2 + 1) * D],
                                                           weight, m.resid[:, T, :], ALU.mult, ALU.add).then_inc(s["y_free"], 1)
                        v.drain().then_inc(s["h_unused"], 1)


def cos_attention(nc, t, m, sems):
    s = m.sem["cos"]
    NAMES = "qkvo"
    with ExitStack() as c:
        sb = lambda n, sh, dt=F32: c.enter_context(nc.sbuf_tensor(n, sh, dt))
        W = sb("W_phm", [P, 4, DC, D])
        bias = sb("phm_bias", [1, 4, D])
        gains = sb("ln_gains", [P, 4, D])
        rows = sb("query", [P, TILES, D])
        qnT = sb("qnT", [P, DC, TOKENS])

        with ExitStack() as c2:
            A = c2.enter_context(nc.sbuf_tensor("phm_A", [P, 4, PHM, DC, PHM], F32))
            S = c2.enter_context(nc.sbuf_tensor("phm_S", [P, 4, PHM, D // PHM], F32))
            prod = c2.enter_context(nc.sbuf_tensor("phm_prod", [P, 4, DC * D], F32))
            block = c2.enter_context(nc.Block())

            @block.sync
            def _(sp):
                for x, name in enumerate(NAMES):
                    for half in range(2):
                        sp.dma_start(A[half * 64:(half + 1) * 64, x, :, :, :],
                                     t["A_" + name][half:half + 1].to_broadcast((64, PHM * DC * PHM)).rearrange("p (n c j) -> p n c j", n=PHM, c=DC)).then_inc(s["loaded"], 16)
                        sp.dma_start(S[half * 64:(half + 1) * 64, x, :, :], t["S_" + name].rearrange("n k l -> k n l")).then_inc(s["loaded"], 16)
                    sp.dma_start(bias[:, x, :], t["bias_" + name]).then_inc(s["loaded"], 16)
                for x, name in enumerate(("g1", "b1", "g2", "b2")):
                    sp.dma_start(gains[:, x, :], t[name].to_broadcast((P, D))).then_inc(s["loaded"], 16)
                sp.wait_ge(s["loaded"], START + 16 * (4 * 5 + 4))

            @block.vector
            def _(v):
                v.wait_ge(s["loaded"], START + 16 * (4 * 5 + 4))
                L = D // PHM
                for n in range(PHM):
                    for x in range(4):
                        dst = W[:, x, :, :] if n == 0 else prod[:, x, :]
                        dst = dst.rearrange("p c (j l) -> p (c j) l", l=L) if n == 0 else dst.rearrange("p (a l) -> p a l", l=L)
                        nc.vector.tensor_tensor(dst, S[:, x, n:n + 1, :].to_broadcast((P, DC * PHM, L)),
                                                A[:, x, n, :, :].rearrange("p c (j o) -> p (c j) o", o=1).to_broadcast((P, DC * PHM, L)), ALU.mult)
                    v.drain()
                    if n:
                        for x in range(4):
                            nc.vector.tensor_tensor(W[:, x, :, :], W[:, x, :, :], prod[:, x, :].rearrange("p (c e) -> p c e", c=DC), ALU.add)
                        v.drain()

        norm_turn(nc, m, sems, "_query", m.resid, rows, m.xT)
        norm_turn(nc, m, sems, "_qn", rows, rows, qnT, gains[:, 0, :], gains[:, 1, :])

        with ExitStack() as c2:
            sb2 = lambda n, sh, dt=F32: c2.enter_context(nc.sbuf_tensor(n, sh, dt))
            Q, K, V = (sb2(n, [P, BATCH, D]) for n in ("cos_q", "cos_k", "cos_v"))
            prod = sb2("cos_prod", [P, BATCH, D])
            mix = sb2("cos_mix", [P, 2, BATCH, D])
            cosines = sb2("cosines", [P, BATCH, BATCH])
            a = sb2("cos_a", [P, 2, BATCH * HEADS])
            den = sb2("cos_den", [P, HEADS])
            att = sb2("cos_att", [P, D])
            psP = c2.enter_context(nc.psum_tensor("psP_cos", [P, 6, 512], F32))
            block = c2.enter_context(nc.Block())

            @block.sync
            def _(sp):
                sp.dma_start(cosines[:].rearrange("p a b -> p (a b)"), t["cosines"].to_broadcast((P, BATCH * BATCH))).then_inc(s["norm"], 16)

            @block.tensor
            def _(pe):
                for it in range(SEQ_TILES):
                    for l in range(BATCH):
                        par = l % 2
                        if l < 2:
                            pe.wait_ge(s["kept"], START + 3 * (it * BATCH))
                        else:
                            pe.wait_ge(s["kept"], START + 3 * (it * BATCH + (l - 1)))
                        for x in range(3):
                            src = qnT if x == 0 else m.xT
                            out = psP[:, 3 * par + x, 0:D]
                            for ch in range(DC):
                                nc.tensor.matmul(out, src[:, ch, bass.ds(l * SEQ + it * P, P)], W[:, x, ch, :], start=(ch == 0), stop=False)
                            mm = nc.tensor.matmul(out, m.ones[0:1, :], bias[:, x, :], start=False, stop=True)
                        mm.then_inc(s["made"], 1)

            @block.scalar
            def _(act):
                with act.Fori(0, SEQ_TILES) as it:
                    act.wait_ge(s["summed"], START + it * BATCH)
                    for l in range(BATCH):
                        act.wait_ge(s["made"], START + it * BATCH + (l + 1))
                        for x, (dst, f) in enumerate(((Q, ACT.Relu), (K, ACT.Relu), (V, ACT.Copy))):
                            nc.scalar.activation(dst[:, l, :], psP[:, 3 * (l % 2) + x, 0:D], f).then_inc(s["kept"], 1)

            @block.gpsimd
            def _(pool):
                with pool.Fori(0, SEQ_TILES) as it:
                    for l in range(BATCH):
                        pool.wait_ge(s["scored"], START + it * BATCH + (l + 1))
                        if l >= 2:
                            pool.wait_ge(s["summed"], START + it * BATCH + (l - 1))
                        nc.gpsimd.tensor_tensor(mix[:, l % 2, :, :].rearrange("p l (h d) -> p (l h) d", d=HD),
                                                V[:].rearrange("p l (h d) -> p (l h) d", d=HD),
                                                a[:, l % 2, :].rearrange("p (x o) -> p x o", o=1).to_broadcast((P, BATCH * HEADS, HD)),
                                                ALU.mult).then_inc(s["mixed"], 1)

            @block.vector
            def _(v):
                v.wait_ge(s["norm"], START + 16)

                def score(it, l):
                    al = a[:, l % 2, :]
                    nc.vector.tensor_tensor(prod[:], Q[:, l:l + 1, :].to_broadcast((P, BATCH, D)), K[:], ALU.mult)
                    v.drain()
                    nc.vector.tensor_reduce(al, prod[:].rearrange("p l (h d) -> p (l h) d", d=HD), AX.X, ALU.add)
                    v.drain()
                    al3 = al.rearrange("p (l h) -> p l h", h=HEADS)
                    nc.vector.tensor_tensor(al3, al3, cosines[:, l, :].rearrange("p (l o) -> p l o", o=1).to_broadcast((P, BATCH, HEADS)), ALU.mult)
                    v.drain()
                    nc.vector.tensor_reduce(den[:], al.rearrange("p (l h) -> p h l", h=HEADS), AX.X, ALU.add)
                    v.drain()
                    nc.vector.tensor_scalar(den[:], den[:], 1e-6, None, ALU.max)
                    v.drain()
                    nc.vector.reciprocal(den[:], den[:])
                    v.drain()
                    nc.vector.tensor_tensor(al3, al3, den[:].rearrange("p (o h) -> p o h", o=1).to_broadcast((P, BATCH, HEADS)), ALU.mult)
                    v.drain().then_inc(s["scored"], 1)

                def collect(it, l):
                    v.wait_ge(s["mixed"], START + it * BATCH + (l + 1))
                    nc.vector.tensor_reduce(att[:], mix[:, l % 2, :, :].rearrange("p l e -> p e l"), AX.X, ALU.add)
                    v.drain()
                    row = rows[:, bass.ds(l * SEQ_TILES + it, 1), :].rearrange("p o d -> p (o d)")
                    nc.vector.tensor_tensor(row, row, att[:], ALU.add)
                    v.drain().then_inc(s["summed"], 1)

                with v.Fori(0, SEQ_TILES) as it:
                    v.wait_ge(s["kept"], START + 3 * BATCH * (it + 1))
                    for l in range(BATCH):
                        score(it, l)
                        if l:
                            collect(it, l - 1)
                    collect(it, BATCH - 1)

        norm_turn(nc, m, sems, "_out", rows, rows, qnT, gains[:, 2, :], gains[:, 3, :])

        with ExitStack() as c2:
            psO = c2.enter_context(nc.psum_tensor("psO_cos", [P, 4, 512], F32))
            block = c2.enter_context(nc.Block())

            @block.gpsimd
            def _(pool):
                nc.gpsimd.tensor_tensor(m.resid[:], m.resid[:], rows[:], ALU.add).then_inc(s["norm"], 1)

            @block.tensor
            def _(pe):
                for i in range(TILES):
                    if i >= 4:
                        pe.wait_ge(s["oadded"], START + i - 3)
                    for ch in range(DC):
                        nc.tensor.matmul(psO[:, i % 4, 0:D], qnT[:, ch, i * P:(i + 1) * P], W[:, 3, ch, :], start=(ch == 0), stop=False)
                    nc.tensor.matmul(psO[:, i % 4, 0:D], m.ones[0:1, :], bias[:, 3, :], start=False, stop=True).then_inc(s["omade"], 1)

            @block.vector
            def _(v):
                v.wait_ge(s["norm"], START + 16 + 1)
                for i in range(TILES):
                    v.wait_ge(s["omade"], START + i + 1)
                    nc.vector.tensor_tensor(m.resid[:, i, :], psO[:, i % 4, 0:D], m.resid[:, i, :], ALU.add).then_inc(s["oadded"], 1)


def block_ffn(nc, t, m, sems, out):
    s = m.sem["ffn"]
    MC = OUTF // P
    with ExitStack() as c:
        sb = lambda n, sh, dt=F32: c.enter_context(nc.sbuf_tensor(n, sh, dt))
        w1 = sb("ffn_w1", [P, DC, OUTF])
        w2 = sb("ffn_w2", [P, MC, D])
        b1 = sb("ffn_b1", [P, MC])
        b2 = sb("ffn_b2", [1, D])
        rw = sb("ffn_rw", [P, DC, BLOCKS])
        rb = sb("ffn_rb", [P, BLOCKS])
        spread = sb("ffn_spread", [BLOCKS, MC, P], BF16)
        spread32 = sb("ffn_spread32", [BLOCKS, MC * P])
        maskT = sb("maskT", [BLOCKS, TOKENS], BF16)
        work = RouteWork(sb, "_ffn", BLOCKS)
        chosen = sb("chosen", [P, TILES, BLOCKS])
        H = sb("ffn_hidden", [P, 2, MC, SEQ])
        psH = c.enter_context(nc.psum_tensor("psH_ffn", [P, 2, 512], F32))
        psM = c.enter_context(nc.psum_tensor("psM_ffn", [P, 2, 512], F32))
        psY = c.enter_context(nc.psum_tensor("psY_ffn", [P, 4, 512], F32))
        out_tiles = out.rearrange("(n p) d -> p n d", p=P)

        with nc.Block() as block:
            @block.sync
            def _(sp):
                for dst, src in ((rw[:], t["ffn_rwT"].rearrange("(c p) e -> p c e", p=P)), (rb[:], t["ffn_rb"].to_broadcast((P, BLOCKS))),
                                 (b1[:], t["ffn_b1"]), (b2[:], t["ffn_b2"]), (spread32[:], t["spread"])):
                    sp.dma_start(dst, src).then_inc(s["small"], 16)
                sp.dma_start(w1[:], t["ffn_w1T"].rearrange("(c p) e -> p c e", p=P)).then_inc(s["w_loaded"], 16)
                sp.dma_start(w2[:], t["ffn_w2T"].rearrange("(c p) e -> p c e", p=P)).then_inc(s["w_loaded"], 16)

            @block.tensor
            def _(pe):
                pe.wait_ge(s["small"], START + 16 * 5)
                for i in range(TILES):
                    for ch in range(DC):
                        mm = nc.tensor.matmul(psH[:, 0, i * BLOCKS:(i + 1) * BLOCKS], m.xT[:, ch, i * P:(i + 1) * P], rw[:, ch, :],
                                              start=(ch == 0), stop=(ch == DC - 1), skip_group_check=True)
                mm.then_inc(s["logits"], 1)
                pe.wait_ge(s["mask"], START + 1)
                for g in range(BATCH):
                    if g >= 2:
                        pe.wait_ge(s["mT_kept"], START + g - 1)
                    for j in range(SEQ_TILES):
                        tr = nc.tensor.transpose(psM[0:BLOCKS, g % 2, j * P:(j + 1) * P], chosen[:, SEQ_TILES * g + j, :], m.ident[:])
                    tr.then_inc(s["mT_made"], 1)

            @block.scalar
            def _(act):
                act.wait_ge(s["shifted"], START + 1)
                nc.scalar.activation(work.probs[:, :, 0:BLOCKS], work.probs[:, :, 0:BLOCKS], ACT.Exp).then_inc(s["exped"], 1)
                for g in range(BATCH):
                    act.wait_ge(s["mT_made"], START + g + 1)
                    nc.scalar.copy(maskT[:, g * SEQ:(g + 1) * SEQ], psM[0:BLOCKS, g % 2, :]).then_inc(s["mT_kept"], 1)

            @block.vector
            def _(v):
                def exp_on_scalar():
                    v.drain().then_inc(s["shifted"], 1)
                    v.wait_ge(s["exped"], START + 1)
                v.wait_ge(s["small"], START + 16 * 5)
                nc.vector.tensor_copy(spread[:].rearrange("b m p -> b (m p)"), spread32[:])
                v.wait_ge(s["logits"], START + 1)
                top_k_mask(nc, v, exp_on_scalar, psH[:, 0, :].rearrange("p (t e) -> p t e", e=BLOCKS), rb[:], BLOCKS, TOP_B, work)
                nc.vector.tensor_scalar(chosen[:], work.found[:, :, 0:BLOCKS], -0.5, None, ALU.is_lt)
                v.drain().then_inc(s["mask"], 1)

        with nc.Block() as block:
            @block.tensor
            def _(pe):
                def hidden(n):
                    for mc in range(MC):
                        k = n * MC + mc
                        if not (isinstance(n, int) and n == 0 and mc < 2):
                            pe.wait_ge(s["masked"], START + k - 1)
                        for ch in range(DC):
                            mm = nc.tensor.matmul(psH[:, mc % 2, :], w1[:, ch, mc * P:(mc + 1) * P], m.xT[:, ch, bass.ds(n * SEQ, SEQ)],
                                                  start=(ch == 0), stop=(ch == DC - 1))
                        mm.then_inc(s["hidden"], 1)
                        nc.tensor.matmul(psM[:, mc % 2, :], spread[:, mc, :], maskT[:, bass.ds(n * SEQ, SEQ)], start=True, stop=True).then_inc(s["spread"], 1)

                def output(n, par):
                    pe.wait_ge(s["masked"], START + (n + 1) * MC)
                    for i in range(SEQ_TILES):
                        if not (isinstance(n, int) and n == 0):
                            pe.wait_ge(s["added"], START + SEQ_TILES * (n - 1) + (i + 1))
                        for mc in range(MC):
                            nc.tensor.matmul(psY[:, i, 0:D], H[:, par, mc, i * P:(i + 1) * P], w2[:, mc, :], start=(mc == 0), stop=False)
                        nc.tensor.matmul(psY[:, i, 0:D], m.ones[0:1, :], b2[:], start=False, stop=True).then_inc(s["made"], 1)

                pe.wait_ge(s["w_loaded"], START + 32)
                hidden(0)
                hidden(1)
                output(0, 0)
                with pe.Fori(0, BATCH // 2 - 1) as pair:
                    n = pair * 2 + 1
                    hidden(n + 1)
                    output(n, 1)
                    hidden(n + 2)
                    output(n + 1, 0)
                output(BATCH - 1, 1)

            @block.scalar
            def _(act):
                with act.Fori(0, BATCH // 2) as pair:
                    n0 = pair * 2
                    for k in range(2):
                        n = n0 + k
                        for mc in range(MC):
                            act.wait_ge(s["hidden"], START + n * MC + (mc + 1))
                            if mc == 0:
                                act.wait_ge(s["h_unused"], START + n + 1)
                            nc.scalar.activation(H[:, k, mc, :], psH[:, mc % 2, :], ACT.Relu, bias=b1[:, mc:mc + 1]).then_inc(s["relu"], 1)

            @block.vector
            def _(v):
                def mask_hidden(n, k):
                    for mc in range(MC):
                        v.wait_ge(s["relu"], START + n * MC + (mc + 1))
                        v.wait_ge(s["spread"], START + n * MC + (mc + 1))
                        nc.vector.tensor_tensor(H[:, k, mc, :], psM[:, mc % 2, :], H[:, k, mc, :], ALU.mult).then_inc(s["masked"], 1)

                def add_output(n):
                    for i in range(SEQ_TILES):
                        v.wait_ge(s["made"], START + SEQ_TILES * n + (i + 1))
                        row = m.resid[:, bass.ds(n * SEQ_TILES + i, 1), :].rearrange("p o d -> p (o d)")
                        nc.vector.tensor_tensor(row, psY[:, i, 0:D], row, ALU.add).then_inc(s["added"], 1)
                    v.drain().then_inc(s["h_unused"], 1)

                v.drain().then_inc(s["h_unused"], 2)
                mask_hidden(0, 0)
                with v.Fori(0, BATCH // 2 - 1) as pair:
                    n = pair * 2
                    mask_hidden(n + 1, 1)
                    add_output(n)
                    mask_hidden(n + 2, 0)
                    add_output(n + 1)
                mask_hidden(BATCH - 1, 1)
                add_output(BATCH - 2)
                add_output(BATCH - 1)

            @block.sync
            def _(sp):
                with sp.Fori(0, BATCH) as n:
                    sp.wait_ge(s["added"], START + SEQ_TILES * (n + 1))
                    sp.dma_start(out_tiles[:, bass.ds(n * SEQ_TILES, SEQ_TILES), :], m.resid[:, bass.ds(n * SEQ_TILES, SEQ_TILES), :]).then_inc(s["stored"], 16)
                sp.wait_ge(s["stored"], START + 16 * BATCH)


class Memory:
    pass


def lm_tower(nc, t, out, stop=None):
    m = Memory()
    m.parts_dram = [nc.dram_tensor(n, (BATCH, 3, D, SEQ), BF16, kind="Internal").ap() for n in ("q_parts", "k_parts")]
    out = out.rearrange("b s d -> (b s) d")

    def dump(sems):
        with nc.Block() as block:
            @block.sync
            def _(sp):
                d = sems("dumped")
                sp.dma_start(out.rearrange("(n p) d -> p n d", p=P), m.resid[:]).then_inc(d, 16)
                sp.wait_ge(d, 16)

    with ExitStack() as c:
        sems = lambda n: c.enter_context(nc.semaphore(n))
        sb = lambda st, n, sh, dt=F32: st.enter_context(nc.sbuf_tensor(n, sh, dt))
        m.sem = {stage: {n: sems(f"{stage}_{n}") for n in names} for stage, names in STAGE_SEMAPHORES.items()}
        m.ident = sb(c, "ident", [P, P])
        m.ids = sb(c, "ids", [P, TILES], I32)
        m.s_col = sb(c, "s_col", [RANK, 1])
        m.vt = sb(c, "vt", [RANK, D])
        m.qk_bias = sb(c, "qk_bias", [P, 2 * DC])
        m.half_mask = sb(c, "half_mask", [P, HALF])
        m.rank8 = sb(c, "rank8", [P, 8])
        m.eps = sb(c, "eps", [P, 1])
        m.ones = sb(c, "ones", [P, P])
        m.resid = sb(c, "resid", [P, TILES, D])
        load_constants(nc, t, m, sems)
        embed(nc, t, m, sems)
        if stop == "embed":
            return dump(sems)
        with ExitStack() as c0:
            m.v_aug = sb(c0, "v_aug", [P, BH, SEQ_TILES, HD + 1])
            m.thr0 = sb(c0, "thr0", [P, BH, SEQ_TILES])
            m.step = sb(c0, "step", [P, BH, SEQ_TILES])
            with ExitStack() as c1:
                m.xT = sb(c1, "xT", [P, DC, TOKENS])
                norm_turn(nc, m, sems, "_0", m.resid, None, m.xT)
                qkv(nc, t, m, sems)
            m.heads_out = sb(c0, "heads_out", [P, BH, SEQ_TILES, HD])
            attend(nc, t, m, sems)
            project(nc, t, m, sems)
        if stop == "attn":
            return dump(sems)
        m.xT = sb(c, "xT1", [P, DC, TOKENS])
        norm_turn(nc, m, sems, "_1", m.resid, None, m.xT)
        moe(nc, t, m, sems)
        if stop == "moe":
            return dump(sems)
        cos_attention(nc, t, m, sems)
        if stop == "cos":
            return dump(sems)
        norm_turn(nc, m, sems, "_2", m.resid, None, m.xT)
        block_ffn(nc, t, m, sems, out)


def layouts(i):
    r = {}
    a = {k: np.asarray(v) for k, v in i.items()}
    r["ids"] = a["x"].reshape(TILES, P).T
    r["U"], r["s_col"], r["Vt"] = a["L0_tok_U"], a["L0_tok_s"].reshape(RANK, 1), a["L0_tok_Vt"]
    r["W_qkvT"] = a["L0_attn_W_qkv"].T
    r["qk_bias"] = a["L0_attn_b_qkv"][:2 * D].reshape(2 * DC, P).T
    r["v_bias"] = a["L0_attn_b_qkv"][2 * D:].reshape(1, D)
    r["W_outT"], r["b_out"] = a["L0_attn_W_out"].T, a["L0_attn_b_out"].reshape(1, D)
    r["router_w"], r["router_b"] = a["L0_ffn_router_w"], a["L0_ffn_router_b"].reshape(1, EXPERTS)
    r["w1_all"] = np.concatenate([a["L0_ffn_sw1"][None], a["L0_ffn_rw1"]])
    r["w2_all"] = np.concatenate([a["L0_ffn_sw2"][None], a["L0_ffn_rw2"]])
    r["b1_all"] = np.concatenate([a["L0_ffn_sb1"][None], a["L0_ffn_rb1"]]).reshape(-1, P).T
    r["sb2"], r["rb2"] = a["L0_ffn_sb2"].reshape(1, D), a["L0_ffn_rb2"]
    for x in "qkvo":
        r["A_" + x] = a[f"L1_attn_{x}A"].reshape(PHM, DC, 2, PHM).transpose(2, 0, 1, 3).reshape(2, -1)
        r["S_" + x], r["bias_" + x] = a[f"L1_attn_{x}S"], a[f"L1_attn_{x}b"].reshape(1, D)
    for x in ("g1", "b1", "g2", "b2"):
        r[x] = a["L1_attn_" + x].reshape(1, D)
    r["ffn_rwT"], r["ffn_rb"] = a["L1_ffn_router_w"].T, a["L1_ffn_router_b"].reshape(1, BLOCKS)
    r["ffn_w1T"], r["ffn_w2T"] = a["L1_ffn_w1"].T, a["L1_ffn_w2"].T
    r["ffn_b1"], r["ffn_b2"] = a["L1_ffn_b1"].reshape(-1, P).T, a["L1_ffn_b2"].reshape(1, D)
    r["ident"] = np.eye(P, dtype=np.float32)
    r["half_mask"] = np.repeat(np.eye(HALF, dtype=np.float32), HD, axis=0)
    r["rank8"] = np.arange(8, dtype=np.float32).reshape(1, 8)
    angle = (np.pi / 2) * np.arange(1, BATCH + 1) / BATCH
    r["cosines"] = np.cos(angle[:, None] - angle[None, :]).astype(np.float32).reshape(1, -1)
    r["spread"] = np.repeat(np.eye(BLOCKS, dtype=np.float32), BLOCK, axis=1)
    return {k: np.ascontiguousarray(v) for k, v in r.items()}


def kernel(**inputs):
    import concourse.bacc as bacc
    from concourse.bass_utils import run_bass_kernel_spmd

    nc = bacc.Bacc("TRN2", target_bir_lowering=False, num_devices=1)
    arrays = {f"in_{k}": v for k, v in layouts(inputs).items()}
    t = {k[3:]: nc.dram_tensor(k, v.shape, mybir.dt.from_np(v.dtype), kind="ExternalInput").ap() for k, v in arrays.items()}
    out = nc.dram_tensor("out_0", (BATCH, SEQ, D), F32, kind="ExternalOutput").ap()
    lm_tower(nc, t, out)
    r = run_bass_kernel_spmd(nc, [arrays], core_ids=[0])
    return r.results[0]["out_0"]
```

```python
from contextlib import ExitStack

import numpy as np

import concourse.bass as bass
from concourse import mybir

ALU = mybir.AluOpType
ACT = mybir.ActivationFunctionType
AX = mybir.AxisListType
F32 = mybir.dt.float32
BF16 = mybir.dt.bfloat16
I32 = mybir.dt.int32

P = 128
BATCH, SEQ, D = 8, 512, 256
TOKENS = BATCH * SEQ
TILES = TOKENS // P
SEQ_TILES = SEQ // P
DC = D // P
RANK = 64
HEADS, HD = 16, 16
HALF = HEADS // 2
BH = BATCH * HEADS
KEEP = int(SEQ * 0.3)
QK_SCALE = D ** -0.5
PARTS_Q = (0, 0, 0, 1, 1, 1, 2, 2)
PARTS_K = (0, 1, 2, 0, 1, 2, 0, 1)
SLOTS = len(PARTS_Q)
BIG = 2.0 ** 100
WINDOW = 8
LN_EPS = 1e-5
EXPERTS, TOP_E, EH = 8, 2, 512
BLOCKS, BLOCK, TOP_B, OUTF = 16, 64, 4, 1024
FULL_SLOT = 43
PHM = 4
PICKED_BY_POOL, PICKED_BY_SCALAR = (0, 1), (2, 3)


START = 1


STAGE_SEMAPHORES = {'qkv': ['proj', 'biased', 'part1', 'rest1', 'part2', 'part3', 'stored', 'squares', 'kstats', 'guess', 'guess_kept', 'v_made',
         'v_kept', 'sd', 'ones'],
 'attend': ['half0_loaded', 'half1_loaded', 'scores', 'copied', 'count0', 'count1', 'count2', 'thr1', 'thr2', 'masked', 'pushed',
            'replaced', 'over', 'picked', 'exps', 'probs', 'turned', 'moved', 'pv', 'normed', 'needs', 'over_read',
            'small', 'nmaxed', 'kept_by_pool', 'kept_by_scalar'],
 'moe': ['small', 'logits', 'shifted', 'exped', 'weights', 'wT_made', 'wT_kept', 'bias_made', 'bias_added', 'w_loaded0',
         'w_loaded1', 'hidden', 'active', 'made', 'h_unused', 'y_free'],
 'cos': ['rows_added', 'v_made', 'v_kept', 'sum_made', 'loaded', 'made', 'kept', 'scored', 'mixed', 'summed', 'norm', 'omade', 'oadded'],
 'ffn': ['small', 'w_loaded', 'logits', 'shifted', 'exped', 'mask', 'mT_made', 'mT_kept', 'hidden', 'spread', 'relu', 'masked',
         'made', 'added', 'stored', 'h_unused']}


class Steps:

    def __init__(self, engine, semaphore, base):
        self.engine, self.semaphore, self.base, self.number = engine, semaphore, base, {}

    def did(self, name, operation):
        operation.then_inc(self.semaphore, 1)
        self.number[name] = len(self.number) + 1

    def after(self, name):
        self.engine.wait_ge(self.semaphore, self.base + self.number[name])

    def end(self):
        return self.base + len(self.number)


def load_constants(nc, t, m, sems):
    loaded = sems("const_loaded")
    with nc.Block() as block:
        @block.sync
        def _(sp):
            pairs = [(m.ident[:], t["ident"]), (m.ids[:], t["ids"]), (m.s_col[:], t["s_col"]),
                     (m.vt[:], t["Vt"]), (m.qk_bias[:], t["qk_bias"]), (m.half_mask[:], t["half_mask"]),
                     (m.rank8[:], t["rank8"].to_broadcast((P, 8)))]
            for dst, src in pairs:
                sp.dma_start(dst, src).then_inc(loaded, 16)
            sp.wait_ge(loaded, 16 * len(pairs))

            for stage in m.sem.values():
                for semaphore in stage.values():
                    sp.sem_inc(semaphore, START)

        @block.vector
        def _(v):
            nc.vector.memset(m.eps[:], LN_EPS)
            nc.vector.memset(m.ones[:], 1.0)
            v.wait_ge(loaded, 16 * 7)
            nc.vector.tensor_scalar(m.qk_bias[:, 0:DC], m.qk_bias[:, 0:DC], QK_SCALE, None, ALU.mult)


def embed(nc, t, m, sems):
    gathered = [sems(f"gathered{g}") for g in range(4)]
    turned, scaled, made, kept = sems("u_turned"), sems("u_scaled"), sems("rows_made"), sems("rows_kept")
    with ExitStack() as c:
        rows = c.enter_context(nc.sbuf_tensor("u_rows", [P, TILES, RANK], F32))
        uT = c.enter_context(nc.sbuf_tensor("uT", [RANK, 2, SEQ], F32))
        psT = c.enter_context(nc.psum_tensor("psT_emb", [P, 2, 512], F32))
        psH = c.enter_context(nc.psum_tensor("psH_emb", [P, 4, 512], F32))
        block = c.enter_context(nc.Block())

        @block.gpsimd
        def _(pool):
            for i in range(TILES):
                pool.indirect_dma_start(
                    out=rows[:, i, :], out_offset=None, in_=t["U"],
                    in_offset=bass.IndirectOffsetOnAxis(ap=m.ids[:, i:i + 1], axis=0),
                ).then_inc(gathered[i // 8], 16)

        @block.tensor
        def _(pe):
            for g in range(BATCH):
                if g % 2 == 0:
                    pe.wait_ge(gathered[g // 2], 16 * 8)
                if g >= 2:
                    pe.wait_ge(scaled, g - 1)
                for j in range(4):
                    tr = nc.tensor.transpose(psT[0:RANK, g % 2, j * P:(j + 1) * P], rows[:, 4 * g + j, :], m.ident[:])
                tr.then_inc(turned, 1)
                pe.wait_ge(scaled, g + 1)
                if g >= 2:
                    pe.wait_ge(kept, 2 * (g - 1))
                for j in range(4):
                    nc.tensor.matmul(psH[:, 2 * (g % 2) + j // 2, (j % 2) * D:(j % 2 + 1) * D],
                                     uT[:, g % 2, j * P:(j + 1) * P], m.vt[:],
                                     start=True, stop=True, skip_group_check=True).then_inc(made, 1)

        @block.vector
        def _(v):
            for g in range(BATCH):
                v.wait_ge(turned, g + 1)
                if g >= 2:
                    v.wait_ge(made, 4 * (g - 1))
                nc.vector.tensor_scalar(uT[:, g % 2, :], psT[0:RANK, g % 2, :], m.s_col[:], None, ALU.mult).then_inc(scaled, 1)
                if g:
                    v.wait_ge(kept, 2 * g)
                    for i in range(4 * g - 4, 4 * g):
                        moments(nc, m, i, m.resid)
            v.wait_ge(kept, 2 * BATCH)
            for i in range(TILES - 4, TILES):
                moments(nc, m, i, m.resid)

        @block.scalar
        def _(act):
            for i in range(0, TILES, 2):
                act.wait_ge(made, i + 2)
                nc.scalar.copy(m.resid[:, i:i + 2, :], psH[:, (i // 2) % 4, :].rearrange("p (n d) -> p n d", n=2)).then_inc(kept, 1)


def moments(nc, m, i, src):
    return nc.vector.bn_stats(m.moments[:, i:i + 1, :] if isinstance(i, int) else m.moments[:, bass.ds(i, 1), :],
                              src[:, i:i + 1, :] if isinstance(i, int) else src[:, bass.ds(i, 1), :])


def norm_stats(nc, v, st, mean, var):
    even, odd = st[:, :, 1:2].rearrange("p n a -> p (n a)"), st[:, :, 4:5].rearrange("p n a -> p (n a)")
    m2e, m2o = st[:, :, 2:3].rearrange("p n a -> p (n a)"), st[:, :, 5:6].rearrange("p n a -> p (n a)")
    nc.vector.tensor_tensor(mean, even, odd, ALU.add)
    nc.vector.tensor_tensor(var, even, odd, ALU.subtract)
    v.drain()
    nc.vector.tensor_scalar(mean, mean, 0.5, None, ALU.mult)
    nc.vector.tensor_tensor(var, var, var, ALU.mult)
    nc.vector.tensor_tensor(m2e, m2e, m2o, ALU.add)
    v.drain()
    nc.vector.tensor_scalar(var, var, 0.25, None, ALU.mult)
    nc.vector.tensor_scalar(m2e, m2e, 1.0 / D, None, ALU.mult)
    v.drain()
    nc.vector.tensor_tensor(var, var, m2e, ALU.add)


def norm_turn(nc, m, sems, tag, src, keep, xT, gain=None, shift=None, leave_moments=False):
    vars_ready, root, rows_ready = sems("vars_ready" + tag), sems("root" + tag), sems("xhat_ready" + tag)
    turned, moved = sems("x_turned" + tag), sems("x_moved" + tag)
    G = 2
    STEPS = TILES // G
    WIDE = 8
    with ExitStack() as c:
        mean = c.enter_context(nc.sbuf_tensor("ln_mean" + tag, [P, TILES], F32))
        var = c.enter_context(nc.sbuf_tensor("ln_var" + tag, [P, TILES], F32))
        rstd = c.enter_context(nc.sbuf_tensor("ln_rstd" + tag, [P, TILES], F32))
        ring = None
        if keep is None:
            ring = c.enter_context(nc.sbuf_tensor("xhat" + tag, [P, 2 * G, D], F32))
        ps = c.enter_context(nc.psum_tensor("psN" + tag, [P, 2, 512], F32))
        block = c.enter_context(nc.Block())
        row = (lambda i: ring[:, i % (2 * G), :]) if keep is None else (lambda i: keep[:, i, :])

        @block.vector
        def _(v):
            norm_stats(nc, v, m.moments, mean[:], var[:])
            v.drain().then_inc(vars_ready, 1)
            v.wait_ge(root, 1)
            nc.vector.reciprocal(rstd[:], rstd[:])
            v.drain()
            for i in range(TILES):
                step = i // G
                if keep is None and i % G == 0 and step >= 2:
                    v.wait_ge(turned, step - 1)
                op = nc.vector.tensor_scalar(row(i), src[:, i, :], mean[:, i:i + 1], rstd[:, i:i + 1], ALU.subtract, ALU.mult)
                if i % G == G - 1 and gain is None:
                    op.then_inc(rows_ready, 1)
                    if leave_moments and step:
                        v.wait_ge(rows_ready, step)
                        for j in range((step - 1) * G, step * G):
                            moments(nc, m, j, keep)
                if gain is not None and i % WIDE == WIDE - 1:
                    v.drain()
                    part = keep[:, i - WIDE + 1:i + 1, :]
                    for other, how in ((gain, ALU.mult), (shift, ALU.add)):
                        nc.vector.tensor_tensor(part, part, other.rearrange("p (o d) -> p o d", o=1).to_broadcast((P, WIDE, D)), how)
                        last = v.drain()
                    last.then_inc(rows_ready, WIDE // G)
            if leave_moments:
                v.wait_ge(rows_ready, STEPS)
                for j in range(TILES - G, TILES):
                    moments(nc, m, j, keep)

        @block.tensor
        def _(pe):
            for s in range(STEPS):
                pe.wait_ge(rows_ready, s + 1)
                if s >= 2:
                    pe.wait_ge(moved, s - 1)
                for ch in range(DC):
                    for j in range(G):
                        tr = nc.tensor.transpose(ps[:, s % 2, (ch * G + j) * P:(ch * G + j + 1) * P],
                                                 row(s * G + j)[:, ch * P:(ch + 1) * P], m.ident[:])
                tr.then_inc(turned, 1)

        @block.scalar
        def _(act):
            act.wait_ge(vars_ready, 1)
            nc.scalar.activation(rstd[:], var[:], ACT.Sqrt, bias=m.eps[:]).then_inc(root, 1)
            for s in range(STEPS):
                act.wait_ge(turned, s + 1)
                nc.scalar.copy(xT[:, :, s * G * P:(s + 1) * G * P],
                               ps[:, s % 2, :].rearrange("p (c n) -> p c n", c=DC)).then_inc(moved, 1)


def qkv(nc, t, m, sems):
    w_loaded = sems("w_qkv_loaded")
    s = m.sem["qkv"]
    NCH = 2 * DC
    with ExitStack() as c:
        sb = lambda n, sh, dt=F32: c.enter_context(nc.sbuf_tensor(n, sh, dt))
        w = sb("w_qkv", [P, DC, 3 * D])
        vb = sb("v_bias", [P, D])
        qk = sb("qk", [P, NCH, SEQ])
        rest = sb("rest", [P, NCH, SEQ])
        parts = sb("parts", [P, NCH, 3, SEQ], BF16)
        sq = sb("q_sq", [P, DC, SEQ])
        kst = sb("k_st", [P, DC, 6])
        kmv = sb("k_mv", [P, DC, 2])
        kdiag = sb("k_diag", [P, DC, 2, HALF])
        psQ = c.enter_context(nc.psum_tensor("psQ_qkv", [P, NCH, 512], F32))
        psV = c.enter_context(nc.psum_tensor("psV_qkv", [P, 2, 512], F32))
        psG = c.enter_context(nc.psum_tensor("psG_qkv", [P, 512], F32))
        guess = psG[:, 0:SEQ_TILES * DC * 2 * HALF].rearrange("p (i c a h) -> p i c a h", i=SEQ_TILES, c=DC, a=2)
        block = c.enter_context(nc.Block())

        @block.sync
        def _(sp):
            sp.dma_start(w[:], t["W_qkvT"].rearrange("(c p) e -> p c e", p=P)).then_inc(w_loaded, 16)
            sp.dma_start(vb[:], t["v_bias"].to_broadcast((P, D))).then_inc(w_loaded, 16)
            with sp.Fori(0, BATCH) as b:
                for j in range(NCH):
                    which, ch = j // DC, j % DC
                    sp.wait_ge(s["part3"], START + b * NCH + (j + 1))
                    dst = m.parts_dram[which][bass.ds(b, 1), :, ch * P:(ch + 1) * P, :].rearrange("o a p n -> p (o a) n")
                    sp.dma_start(dst, parts[:, j, :, :]).then_inc(s["stored"], 16)
            sp.wait_ge(s["stored"], START + 16 * BATCH * NCH)

        @block.tensor
        def _(pe):
            pe.wait_ge(w_loaded, 32)
            for b in range(BATCH):
                pe.wait_ge(s["biased"], START + b * NCH)
                for j in range(NCH):
                    for ch in range(DC):
                        mm = nc.tensor.matmul(psQ[:, j, :], w[:, ch, j * P:(j + 1) * P],
                                              m.xT[:, ch, bass.ds(b * SEQ, SEQ)], start=(ch == 0), stop=(ch == DC - 1))
                    mm.then_inc(s["proj"], 1)
                pe.wait_ge(s["v_kept"], START + b * SEQ_TILES)
                for i in range(SEQ_TILES):
                    for ch in range(DC):
                        mm = nc.tensor.matmul(psV[:, i // 2, (i % 2) * D:(i % 2 + 1) * D],
                                              m.xT[:, ch, bass.ds(b * SEQ + i * P, P)], w[:, ch, 2 * D:3 * D],
                                              start=(ch == 0), stop=(ch == DC - 1), skip_group_check=True)
                    mm.then_inc(s["v_made"], 1)
                pe.wait_ge(s["squares"], START + (b + 1) * DC)
                pe.wait_ge(s["kstats"], START + b + 1)
                pe.wait_ge(s["guess_kept"], START + b)
                for i in range(SEQ_TILES):
                    for ch in range(DC):
                        nc.tensor.matmul(guess[:, i, ch, 0, :], qk[:, ch, i * P:(i + 1) * P], kdiag[:, ch, 0, :],
                                         start=True, stop=True, skip_group_check=True)
                        mm = nc.tensor.matmul(guess[:, i, ch, 1, :], sq[:, ch, i * P:(i + 1) * P], kdiag[:, ch, 1, :],
                                              start=True, stop=True, skip_group_check=True)
                mm.then_inc(s["guess"], 1)

        @block.scalar
        def _(act):
            with act.Fori(0, BATCH) as b:
                act.wait_ge(s["guess"], START + b)
                act.wait_ge(s["rest1"], START + b * NCH)
                for j in range(NCH):
                    act.wait_ge(s["proj"], START + b * NCH + (j + 1))
                    nc.scalar.activation(qk[:, j, :], psQ[:, j, :], ACT.Identity, bias=m.qk_bias[:, j:j + 1],
                                         scale=QK_SCALE if j < DC else 1.0).then_inc(s["biased"], 1)
                for ch in range(DC):
                    act.wait_ge(s["biased"], START + b * NCH + (ch + 1))
                    nc.scalar.activation(sq[:, ch, :], qk[:, ch, :], ACT.Square).then_inc(s["squares"], 1)
                for j in range(NCH):
                    act.wait_ge(s["rest1"], START + b * NCH + (j + 1))
                    nc.scalar.copy(parts[:, j, 1, :], rest[:, j, :]).then_inc(s["part2"], 1)
            act.wait_ge(s["guess_kept"], START + BATCH)
            nc.scalar.activation(m.step[:], m.step[:], ACT.Sqrt).then_inc(s["sd"], 1)

        @block.gpsimd
        def _(pool):
            with pool.Fori(0, BATCH) as b:
                for j in range(NCH):
                    pool.wait_ge(s["part2"], START + b * NCH + (j + 1))
                    nc.gpsimd.tensor_tensor(parts[:, j, 2, :], rest[:, j, :], parts[:, j, 1, :], ALU.subtract).then_inc(s["part3"], 1)

        @block.vector
        def _(v):
            nc.vector.memset(m.v_aug[:, :, :, HD:HD + 1], 1.0).then_inc(s["ones"], 1)
            v.wait_ge(w_loaded, 32)
            with v.Fori(0, BATCH) as b:
                v.wait_ge(s["stored"], START + 16 * NCH * b)
                v.wait_ge(s["guess"], START + b)
                for j in range(NCH):
                    v.wait_ge(s["biased"], START + b * NCH + (j + 1))
                    nc.vector.tensor_copy(parts[:, j, 0, :], qk[:, j, :]).then_inc(s["part1"], 1)
                    if j >= DC:
                        nc.vector.bn_stats(kst[:, j - DC, :], qk[:, j, :])
                    v.wait_ge(s["part1"], START + b * NCH + (j + 1))
                    nc.vector.tensor_tensor(rest[:, j, :], qk[:, j, :], parts[:, j, 0, :], ALU.subtract).then_inc(s["rest1"], 1)
                v.drain()
                for ch in range(DC):
                    nc.vector.bn_aggr(kmv[:, ch, :], kst[:, ch, :])
                v.drain()
                for ch in range(DC):
                    for a in range(2):
                        op = nc.vector.tensor_scalar(kdiag[:, ch, a, :], m.half_mask[:], kmv[:, ch, a:a + 1], None, ALU.mult)
                op.then_inc(s["kstats"], 1)
                for i in range(SEQ_TILES):
                    v.wait_ge(s["v_made"], START + b * SEQ_TILES + (i // 2 * 2 + 2))
                    nc.vector.tensor_tensor(m.v_aug[:, bass.ds(b * HEADS, HEADS), i, 0:HD],
                                            psV[:, i // 2, (i % 2) * D:(i % 2 + 1) * D].rearrange("p (h d) -> p h d", h=HEADS),
                                            vb[:].rearrange("p (h d) -> p h d", h=HEADS), ALU.add).then_inc(s["v_kept"], 1)
                v.wait_ge(s["guess"], START + b + 1)
                for ch in range(DC):
                    nc.vector.tensor_copy(m.thr0[:, bass.ds(b * HEADS + ch * HALF, HALF), :],
                                          guess[:, :, ch, 0, :].rearrange("p i h -> p h i"))
                    op = nc.vector.tensor_copy(m.step[:, bass.ds(b * HEADS + ch * HALF, HALF), :],
                                               guess[:, :, ch, 1, :].rearrange("p i h -> p h i"))
                v.drain().then_inc(s["guess_kept"], 1)
            v.wait_ge(s["sd"], START + 1)
            nc.vector.scalar_tensor_tensor(m.thr0[:], m.step[:], -0.545, m.thr0[:], ALU.mult, ALU.subtract)
            v.drain()
            nc.vector.tensor_scalar(m.step[:], m.step[:], 0.5 / (SEQ * 0.313), None, ALU.mult)


def attend(nc, t, m, sems):
    s = m.sem["attend"]
    ST = SEQ_TILES
    HB = 2 * BATCH
    with ExitStack() as c:
        sb = lambda n, sh, dt=F32: c.enter_context(nc.sbuf_tensor(n, sh, dt))
        ring = [sb(n, [P, HEADS, SEQ], BF16) for n in ("q_ring", "k_ring")]
        X = sb("X", [P, 2, ST, SEQ])
        E = sb("E", [P, 2, ST, SEQ])
        sgn = sb("sgn", [P, 2, ST, SEQ], BF16)
        M = sb("M", [P, ST, SEQ], BF16)
        Z = sb("Z", [P, ST, SEQ])
        kept = sb("kept", [P, ST, SEQ], BF16)
        minus_one = sb("minus_one", [P, 1])
        gate = sb("gate", [P, 1])
        PT = sb("PT", [P, ST, SEQ])
        push = sb("push", [P, P], BF16)
        nmax = sb("nmax", [P, 2, ST])
        cnt = sb("cnt", [P, 3, ST])
        dist = sb("dist", [P, 4, ST])
        nthr = sb("nthr", [P, 4, ST])
        thr = sb("thr", [P, ST])
        top = sb("top", [P, ST])
        secant, wish, sq_d, gap, partner = (sb("upd_" + n, [P, ST]) for n in ("secant", "wish", "sq", "gap", "partner"))
        far_d = sb("upd_far", [P, ST])
        mv = sb("upd_moves", [P, 3, ST])
        flip = sb("upd_flips", [P, 3, ST], I32)
        c3 = sb("c3", [P, ST])
        need = sb("need", [P, ST])
        lim = sb("lim", [P, ST, 8])
        best = sb("best", [P, ST, 8])
        overs = sb("overs", [P, 3, ST])
        code = sb("code", [1, 1], I32)
        flags = sb("flags", [1, 3 * ST])
        flag_weights = sb("flag_weights", [1, 3 * ST])
        rz = sb("rz", [P, ST, 1])
        psS = c.enter_context(nc.psum_tensor("psS_at", [P, ST, 512], F32))
        psT = c.enter_context(nc.psum_tensor("psPT_at", [P, 3, 512], F32))
        psO = c.enter_context(nc.psum_tensor("psO_at", [P, 512], F32))
        O = psO[:, 0:ST * (HD + 1)].rearrange("p (i d) -> p i d", i=ST)
        over_ps = psO[0:1, 256:256 + 3 * ST]
        block = c.enter_context(nc.Block())

        @block.sync
        def _(sp):
            def load(hb_of, half):
                for which, parts in ((0, PARTS_Q), (1, PARTS_K)):
                    for slot in range(SLOTS):
                        src = m.parts_dram[which][bass.ds(hb_of, 1), parts[slot], half * P:(half + 1) * P, :]
                        sp.dma_start(ring[which][slot * HD:(slot + 1) * HD, half * HALF:(half + 1) * HALF, :],
                                     src.rearrange("o (h d) n -> d (o h) n", d=HD)).then_inc(s[f"half{half}_loaded"], 16)
            load(0, 0)
            load(0, 1)
            with sp.Fori(1, BATCH) as b:
                for half in range(2):
                    sp.wait_ge(s["pushed"], START + ST * (HEADS * (b - 1) + (half + 1) * HALF))
                    load(b, half)

        @block.tensor
        def _(pe):
            def ring_ready(h):
                load = 2 * SLOTS * 16
                pe.wait_ge(s["half0_loaded"], START + load * (h // HEADS + 1))
                pe.wait_ge(s["half1_loaded"], START + load * ((h + HALF) // HEADS))

            def scores(h, i):
                r = h % HEADS
                return nc.tensor.matmul(psS[:, i, :], ring[0][:, bass.ds(r, 1), i * P:(i + 1) * P].rearrange("p o n -> p (o n)"),
                                        ring[1][:, bass.ds(r, 1), :].rearrange("p o n -> p (o n)"), start=True, stop=True)

            def first_scores(h):
                ring_ready(h)
                for i in range(ST):
                    scores(h, i).then_inc(s["scores"], 1)

            def scores_again(h):
                r = h % HEADS
                for i in range(ST):
                    if isinstance(h, int) and h == BH - 1:
                        pe.wait_ge(s["replaced"], START + ST * (h - 1) + (i + 1))
                    else:
                        pe.wait_ge(s["copied"], START + ST * (h + 1) + (i + 1))
                    nc.tensor.matmul(psS[:, i, :], ring[0][:, bass.ds(r, 1), i * P:(i + 1) * P].rearrange("p o n -> p (o n)"),
                                     ring[1][:, bass.ds(r, 1), :].rearrange("p o n -> p (o n)"), start=True, stop=False)

            def push_selected(h):
                for i in range(ST):
                    pe.wait_ge(s["masked"], START + ST * h + (i + 1))
                    nc.tensor.matmul(psS[:, i, :], push[:], M[:, i, :], start=False, stop=True).then_inc(s["pushed"], 1)

            def next_scores(h, tiles=range(ST)):
                ring_ready(h)
                for i in tiles:
                    pe.wait_ge(s["replaced"], START + ST * (h - 2) + (i + 1))
                    scores(h, i).then_inc(s["scores"], 1)

            def count_over(h):
                pe.wait_ge(s["needs"], START + h + 1)
                if not (isinstance(h, int) and h < 2):
                    pe.wait_ge(s["normed"], START + h - 1)
                nc.tensor.matmul(over_ps, m.ones[:, 0:1], overs[:].rearrange("p a i -> p (a i)"),
                                 start=True, stop=True, skip_group_check=True).then_inc(s["over"], 1)

            def values_ready(h):
                pe.wait_ge(s["moved"], START + ST * (h + 1))
                pe.wait_ge(s["over_read"], START + (BH if isinstance(h, int) and h >= BH - 2 else h + 2))
                if not (isinstance(h, int) and h == 0):
                    pe.wait_ge(s["normed"], START + h)

            def values(h, tiles):
                for i in tiles:
                    for j in range(ST):
                        mm = nc.tensor.matmul(O[:, i, :], PT[:, i, j * P:(j + 1) * P],
                                              m.v_aug[:, bass.ds(h, 1), j, :].rearrange("p o d -> p (o d)"),
                                              start=(j == 0), stop=(j == ST - 1), skip_group_check=True)
                if i == ST - 1:
                    mm.then_inc(s["pv"], 1)

            def turn(h, par, tiles):
                for i in tiles:
                    pe.wait_ge(s["moved"], START + ST * h + (1 if i == 3 else 0))
                    pe.wait_ge(s["probs"], START + ST * h + (i + 1))
                    for j in range(ST):
                        tr = nc.tensor.transpose(psT[:, i % 3, j * P:(j + 1) * P], E[:, par, i, j * P:(j + 1) * P], m.ident[:])
                    tr.then_inc(s["turned"], 1)

            def slot(sl, par, prev=True, cur=True, nxt=True):
                if prev:
                    push_selected(sl - 1)
                    count_over(sl - 1)
                turn(sl - 2, par, (3,))
                values_ready(sl - 2)
                values(sl - 2, (0,))
                if nxt:
                    next_scores(sl + 1, (0,))
                values(sl - 2, (1,))
                if nxt:
                    next_scores(sl + 1, (1, 2))
                values(sl - 2, (2,))
                if nxt:
                    next_scores(sl + 1, (3,))
                values(sl - 2, (3,))
                if cur:
                    scores_again(sl)
                if prev:
                    turn(sl - 1, 1 - par, (0, 1, 2))

            first_scores(0)
            for i in range(ST):
                pe.wait_ge(s["copied"], START + i + 1)
                if i == 0:
                    ring_ready(1)
                scores(1, i).then_inc(s["scores"], 1)
            scores_again(0)
            push_selected(0)
            count_over(0)
            next_scores(2)
            scores_again(1)
            turn(0, 0, (0, 1, 2))
            with pe.Fori(1, BH // 2 - 1) as pair:
                s0 = pair * 2
                slot(s0, 0)
                slot(s0 + 1, 1)
            slot(BH - 2, 0)
            slot(BH - 1, 1, nxt=False)
            slot(BH, 0, cur=False, nxt=False)
            slot(BH + 1, 1, prev=False, cur=False, nxt=False)

        @block.scalar
        def _(act):
            def count(h, par, which):
                if which == 0:
                    pass
                else:
                    act.wait_ge(s[f"thr{which}"], START + h + 1)
                for i in range(ST):
                    if which == 0:
                        act.wait_ge(s["copied"], START + ST * h + (i + 1))
                    bias = m.thr0[:, bass.ds(h, 1), i:i + 1].rearrange("p o i -> p (o i)") if which == 0 else nthr[:, which, i:i + 1]
                    nc.scalar.activation(sgn[:, 1 if which else 0, i, :], X[:, par, i, :], ACT.Sign, bias=bias,
                                         accum_out=cnt[:, which, i:i + 1]).then_inc(s[f"count{which}"], 1)

            def exps(h, par, first=False):
                act.wait_ge(s["nmaxed"], START + h + 1)
                if not first:
                    act.wait_ge(s["turned"], START + ST * (h - 1))
                for i in range(ST):
                    nc.scalar.activation(E[:, par, i, :], X[:, par, i, :], ACT.Exp, bias=nmax[:, par, i:i + 1]).then_inc(s["exps"], 1)

            def pick(h):
                act.wait_ge(s["picked"], START + h + 1)
                for i in PICKED_BY_SCALAR:
                    nc.scalar.activation(kept[:, i, :], Z[:, i, :], ACT.Relu, bias=minus_one[:, 0:1],
                                         scale=-2.0 / BIG).then_inc(s["kept_by_scalar"], 1)

            def move(h, tiles):
                if 0 in tiles:
                    act.wait_ge(s["pv"], START + h)
                for i in tiles:
                    act.wait_ge(s["turned"], START + ST * h + (i + 1))
                    nc.scalar.copy(PT[:, i, :], psT[:, i % 3, :]).then_inc(s["moved"], 1)

            def slot(sl, par, prev=True, old=True, nxt=True):
                count(sl, par, 1)
                if old:
                    move(sl - 2, (3,))
                exps(sl, par, not old)
                count(sl, par, 2)
                if prev:
                    pick(sl - 1)
                if nxt:
                    count(sl + 1, 1 - par, 0)
                if prev:
                    move(sl - 1, (0, 1, 2))

            nc.scalar.activation(minus_one[:], m.ones[:, 0:1], ACT.Copy, scale=-1.0)
            act.drain()
            count(0, 0, 0)
            slot(0, 0, prev=False, old=False)
            slot(1, 1, old=False)
            with act.Fori(1, BH // 2 - 1) as pair:
                s0 = pair * 2
                slot(s0, 0)
                slot(s0 + 1, 1)
            slot(BH - 2, 0)
            slot(BH - 1, 1, nxt=False)
            move(BH - 2, (3,))
            pick(BH - 1)
            move(BH - 1, range(ST))

        @block.gpsimd
        def _(pool):
            with pool.Fori(0, BH // 2) as pair:
                h0 = pair * 2
                for k in range(2):
                    h = h0 + k
                    pool.wait_ge(s["exps"], START + ST * (h + 1))
                    pool.wait_ge(s["picked"], START + h + 1)
                    nc.gpsimd.tensor_tensor(gate[:], m.ones[:, 0:1], m.ones[:, 0:1], ALU.mult)
                    for i in PICKED_BY_POOL:
                        nc.gpsimd.tensor_scalar(kept[:, i, :], Z[:, i, :], -BIG / 2, None, ALU.is_lt).then_inc(s["kept_by_pool"], 1)
                    for i in range(ST):
                        for semaphore, tiles in (("kept_by_pool", PICKED_BY_POOL), ("kept_by_scalar", PICKED_BY_SCALAR)):
                            if i in tiles:
                                pool.wait_ge(s[semaphore], START + len(tiles) * h + (tiles.index(i) + 1))
                        nc.gpsimd.tensor_tensor(E[:, k, i, :], E[:, k, i, :], kept[:, i, :], ALU.mult).then_inc(s["probs"], 1)

        @block.vector
        def _(v):
            AIM = KEEP - WINDOW // 2
            OFF = (0.0, 0.25, 0.625)
            FAR2 = (WINDOW + 1.0) ** 2

            def row(ap, h):
                return ap[:, bass.ds(h, 1), :].rearrange("p o i -> p (o i)")

            def mask(h, par, i):
                nc.vector.tensor_scalar(M[:, i, :], X[:, par, i, :], thr[:, i:i + 1], None, ALU.is_gt, ALU.add,
                                        accum_out=c3[:, i:i + 1]).then_inc(s["masked"], 1)

            def copy_scores(h, par, i):
                v.wait_ge(s["scores"], START + ST * h + (i + 1))
                nc.vector.tensor_scalar(X[:, par, i, :], psS[:, i, :], 1.0, None, ALU.mult, ALU.max,
                                        accum_out=top[:, i:i + 1]).then_inc(s["copied"], 1)

            def take_best(i):
                nc.vector.match_replace(Z[:, i, :], best[:, i, :], psS[:, i, :], -BIG).then_inc(s["replaced"], 1)

            def negate_max(h, par):
                nc.vector.tensor_scalar(nmax[:, par, :], top[:], -1.0, None, ALU.mult).then_inc(s["nmaxed"], 1)

            def distance(st, h, k):
                v.wait_ge(s[f"count{k}"], START + ST * (h + 1))
                st.did(f"dist{k}", nc.vector.tensor_scalar(dist[:, k, :], cnt[:, k, :], SEQ - 2.0 * AIM + OFF[k], None, ALU.add))

            def add_round(i, count):
                tiles = slice(i, i + count)
                nc.vector.tensor_scalar(need[:, tiles], need[:, tiles], -float(WINDOW), None, ALU.add)
                for k in range(i, i + count):
                    nc.vector.max(best[:, k, :], Z[:, k, :])
                v.drain()
                nc.vector.tensor_tensor(lim[:, tiles, :], ranks[:, tiles, :], needs8[:, tiles, :], ALU.is_lt)
                v.drain()
                nc.vector.tensor_scalar(lim[:, tiles, :], lim[:, tiles, :], 2 * BIG, -BIG, ALU.mult, ALU.add)
                v.drain()
                nc.vector.tensor_tensor(best[:, tiles, :], best[:, tiles, :], lim[:, tiles, :], ALU.min)
                v.drain()
                for k in range(i, i + count):
                    nc.vector.match_replace(Z[:, k, :], best[:, k, :], Z[:, k, :], -BIG)
                v.drain()

            def rare_rows(par):
                found = v.value_load(code[0:1, 0:1], min_val=0, max_val=3 * ST * SERIOUS)
                with v.If(found > 0):
                    v.drain()
                    for i in range(ST):
                        with v.If(found % 2 ** (i + 1) > 2 ** i - 1):
                            add_round(i, 1)
                        v.end_ifs()
                    with v.If(found > SERIOUS - 1):
                        nc.vector.memset(need[:], float(KEEP + WINDOW))
                        for i in range(ST):
                            nc.vector.tensor_scalar(Z[:, i, :], X[:, par, i, :], 1.0, None, ALU.mult)
                        v.drain()
                        with v.Fori(0, -(-KEEP // WINDOW)):
                            add_round(0, ST)
                    v.end_ifs()
                v.end_ifs()

            SERIOUS = 2 ** ST
            ranks = m.rank8[:].rearrange("p (o e) -> p o e", o=1).to_broadcast((P, ST, 8))
            needs8 = need[:].rearrange("p (i o) -> p i o", o=1).to_broadcast((P, ST, 8))

            def slot(sl, par, base, prev=True, nxt=True, cur=True, old=True):
                st = Steps(v, s["small"], base)
                h, other = sl - 1, 1 - par
                if prev:
                    v.wait_ge(s["small"], base)
                    mask(h, other, 0)
                    mask(h, other, 1)
                if cur:
                    distance(st, sl, 0)
                if prev:
                    mask(h, other, 2)
                if cur:
                    st.after("dist0")
                    st.did("q0", nc.vector.tensor_tensor(sq_d[:], dist[:, 0, :], dist[:, 0, :], ALU.mult))
                    st.did("x0", nc.vector.tensor_tensor(wish[:], dist[:, 0, :], row(m.step, sl), ALU.mult))
                if prev:
                    mask(h, other, 3)
                if cur:
                    st.after("x0")
                    st.did("mv1", nc.vector.scalar_tensor_tensor(mv[:, 0, :], sq_d[:], FAR2, wish[:], ALU.is_gt, ALU.mult))
                if old:
                    v.wait_ge(s["pv"], START + sl - 2)
                    st.did("sum", nc.vector.reciprocal(rz[:], O[:, :, HD:HD + 1]))
                if prev:
                    v.wait_ge(s["masked"], START + ST * (h + 1))
                    st.did("need", nc.vector.tensor_scalar(need[:], c3[:], -1.0, float(KEEP), ALU.mult, ALU.add))
                if cur:
                    st.after("mv1")
                    nc.vector.tensor_tensor(nthr[:, 1, :], row(m.thr0, sl), mv[:, 0, :], ALU.subtract).then_inc(s["thr1"], 1)
                if old:
                    st.after("sum")
                    nc.vector.tensor_tensor(m.heads_out[:, bass.ds(sl - 3, 1), :, :].rearrange("p o i d -> p (o i) d"),
                                            O[:, :, 0:HD], rz[:].to_broadcast((P, ST, HD)), ALU.mult).then_inc(s["normed"], 1)
                if prev:
                    st.after("need")
                    st.did("below", nc.vector.tensor_tensor(lim[:], ranks, needs8, ALU.is_lt))
                    st.did("over8", nc.vector.tensor_scalar(overs[:, 0, :], need[:], float(WINDOW), None, ALU.is_gt))
                    st.did("over16", nc.vector.tensor_scalar(overs[:, 1, :], need[:], 2.0 * WINDOW, None, ALU.is_gt))
                    nc.vector.tensor_scalar(overs[:, 2, :], need[:], 0.0, None, ALU.is_lt).then_inc(s["needs"], 1)
                    st.after("below")
                    st.did("lim", nc.vector.tensor_scalar(lim[:], lim[:], 2 * BIG, -BIG, ALU.mult, ALU.add))
                    st.after("lim")
                    v.wait_ge(s["pushed"], START + ST * (h + 1))
                if cur:
                    st.did("dp", nc.vector.tensor_copy(partner[:], dist[:, 0, :]))
                if prev:
                    for i in range(ST - 1):
                        nc.vector.max(best[:, i, :], psS[:, i, :])
                    v.wait_ge(s["over"], START + h + 1)
                    nc.vector.scalar_tensor_tensor(flags[:], over_ps, 1.0, flag_weights[:], ALU.min, ALU.mult).then_inc(s["over_read"], 1)
                if cur:
                    distance(st, sl, 1)
                if prev:
                    st.did("best", nc.vector.max(best[:, ST - 1, :], psS[:, ST - 1, :]))
                if cur:
                    st.after("dist1")
                    st.did("q1", nc.vector.tensor_tensor(sq_d[:], dist[:, 1, :], dist[:, 1, :], ALU.mult))
                    st.did("e", nc.vector.tensor_tensor(gap[:], dist[:, 0, :], dist[:, 1, :], ALU.subtract))
                    if prev:
                        v.wait_ge(s["probs"], START + ST * h)
                    st.did("pr", nc.vector.tensor_tensor(wish[:], dist[:, 0, :], dist[:, 1, :], ALU.mult))
                if prev:
                    if not cur:
                        v.wait_ge(s["probs"], START + ST * h)
                    st.after("best")
                    st.did("chosen01", nc.vector.tensor_tensor(best[:, 0:2, :], best[:, 0:2, :], lim[:, 0:2, :], ALU.min))
                if cur:
                    st.after("q1")
                    st.did("far1", nc.vector.scalar_tensor_tensor(far_d[:], sq_d[:], FAR2, dist[:, 1, :], ALU.is_gt, ALU.mult))
                    st.after("e")
                    st.did("re", nc.vector.reciprocal(gap[:], gap[:]))
                if prev:
                    st.after("chosen01")
                if cur:
                    if not prev:
                        st.after("pr")
                    st.did("flip1", nc.vector.tensor_scalar(flip[:, 0, :], wish[:], 0.0, None, ALU.is_lt))
                if prev:
                    take_best(0)
                if cur:
                    st.after("far1")
                    st.did("by_step1", nc.vector.tensor_tensor(mv[:, 1, :], far_d[:], row(m.step, sl), ALU.mult))
                    st.did("g1", nc.vector.tensor_tensor(secant[:], far_d[:], mv[:, 0, :], ALU.mult))
                if prev:
                    v.wait_ge(s["over_read"], START + h + 1)
                    with nc.allow_low_precision(reason="a sum of small whole numbers"):
                        st.did("code", nc.vector.tensor_reduce(code[:], flags[:], AX.X, ALU.add))
                if cur:
                    st.after("g1")
                    st.did("secant1", nc.vector.tensor_tensor(gap[:], gap[:], secant[:], ALU.mult))
                if prev:
                    take_best(1)
                if cur:
                    st.after("secant1")
                if prev:
                    st.did("chosen23", nc.vector.tensor_tensor(best[:, 2:4, :], best[:, 2:4, :], lim[:, 2:4, :], ALU.min))
                if cur:
                    st.did("mv2", nc.vector.copy_predicated(mv[:, 1, :], flip[:, 0, :], gap[:]))
                    st.after("mv2")
                elif prev:
                    st.after("chosen23")
                if cur:
                    nc.vector.tensor_tensor(nthr[:, 2, :], nthr[:, 1, :], mv[:, 1, :], ALU.subtract).then_inc(s["thr2"], 1)
                if prev:
                    take_best(2)
                    take_best(3)
                if prev:
                    rare_rows(other)
                    v.drain().then_inc(s["picked"], 1)
                if nxt:
                    copy_scores(sl + 1, other, 0)
                    copy_scores(sl + 1, other, 1)
                if cur:
                    v.wait_ge(s["thr2"], START + sl + 1)
                    st.did("back0", nc.vector.tensor_tensor(mv[:, 2, :], mv[:, 0, :], mv[:, 1, :], ALU.add))
                    distance(st, sl, 2)
                    st.after("dist2")
                    st.did("pr2", nc.vector.tensor_tensor(wish[:], dist[:, 1, :], dist[:, 2, :], ALU.mult))
                    st.did("q2", nc.vector.tensor_tensor(sq_d[:], dist[:, 2, :], dist[:, 2, :], ALU.mult))
                if nxt:
                    copy_scores(sl + 1, other, 2)
                if cur:
                    st.after("pr2")
                    st.did("flip2", nc.vector.tensor_scalar(flip[:, 1, :], wish[:], 0.0, None, ALU.is_lt))
                    st.after("q2")
                    st.did("far2", nc.vector.tensor_scalar(sq_d[:], sq_d[:], FAR2, None, ALU.is_gt))
                    st.after("flip2")
                    st.did("flips", nc.vector.tensor_tensor(flip[:, 2, :], flip[:, 0, :], flip[:, 1, :], ALU.max))
                    st.did("pt", nc.vector.copy_predicated(mv[:, 2, :], flip[:, 1, :], mv[:, 1, :]))
                    st.did("pd", nc.vector.copy_predicated(partner[:], flip[:, 1, :], dist[:, 1, :]))
                    st.after("far2")
                    st.did("far_d2", nc.vector.scalar_tensor_tensor(far_d[:], dist[:, 2, :], 3.0, sq_d[:], ALU.add, ALU.mult))
                if nxt:
                    copy_scores(sl + 1, other, 3)
                if cur:
                    st.after("pd")
                    st.did("e2", nc.vector.tensor_tensor(gap[:], partner[:], dist[:, 2, :], ALU.subtract))
                    st.after("far_d2")
                    st.did("by_step2", nc.vector.tensor_tensor(wish[:], far_d[:], row(m.step, sl), ALU.mult))
                    st.after("e2")
                    st.did("re2", nc.vector.reciprocal(gap[:], gap[:]))
                    if nxt:
                        v.wait_ge(s["copied"], START + ST * (sl + 2))
                    st.did("g2", nc.vector.tensor_tensor(secant[:], far_d[:], mv[:, 2, :], ALU.mult))
                    st.after("g2")
                    st.did("secant2", nc.vector.tensor_tensor(gap[:], gap[:], secant[:], ALU.mult))
                    st.after("secant2")
                if nxt:
                    negate_max(sl + 1, other)
                if cur:
                    st.did("mv3", nc.vector.copy_predicated(wish[:], flip[:, 2, :], gap[:]))
                    st.after("mv3")
                    st.did("thr", nc.vector.tensor_tensor(thr[:], wish[:], nthr[:, 2, :], ALU.subtract))
                return st

            v.drain()
            nc.vector.tensor_scalar(push[:], m.ident[:], -BIG, None, ALU.mult)
            nc.vector.memset(flag_weights[:, ST:3 * ST], float(SERIOUS))
            for i in range(ST):
                nc.vector.memset(flag_weights[:, i:i + 1], 2.0 ** i)
            v.drain()
            for i in range(ST):
                copy_scores(0, 0, i)
            v.wait_ge(s["copied"], START + ST)
            negate_max(0, 0)
            base = slot(0, 0, START, prev=False, old=False).end()
            base = slot(1, 1, base, old=False).end()
            base = slot(2, 0, base, old=False).end()
            base = slot(3, 1, base).end()
            with v.Fori(2, BH // 2 - 1) as pair:
                even = slot(pair * 2, 0, pair * (2 * FULL_SLOT) + (base - 4 * FULL_SLOT))
                odd = slot(pair * 2 + 1, 1, pair * (2 * FULL_SLOT) + (base - 3 * FULL_SLOT))
                assert len(even.number) == len(odd.number) == FULL_SLOT
            base = base + (BH // 2 - 3) * 2 * FULL_SLOT
            base = slot(BH - 2, 0, base).end()
            base = slot(BH - 1, 1, base, nxt=False).end()
            base = slot(BH, 0, base, nxt=False, cur=False).end()
            base = slot(BH + 1, 1, base, prev=False, nxt=False, cur=False).end()
            slot(BH + 2, 0, base, prev=False, nxt=False, cur=False)


def project(nc, t, m, sems):
    w_loaded, turned, moved, made, added = (sems("pr_" + k) for k in ("w_loaded", "turned", "moved", "made", "added"))
    with ExitStack() as c:
        sb = lambda n, sh, dt=F32: c.enter_context(nc.sbuf_tensor(n, sh, dt))
        w = sb("w_out", [P, DC, D])
        bias = sb("b_out", [P, D])
        aT = sb("attnT", [P, 2, DC, P])
        flat = sb("attn_rows", [P, 2, D])
        psA = c.enter_context(nc.psum_tensor("psA_pr", [P, 2, 512], F32))
        psP = c.enter_context(nc.psum_tensor("psP_pr", [P, 2, 512], F32))
        rows, gathered = flat, sems("pr_rows")
        block = c.enter_context(nc.Block())

        @block.sync
        def _(sp):
            sp.dma_start(w[:], t["W_outT"].rearrange("(c p) e -> p c e", p=P)).then_inc(w_loaded, 16)
            sp.dma_start(bias[:], t["b_out"].to_broadcast((P, D))).then_inc(w_loaded, 16)

        @block.gpsimd
        def _(pool):
            for n in range(TILES):
                b, i = n // SEQ_TILES, n % SEQ_TILES
                if n >= 2:
                    pool.wait_ge(turned, n - 1)
                nc.gpsimd.tensor_copy(rows[:, n % 2, :].rearrange("p (h d) -> p h d", h=HEADS),
                                      m.heads_out[:, b * HEADS:(b + 1) * HEADS, i, :]).then_inc(gathered, 1)

        @block.tensor
        def _(pe):
            pe.wait_ge(w_loaded, 32)
            for n in range(TILES + 1):
                if n < TILES:
                    pe.wait_ge(gathered, n + 1)
                    if n >= 2:
                        pe.wait_ge(moved, n - 1)
                    for ch in range(DC):
                        tr = nc.tensor.transpose(psA[:, n % 2, ch * P:(ch + 1) * P], rows[:, n % 2, ch * P:(ch + 1) * P], m.ident[:])
                    tr.then_inc(turned, 1)
                n -= 1
                if n < 0:
                    continue
                if n >= 2:
                    pe.wait_ge(added, n - 1)
                pe.wait_ge(moved, n + 1)
                for ch in range(DC):
                    mm = nc.tensor.matmul(psP[:, n % 2, 0:D], aT[:, n % 2, ch, :], w[:, ch, :], start=(ch == 0), stop=(ch == DC - 1))
                mm.then_inc(made, 1)

        @block.scalar
        def _(act):
            for n in range(TILES):
                act.wait_ge(turned, n + 1)
                if n >= 2:
                    act.wait_ge(made, n - 1)
                nc.scalar.copy(aT[:, n % 2, :, :], psA[:, n % 2, 0:D].rearrange("p (c n) -> p c n", c=DC)).then_inc(moved, 1)

        @block.vector
        def _(v):
            v.wait_ge(w_loaded, 32)
            for n in range(TILES):
                nc.vector.tensor_tensor(m.resid[:, n, :], m.resid[:, n, :], bias[:], ALU.add)
                v.drain()
                v.wait_ge(made, n + 1)
                nc.vector.tensor_tensor(m.resid[:, n, :], psP[:, n % 2, 0:D], m.resid[:, n, :], ALU.add).then_inc(added, 1)
                if n:
                    v.wait_ge(added, n)
                    moments(nc, m, n - 1, m.resid)
            v.wait_ge(added, TILES)
            moments(nc, m, TILES - 1, m.resid)


def top_k_mask(nc, v, act_exp, logits, bias, n, top, work):
    p = work.probs[:, :, 0:n]
    one = lambda ap: ap.rearrange("p (t o) -> p t o", o=1).to_broadcast((P, TILES, n))
    nc.vector.tensor_tensor(p, logits, bias.rearrange("p (o e) -> p o e", o=1).to_broadcast((P, TILES, n)), ALU.add)
    nc.vector.memset(work.probs[:, :, n:n + 8], -2.0)
    v.drain()
    nc.vector.tensor_reduce(work.row[:], p, AX.X, ALU.max)
    v.drain()
    nc.vector.tensor_tensor(p, p, one(work.row[:]), ALU.subtract)
    act_exp()
    nc.vector.tensor_reduce(work.row[:], p, AX.X, ALU.add)
    v.drain()
    nc.vector.reciprocal(work.row[:], work.row[:])
    v.drain()
    nc.vector.tensor_tensor(p, p, one(work.row[:]), ALU.mult)
    v.drain()
    for i in range(TILES):
        nc.vector.max(work.best[:, i, :], work.probs[:, i, 0:n])
    v.drain()
    nc.vector.memset(work.best[:, :, top:8], -2.0)
    v.drain()
    for i in range(TILES):
        nc.vector.match_replace(work.found[:, i, :], work.best[:, i, :], work.probs[:, i, :], -1.0)
    v.drain()


class RouteWork:

    def __init__(self, sb, tag, n):
        self.probs = sb("probs" + tag, [P, TILES, n + 8])
        self.found = sb("found" + tag, [P, TILES, n + 8])
        self.best = sb("best" + tag, [P, TILES, 8])
        self.row = sb("row" + tag, [P, TILES])


PHM_NAMES = "qkvo"


def load_phm(sp, t, m, A, S):
    s = m.sem["cos"]
    for x, name in enumerate(PHM_NAMES):
        for half in range(2):
            sp.dma_start(A[half * 64:(half + 1) * 64, x, :, :, :],
                         t["A_" + name][half:half + 1].to_broadcast((64, PHM * DC * PHM)).rearrange("p (n c j) -> p n c j", n=PHM, c=DC)).then_inc(s["loaded"], 16)
            sp.dma_start(S[half * 64:(half + 1) * 64, x, :, :], t["S_" + name].rearrange("n k l -> k n l")).then_inc(s["loaded"], 16)
        sp.dma_start(m.phm_bias[:, x, :], t["bias_" + name]).then_inc(s["loaded"], 16)
    for x, name in enumerate(("g1", "b1", "g2", "b2")):
        sp.dma_start(m.ln_gains[:, x, :], t[name].to_broadcast((P, D))).then_inc(s["loaded"], 16)
    sp.wait_ge(s["loaded"], START + 16 * (4 * 5 + 4))


def build_phm(nc, pool, m, A, S, prod):
    s = m.sem["cos"]
    pool.wait_ge(s["loaded"], START + 16 * (4 * 5 + 4))
    L = D // PHM
    for n in range(PHM):
        for x in range(4):
            dst = m.W_phm[:, x, :, :] if n == 0 else prod[:, x, :]
            dst = dst.rearrange("p c (j l) -> p (c j) l", l=L) if n == 0 else dst.rearrange("p (a l) -> p a l", l=L)
            nc.gpsimd.tensor_tensor(dst, S[:, x, n:n + 1, :].to_broadcast((P, DC * PHM, L)),
                                    A[:, x, n, :, :].rearrange("p c (j o) -> p (c j) o", o=1).to_broadcast((P, DC * PHM, L)), ALU.mult)
        pool.drain()
        if n:
            for x in range(4):
                nc.gpsimd.tensor_tensor(m.W_phm[:, x, :, :], m.W_phm[:, x, :, :], prod[:, x, :].rearrange("p (c e) -> p c e", c=DC), ALU.add)
            pool.drain()


def moe(nc, t, m, sems):
    s = m.sem["moe"]
    ALL = EXPERTS + 1
    HC = EH // P
    CH = BATCH
    with ExitStack() as c:
        sb = lambda n, sh, dt=F32: c.enter_context(nc.sbuf_tensor(n, sh, dt))
        w1 = sb("w1", [P, 2, DC, EH])
        w2 = sb("w2", [P, 2, HC, D])
        b1 = sb("b1", [P, ALL * HC])
        b1_now = sb("b1_now", [P, HC])
        rw = sb("router_w", [P, DC, EXPERTS])
        rb = sb("router_b", [P, EXPERTS])
        b2 = sb("b2", [ALL, D])
        work = RouteWork(sb, "_moe", EXPERTS)
        wt = sb("expert_weights", [P, TILES, ALL])
        wT = sb("weightsT", [ALL, 2, SEQ])
        phm_A = sb("phm_A", [P, 4, PHM, DC, PHM])
        phm_S = sb("phm_S", [P, 4, PHM, D // PHM])
        phm_prod = sb("phm_prod", [P, 4, DC * D])
        H = sb("hidden", [P, 2, HC, SEQ])
        psH = c.enter_context(nc.psum_tensor("psH_moe", [P, HC, 512], F32))
        psY = c.enter_context(nc.psum_tensor("psY_moe", [P, 4, 512], F32))
        bias_bank = lambda i: psH[:, i % 4, 0:D]

        with nc.Block() as block:
            @block.sync
            def _(sp):
                for dst, src in ((rw[:], t["router_w"].rearrange("(c p) e -> p c e", p=P)), (rb[:], t["router_b"].to_broadcast((P, EXPERTS))),
                                 (b2[0:1, :], t["sb2"]), (b2[1:ALL, :], t["rb2"]), (b1[:], t["b1_all"])):
                    sp.dma_start(dst, src).then_inc(s["small"], 16)

            @block.tensor
            def _(pe):
                pe.wait_ge(s["small"], START + 16 * 5)
                for i in range(TILES):
                    for ch in range(DC):
                        mm = nc.tensor.matmul(psH[:, 0, i * EXPERTS:(i + 1) * EXPERTS], m.xT[:, ch, i * P:(i + 1) * P], rw[:, ch, :],
                                              start=(ch == 0), stop=(ch == DC - 1), skip_group_check=True)
                mm.then_inc(s["logits"], 1)
                pe.wait_ge(s["weights"], START + 1)
                for g in range(BATCH + 1):
                    if g < BATCH:
                        if g >= 2:
                            pe.wait_ge(s["wT_kept"], START + g - 1)
                        for j in range(SEQ_TILES):
                            tr = nc.tensor.transpose(psY[0:ALL, g % 2, j * P:(j + 1) * P], wt[:, g * SEQ_TILES + j, :], m.ident[:])
                        tr.then_inc(s["wT_made"], 1)
                    if g >= 1:
                        pe.wait_ge(s["wT_kept"], START + g)
                        for j in range(SEQ_TILES):
                            i = (g - 1) * SEQ_TILES + j
                            if i >= 4:
                                pe.wait_ge(s["bias_added"], START + i - 3)
                            nc.tensor.matmul(bias_bank(i), wT[:, (g - 1) % 2, j * P:(j + 1) * P], b2[:],
                                             start=True, stop=True).then_inc(s["bias_made"], 1)

            @block.scalar
            def _(act):
                act.wait_ge(s["shifted"], START + 1)
                nc.scalar.activation(work.probs[:, :, 0:EXPERTS], work.probs[:, :, 0:EXPERTS], ACT.Exp).then_inc(s["exped"], 1)
                for g in range(BATCH):
                    act.wait_ge(s["wT_made"], START + g + 1)
                    if g >= 2:
                        act.wait_ge(s["bias_made"], START + SEQ_TILES * (g - 1))
                    nc.scalar.copy(wT[:, g % 2, :], psY[0:ALL, g % 2, :]).then_inc(s["wT_kept"], 1)

            @block.vector
            def _(v):
                def exp_on_scalar():
                    v.drain().then_inc(s["shifted"], 1)
                    v.wait_ge(s["exped"], START + 1)
                v.wait_ge(s["logits"], START + 1)
                top_k_mask(nc, v, exp_on_scalar, psH[:, 0, 0:TILES * EXPERTS].rearrange("p (t e) -> p t e", e=EXPERTS), rb[:], EXPERTS, TOP_E, work)
                nc.vector.memset(wt[:, :, 0:1], 1.0)
                nc.vector.scalar_tensor_tensor(wt[:, :, 1:ALL], work.found[:, :, 0:EXPERTS], -0.5, work.probs[:, :, 0:EXPERTS], ALU.is_lt, ALU.mult)
                v.drain().then_inc(s["weights"], 1)
                for i in range(TILES):
                    v.wait_ge(s["bias_made"], START + i + 1)
                    nc.vector.tensor_tensor(m.resid[:, i, :], bias_bank(i), m.resid[:, i, :], ALU.add).then_inc(s["bias_added"], 1)

        with nc.Block() as block:
            @block.sync
            def _(sp):
                def load(e, r):
                    sp.dma_start(w1[:, r, :, :], t["w1_all"][bass.ds(e, 1)].rearrange("o (c p) n -> p (o c) n", p=P)).then_inc(s[f"w_loaded{r}"], 16)
                    sp.dma_start(w2[:, r, :, :], t["w2_all"][bass.ds(e, 1)].rearrange("o (c p) n -> p (o c) n", p=P)).then_inc(s[f"w_loaded{r}"], 16)
                load(0, 0)
                load(1, 1)
                load_phm(sp, t, m, phm_A, phm_S)
                with sp.Fori(1, ALL // 2) as pair:
                    e = pair * 2
                    for r in range(2):
                        sp.wait_ge(s["made"], START + SEQ_TILES * CH * (e + (r - 1)))
                        load(e + r, r)
                sp.wait_ge(s["made"], START + SEQ_TILES * CH * (ALL - 2))
                load(ALL - 1, 0)

            @block.tensor
            def _(pe):
                def hidden(e, r, n):
                    g = e * CH + n
                    for hc in range(HC):
                        pe.wait_ge(s["active"], START + HC * g + (hc + 1))
                        for ch in range(DC):
                            mm = nc.tensor.matmul(psH[:, hc, :], w1[:, r, ch, hc * P:(hc + 1) * P], m.xT[:, ch, n * SEQ:(n + 1) * SEQ],
                                                  start=(ch == 0), stop=(ch == DC - 1))
                        mm.then_inc(s["hidden"], 1)

                def output(e, r, n):
                    g = e * CH + n
                    pe.wait_ge(s["active"], START + HC * (g + 2))
                    for i in range(SEQ_TILES):
                        pe.wait_ge(s["y_free"], START + SEQ_TILES * g + (i // 2 * 2 + 2))
                        for hc in range(HC):
                            mm = nc.tensor.matmul(psY[:, 2 * (n % 2) + i // 2, (i % 2) * D:(i % 2 + 1) * D],
                                                  H[:, n % 2, hc, i * P:(i + 1) * P], w2[:, r, hc, :],
                                                  start=(hc == 0), stop=(hc == HC - 1), skip_group_check=True)
                        mm.then_inc(s["made"], 1)

                def expert(e, r, last=False):
                    for n in range(CH):
                        if n < CH - 1:
                            hidden(e, r, n + 1)
                        elif not last:
                            pe.wait_ge(s[f"w_loaded{1 - r}"], START + e * 16 + (48 if r else 32))
                            hidden(e + 1, 1 - r, 0)
                        output(e, r, n)

                pe.wait_ge(s["w_loaded0"], START + 32)
                hidden(0, 0, 0)
                with pe.Fori(0, ALL // 2) as pair:
                    e = pair * 2
                    expert(e, 0)
                    expert(e + 1, 1)
                expert(ALL - 1, 0, last=True)

            @block.gpsimd
            def _(pool):
                build_phm(nc, pool, m, phm_A, phm_S, phm_prod)

            @block.scalar
            def _(act):
                act.drain().then_inc(s["active"], HC)
                with act.Fori(0, ALL) as e:
                    act.drain()
                    nc.scalar.copy(b1_now[:], b1[:, bass.ds(e * HC, HC)])
                    act.drain()
                    for n in range(CH):
                        g = e * CH + n
                        act.wait_ge(s["h_unused"], START + g + 1)
                        for hc in range(HC):
                            act.wait_ge(s["hidden"], START + HC * g + (hc + 1))
                            nc.scalar.activation(H[:, n % 2, hc, :], psH[:, hc, :], ACT.Gelu, bias=b1_now[:, hc:hc + 1]).then_inc(s["active"], 1)

            @block.vector
            def _(v):
                v.drain().then_inc(s["y_free"], 2 * SEQ_TILES)
                v.drain().then_inc(s["h_unused"], 2)
                def add_expert(e, last=False):
                    for n in range(CH):
                        g = e * CH + n
                        for i in range(SEQ_TILES):
                            v.wait_ge(s["made"], START + SEQ_TILES * g + (i // 2 * 2 + 2))
                            T = n * SEQ_TILES + i
                            v.wait_ge(s["y_free"], START + SEQ_TILES * g)
                            weight = wt[:, T, bass.ds(e, 1)]
                            nc.vector.scalar_tensor_tensor(m.resid[:, T, :], psY[:, 2 * (n % 2) + i // 2, (i % 2) * D:(i % 2 + 1) * D],
                                                           weight, m.resid[:, T, :], ALU.mult, ALU.add).then_inc(s["y_free"], 1)
                        v.drain().then_inc(s["h_unused"], 1)
                        if last:
                            for T in range(n * SEQ_TILES, (n + 1) * SEQ_TILES):
                                moments(nc, m, T, m.resid)

                with v.Fori(0, ALL - 1) as e:
                    add_expert(e)
                add_expert(ALL - 1, last=True)


def cos_attention(nc, t, m, sems):
    s = m.sem["cos"]
    with ExitStack() as c:
        sb = lambda n, sh, dt=F32: c.enter_context(nc.sbuf_tensor(n, sh, dt))
        W, bias, gains = m.W_phm, m.phm_bias, m.ln_gains
        rows = sb("query", [P, TILES, D])
        qnT = sb("qnT", [P, DC, TOKENS])

        norm_turn(nc, m, sems, "_query", m.resid, rows, m.xT, leave_moments=True)
        norm_turn(nc, m, sems, "_qn", rows, rows, qnT, gains[:, 0, :], gains[:, 1, :])

        with ExitStack() as c2:
            sb2 = lambda n, sh, dt=F32: c2.enter_context(nc.sbuf_tensor(n, sh, dt))
            Q, V = (sb2(n, [P, BATCH, D]) for n in ("cos_q", "cos_v"))
            K = sb2("cos_k", [P, 2, BATCH, D])
            prod = sb2("cos_prod", [P, BATCH, D])
            mix = sb2("cos_mix", [P, 2, BATCH, D])
            cosines = sb2("cosines", [P, BATCH, BATCH])
            a = sb2("cos_a", [P, 2, BATCH * HEADS])
            den = sb2("cos_den", [P, HEADS])
            psQK = c2.enter_context(nc.psum_tensor("psQK_cos", [P, 4, 512], F32))
            psV = c2.enter_context(nc.psum_tensor("psV_cos", [P, 2, 512], F32))
            psSum = c2.enter_context(nc.psum_tensor("psSum_cos", [P, 2, 512], F32))
            block = c2.enter_context(nc.Block())

            @block.sync
            def _(sp):
                sp.dma_start(cosines[:].rearrange("p a b -> p (a b)"), t["cosines"].to_broadcast((P, BATCH * BATCH))).then_inc(s["norm"], 16)

            @block.tensor
            def _(pe):
                def projection(x, out, src, n):
                    it, l = n // BATCH, n % BATCH
                    for ch in range(DC):
                        nc.tensor.matmul(out, src[:, ch, bass.ds(l * SEQ + it * P, P)], W[:, x, ch, :], start=(ch == 0), stop=False)
                    return nc.tensor.matmul(out, m.ones[0:1, :], bias[:, x, :], start=False, stop=True)

                def queries_keys(n):
                    if n >= 2:
                        pe.wait_ge(s["kept"], START + 2 * (n - 1))
                    projection(0, psQK[:, 2 * (n % 2), 0:D], qnT, n)
                    projection(1, psQK[:, 2 * (n % 2) + 1, 0:D], m.xT, n).then_inc(s["made"], 1)

                for n in range(BATCH):
                    queries_keys(n)
                for it in range(SEQ_TILES):
                    for n in range(it * BATCH, (it + 1) * BATCH):
                        if n >= 2:
                            pe.wait_ge(s["v_kept"], START + n - 1)
                        projection(2, psV[:, n % 2, 0:D], m.xT, n).then_inc(s["v_made"], 1)
                    for n in range(it * BATCH, (it + 1) * BATCH):
                        if it < SEQ_TILES - 1:
                            queries_keys(n + BATCH)
                        pe.wait_ge(s["mixed"], START + n + 1)
                        if n >= 2:
                            pe.wait_ge(s["summed"], START + n - 1)
                        for partner in range(BATCH):
                            mm = nc.tensor.matmul(psSum[:, n % 2, 0:D], m.ident[:], mix[:, n % 2, partner, :],
                                                  start=(partner == 0), stop=(partner == BATCH - 1))
                        mm.then_inc(s["sum_made"], 1)

            @block.scalar
            def _(act):
                def keep_queries_keys(n):
                    it, l = n // BATCH, n % BATCH
                    if it:
                        act.wait_ge(s["scored"], START + n - BATCH + 1)
                    act.wait_ge(s["made"], START + n + 1)
                    for x, dst in ((0, Q[:, l, :]), (1, K[:, it % 2, l, :])):
                        nc.scalar.activation(dst, psQK[:, 2 * (n % 2) + x, 0:D], ACT.Relu).then_inc(s["kept"], 1)

                for n in range(BATCH):
                    keep_queries_keys(n)
                for it in range(SEQ_TILES):
                    if it:
                        act.wait_ge(s["mixed"], START + BATCH * it)
                    for n in range(it * BATCH, (it + 1) * BATCH):
                        act.wait_ge(s["v_made"], START + n + 1)
                        nc.scalar.copy(V[:, n % BATCH, :], psV[:, n % 2, 0:D]).then_inc(s["v_kept"], 1)
                    if it < SEQ_TILES - 1:
                        for n in range((it + 1) * BATCH, (it + 2) * BATCH):
                            keep_queries_keys(n)

            @block.gpsimd
            def _(pool):
                with pool.Fori(0, SEQ_TILES) as it:
                    pool.wait_ge(s["v_kept"], START + BATCH * (it + 1))
                    for l in range(BATCH):
                        pool.wait_ge(s["scored"], START + it * BATCH + (l + 1))
                        if l >= 2:
                            pool.wait_ge(s["sum_made"], START + it * BATCH + (l - 1))
                        else:
                            pool.wait_ge(s["sum_made"], START + it * BATCH)
                        nc.gpsimd.tensor_tensor(mix[:, l % 2, :, :].rearrange("p l (h d) -> p (l h) d", d=HD),
                                                V[:].rearrange("p l (h d) -> p (l h) d", d=HD),
                                                a[:, l % 2, :].rearrange("p (x o) -> p x o", o=1).to_broadcast((P, BATCH * HEADS, HD)),
                                                ALU.mult).then_inc(s["mixed"], 1)

            @block.vector
            def _(v):
                v.wait_ge(s["norm"], START + 16)

                def score(it, k, l):
                    al = a[:, l % 2, :]
                    nc.vector.tensor_tensor(prod[:], Q[:, l:l + 1, :].to_broadcast((P, BATCH, D)), K[:, k, :, :], ALU.mult)
                    v.drain()
                    v.wait_ge(s["mixed"], START + it * BATCH + max(l - 1, 0))
                    nc.vector.tensor_reduce(al, prod[:].rearrange("p l (h d) -> p (l h) d", d=HD), AX.X, ALU.add)
                    v.drain()
                    al3 = al.rearrange("p (l h) -> p l h", h=HEADS)
                    nc.vector.tensor_tensor(al3, al3, cosines[:, l, :].rearrange("p (l o) -> p l o", o=1).to_broadcast((P, BATCH, HEADS)), ALU.mult)
                    v.drain()
                    nc.vector.tensor_reduce(den[:], al.rearrange("p (l h) -> p h l", h=HEADS), AX.X, ALU.add)
                    v.drain()
                    nc.vector.tensor_scalar(den[:], den[:], 1e-6, None, ALU.max)
                    v.drain()
                    nc.vector.reciprocal(den[:], den[:])
                    v.drain()
                    nc.vector.tensor_tensor(al3, al3, den[:].rearrange("p (o h) -> p o h", o=1).to_broadcast((P, BATCH, HEADS)),
                                            ALU.mult).then_inc(s["scored"], 1)

                def collect(it, l):
                    v.wait_ge(s["sum_made"], START + it * BATCH + (l + 1))
                    row = rows[:, bass.ds(l * SEQ_TILES + it, 1), :].rearrange("p o d -> p (o d)")
                    nc.vector.tensor_tensor(row, row, psSum[:, l % 2, 0:D], ALU.add).then_inc(s["summed"], 1)

                with v.Fori(0, SEQ_TILES // 2) as pair:
                    for k in range(2):
                        it = pair * 2 + k
                        v.wait_ge(s["kept"], START + 2 * BATCH * (it + 1))
                        for l in range(BATCH):
                            score(it, k, l)
                            if l >= 3:
                                moments(nc, m, (l - 3) * SEQ_TILES + it, rows)
                            if l >= 2:
                                collect(it, l - 2)
                        collect(it, BATCH - 2)
                        collect(it, BATCH - 1)
                        v.drain()
                        for l in range(BATCH - 3, BATCH):
                            moments(nc, m, l * SEQ_TILES + it, rows)

        norm_turn(nc, m, sems, "_out", rows, rows, qnT, gains[:, 2, :], gains[:, 3, :])

        with ExitStack() as c2:
            psO = c2.enter_context(nc.psum_tensor("psO_cos", [P, 4, 512], F32))
            block = c2.enter_context(nc.Block())

            @block.tensor
            def _(pe):
                for i in range(TILES):
                    if i >= 4:
                        pe.wait_ge(s["oadded"], START + i - 3)
                    for ch in range(DC):
                        nc.tensor.matmul(psO[:, i % 4, 0:D], qnT[:, ch, i * P:(i + 1) * P], W[:, 3, ch, :], start=(ch == 0), stop=False)
                    nc.tensor.matmul(psO[:, i % 4, 0:D], m.ones[0:1, :], bias[:, 3, :], start=False, stop=True).then_inc(s["omade"], 1)

            @block.vector
            def _(v):
                for i in range(TILES):
                    nc.vector.tensor_tensor(m.resid[:, i, :], m.resid[:, i, :], rows[:, i, :], ALU.add).then_inc(s["rows_added"], 1)
                    v.wait_ge(s["rows_added"], START + i + 1)
                    v.wait_ge(s["omade"], START + i + 1)
                    nc.vector.tensor_tensor(m.resid[:, i, :], psO[:, i % 4, 0:D], m.resid[:, i, :], ALU.add).then_inc(s["oadded"], 1)
                    if i:
                        v.wait_ge(s["oadded"], START + i)
                        moments(nc, m, i - 1, m.resid)
                v.wait_ge(s["oadded"], START + TILES)
                moments(nc, m, TILES - 1, m.resid)


def block_ffn(nc, t, m, sems, out):
    s = m.sem["ffn"]
    MC = OUTF // P
    with ExitStack() as c:
        sb = lambda n, sh, dt=F32: c.enter_context(nc.sbuf_tensor(n, sh, dt))
        w1 = sb("ffn_w1", [P, DC, OUTF])
        w2 = sb("ffn_w2", [P, MC, D])
        b1 = sb("ffn_b1", [P, MC])
        b2 = sb("ffn_b2", [1, D])
        rw = sb("ffn_rw", [P, DC, BLOCKS])
        rb = sb("ffn_rb", [P, BLOCKS])
        spread = sb("ffn_spread", [BLOCKS, MC, P], BF16)
        spread32 = sb("ffn_spread32", [BLOCKS, MC * P])
        maskT = sb("maskT", [BLOCKS, TOKENS], BF16)
        work = RouteWork(sb, "_ffn", BLOCKS)
        chosen = sb("chosen", [P, TILES, BLOCKS])
        H = sb("ffn_hidden", [P, 2, MC, SEQ])
        psH = c.enter_context(nc.psum_tensor("psH_ffn", [P, 2, 512], F32))
        psM = c.enter_context(nc.psum_tensor("psM_ffn", [P, 2, 512], F32))
        psY = c.enter_context(nc.psum_tensor("psY_ffn", [P, 4, 512], F32))
        out_tiles = out.rearrange("(n p) d -> p n d", p=P)

        with nc.Block() as block:
            @block.sync
            def _(sp):
                for dst, src in ((rw[:], t["ffn_rwT"].rearrange("(c p) e -> p c e", p=P)), (rb[:], t["ffn_rb"].to_broadcast((P, BLOCKS))),
                                 (b1[:], t["ffn_b1"]), (b2[:], t["ffn_b2"]), (spread32[:], t["spread"])):
                    sp.dma_start(dst, src).then_inc(s["small"], 16)
                sp.dma_start(w1[:], t["ffn_w1T"].rearrange("(c p) e -> p c e", p=P)).then_inc(s["w_loaded"], 16)
                sp.dma_start(w2[:], t["ffn_w2T"].rearrange("(c p) e -> p c e", p=P)).then_inc(s["w_loaded"], 16)

            @block.tensor
            def _(pe):
                pe.wait_ge(s["small"], START + 16 * 5)
                for i in range(TILES):
                    for ch in range(DC):
                        mm = nc.tensor.matmul(psH[:, 0, i * BLOCKS:(i + 1) * BLOCKS], m.xT[:, ch, i * P:(i + 1) * P], rw[:, ch, :],
                                              start=(ch == 0), stop=(ch == DC - 1), skip_group_check=True)
                mm.then_inc(s["logits"], 1)
                pe.wait_ge(s["mask"], START + 1)
                for g in range(BATCH):
                    if g >= 2:
                        pe.wait_ge(s["mT_kept"], START + g - 1)
                    for j in range(SEQ_TILES):
                        tr = nc.tensor.transpose(psM[0:BLOCKS, g % 2, j * P:(j + 1) * P], chosen[:, SEQ_TILES * g + j, :], m.ident[:])
                    tr.then_inc(s["mT_made"], 1)

            @block.scalar
            def _(act):
                act.wait_ge(s["shifted"], START + 1)
                nc.scalar.activation(work.probs[:, :, 0:BLOCKS], work.probs[:, :, 0:BLOCKS], ACT.Exp).then_inc(s["exped"], 1)
                for g in range(BATCH):
                    act.wait_ge(s["mT_made"], START + g + 1)
                    nc.scalar.copy(maskT[:, g * SEQ:(g + 1) * SEQ], psM[0:BLOCKS, g % 2, :]).then_inc(s["mT_kept"], 1)

            @block.vector
            def _(v):
                def exp_on_scalar():
                    v.drain().then_inc(s["shifted"], 1)
                    v.wait_ge(s["exped"], START + 1)
                v.wait_ge(s["small"], START + 16 * 5)
                nc.vector.tensor_copy(spread[:].rearrange("b m p -> b (m p)"), spread32[:])
                v.wait_ge(s["logits"], START + 1)
                top_k_mask(nc, v, exp_on_scalar, psH[:, 0, :].rearrange("p (t e) -> p t e", e=BLOCKS), rb[:], BLOCKS, TOP_B, work)
                nc.vector.tensor_scalar(chosen[:], work.found[:, :, 0:BLOCKS], -0.5, None, ALU.is_lt)
                v.drain().then_inc(s["mask"], 1)

        with nc.Block() as block:
            @block.tensor
            def _(pe):
                def hidden(n):
                    for mc in range(MC):
                        k = n * MC + mc
                        if not (isinstance(n, int) and n == 0 and mc < 2):
                            pe.wait_ge(s["masked"], START + k - 1)
                        for ch in range(DC):
                            mm = nc.tensor.matmul(psH[:, mc % 2, :], w1[:, ch, mc * P:(mc + 1) * P], m.xT[:, ch, bass.ds(n * SEQ, SEQ)],
                                                  start=(ch == 0), stop=(ch == DC - 1))
                        mm.then_inc(s["hidden"], 1)
                        nc.tensor.matmul(psM[:, mc % 2, :], spread[:, mc, :], maskT[:, bass.ds(n * SEQ, SEQ)], start=True, stop=True).then_inc(s["spread"], 1)

                def output(n, par):
                    pe.wait_ge(s["masked"], START + (n + 1) * MC)
                    for i in range(SEQ_TILES):
                        if not (isinstance(n, int) and n == 0):
                            pe.wait_ge(s["added"], START + SEQ_TILES * (n - 1) + (i + 1))
                        for mc in range(MC):
                            nc.tensor.matmul(psY[:, i, 0:D], H[:, par, mc, i * P:(i + 1) * P], w2[:, mc, :], start=(mc == 0), stop=False)
                        nc.tensor.matmul(psY[:, i, 0:D], m.ones[0:1, :], b2[:], start=False, stop=True).then_inc(s["made"], 1)

                pe.wait_ge(s["w_loaded"], START + 32)
                hidden(0)
                hidden(1)
                output(0, 0)
                with pe.Fori(0, BATCH // 2 - 1) as pair:
                    n = pair * 2 + 1
                    hidden(n + 1)
                    output(n, 1)
                    hidden(n + 2)
                    output(n + 1, 0)
                output(BATCH - 1, 1)

            @block.scalar
            def _(act):
                with act.Fori(0, BATCH // 2) as pair:
                    n0 = pair * 2
                    for k in range(2):
                        n = n0 + k
                        for mc in range(MC):
                            act.wait_ge(s["hidden"], START + n * MC + (mc + 1))
                            if mc == 0:
                                act.wait_ge(s["h_unused"], START + n + 1)
                            nc.scalar.activation(H[:, k, mc, :], psH[:, mc % 2, :], ACT.Relu, bias=b1[:, mc:mc + 1]).then_inc(s["relu"], 1)

            @block.vector
            def _(v):
                def mask_hidden(n, k):
                    for mc in range(MC):
                        v.wait_ge(s["relu"], START + n * MC + (mc + 1))
                        v.wait_ge(s["spread"], START + n * MC + (mc + 1))
                        nc.vector.tensor_tensor(H[:, k, mc, :], psM[:, mc % 2, :], H[:, k, mc, :], ALU.mult).then_inc(s["masked"], 1)

                def add_output(n):
                    for i in range(SEQ_TILES):
                        v.wait_ge(s["made"], START + SEQ_TILES * n + (i + 1))
                        row = m.resid[:, bass.ds(n * SEQ_TILES + i, 1), :].rearrange("p o d -> p (o d)")
                        nc.vector.tensor_tensor(row, psY[:, i, 0:D], row, ALU.add).then_inc(s["added"], 1)
                    v.drain().then_inc(s["h_unused"], 1)

                v.drain().then_inc(s["h_unused"], 2)
                mask_hidden(0, 0)
                with v.Fori(0, BATCH // 2 - 1) as pair:
                    n = pair * 2
                    mask_hidden(n + 1, 1)
                    add_output(n)
                    mask_hidden(n + 2, 0)
                    add_output(n + 1)
                mask_hidden(BATCH - 1, 1)
                add_output(BATCH - 2)
                add_output(BATCH - 1)

            @block.sync
            def _(sp):
                with sp.Fori(0, BATCH) as n:
                    sp.wait_ge(s["added"], START + SEQ_TILES * (n + 1))
                    sp.dma_start(out_tiles[:, bass.ds(n * SEQ_TILES, SEQ_TILES), :], m.resid[:, bass.ds(n * SEQ_TILES, SEQ_TILES), :]).then_inc(s["stored"], 16)
                sp.wait_ge(s["stored"], START + 16 * BATCH)


class Memory:
    pass


def lm_tower(nc, t, out, stop=None):
    m = Memory()
    m.parts_dram = [nc.dram_tensor(n, (BATCH, 3, D, SEQ), BF16, kind="Internal").ap() for n in ("q_parts", "k_parts")]
    out = out.rearrange("b s d -> (b s) d")

    def dump(sems):
        with nc.Block() as block:
            @block.sync
            def _(sp):
                d = sems("dumped")
                sp.dma_start(out.rearrange("(n p) d -> p n d", p=P), m.resid[:]).then_inc(d, 16)
                sp.wait_ge(d, 16)

    with ExitStack() as c:
        sems = lambda n: c.enter_context(nc.semaphore(n))
        sb = lambda st, n, sh, dt=F32: st.enter_context(nc.sbuf_tensor(n, sh, dt))
        m.sem = {stage: {n: sems(f"{stage}_{n}") for n in names} for stage, names in STAGE_SEMAPHORES.items()}
        m.ident = sb(c, "ident", [P, P])
        m.ids = sb(c, "ids", [P, TILES], I32)
        m.s_col = sb(c, "s_col", [RANK, 1])
        m.vt = sb(c, "vt", [RANK, D])
        m.qk_bias = sb(c, "qk_bias", [P, 2 * DC])
        m.half_mask = sb(c, "half_mask", [P, HALF])
        m.rank8 = sb(c, "rank8", [P, 8])
        m.eps = sb(c, "eps", [P, 1])
        m.moments = sb(c, "moments", [P, TILES, 6])
        m.ones = sb(c, "ones", [P, P])
        m.resid = sb(c, "resid", [P, TILES, D])
        load_constants(nc, t, m, sems)
        embed(nc, t, m, sems)
        if stop == "embed":
            return dump(sems)
        with ExitStack() as c0:
            m.v_aug = sb(c0, "v_aug", [P, BH, SEQ_TILES, HD + 1])
            m.thr0 = sb(c0, "thr0", [P, BH, SEQ_TILES])
            m.step = sb(c0, "step", [P, BH, SEQ_TILES])
            with ExitStack() as c1:
                m.xT = sb(c1, "xT", [P, DC, TOKENS])
                norm_turn(nc, m, sems, "_0", m.resid, None, m.xT)
                qkv(nc, t, m, sems)
            m.heads_out = sb(c0, "heads_out", [P, BH, SEQ_TILES, HD])
            attend(nc, t, m, sems)
            project(nc, t, m, sems)
        if stop == "attn":
            return dump(sems)
        m.xT = sb(c, "xT1", [P, DC, TOKENS])
        m.W_phm = sb(c, "W_phm", [P, 4, DC, D])
        m.phm_bias = sb(c, "phm_bias", [1, 4, D])
        m.ln_gains = sb(c, "ln_gains", [P, 4, D])
        norm_turn(nc, m, sems, "_1", m.resid, None, m.xT)
        moe(nc, t, m, sems)
        if stop == "moe":
            return dump(sems)
        cos_attention(nc, t, m, sems)
        if stop == "cos":
            return dump(sems)
        norm_turn(nc, m, sems, "_2", m.resid, None, m.xT)
        block_ffn(nc, t, m, sems, out)


def layouts(i):
    r = {}
    a = {k: np.asarray(v) for k, v in i.items()}
    r["ids"] = a["x"].reshape(TILES, P).T
    r["U"], r["s_col"], r["Vt"] = a["L0_tok_U"], a["L0_tok_s"].reshape(RANK, 1), a["L0_tok_Vt"]
    r["W_qkvT"] = a["L0_attn_W_qkv"].T
    r["qk_bias"] = a["L0_attn_b_qkv"][:2 * D].reshape(2 * DC, P).T
    r["v_bias"] = a["L0_attn_b_qkv"][2 * D:].reshape(1, D)
    r["W_outT"], r["b_out"] = a["L0_attn_W_out"].T, a["L0_attn_b_out"].reshape(1, D)
    r["router_w"], r["router_b"] = a["L0_ffn_router_w"], a["L0_ffn_router_b"].reshape(1, EXPERTS)
    r["w1_all"] = np.concatenate([a["L0_ffn_sw1"][None], a["L0_ffn_rw1"]])
    r["w2_all"] = np.concatenate([a["L0_ffn_sw2"][None], a["L0_ffn_rw2"]])
    r["b1_all"] = np.concatenate([a["L0_ffn_sb1"][None], a["L0_ffn_rb1"]]).reshape(-1, P).T
    r["sb2"], r["rb2"] = a["L0_ffn_sb2"].reshape(1, D), a["L0_ffn_rb2"]
    for x in "qkvo":
        r["A_" + x] = a[f"L1_attn_{x}A"].reshape(PHM, DC, 2, PHM).transpose(2, 0, 1, 3).reshape(2, -1)
        r["S_" + x], r["bias_" + x] = a[f"L1_attn_{x}S"], a[f"L1_attn_{x}b"].reshape(1, D)
    for x in ("g1", "b1", "g2", "b2"):
        r[x] = a["L1_attn_" + x].reshape(1, D)
    r["ffn_rwT"], r["ffn_rb"] = a["L1_ffn_router_w"].T, a["L1_ffn_router_b"].reshape(1, BLOCKS)
    r["ffn_w1T"], r["ffn_w2T"] = a["L1_ffn_w1"].T, a["L1_ffn_w2"].T
    r["ffn_b1"], r["ffn_b2"] = a["L1_ffn_b1"].reshape(-1, P).T, a["L1_ffn_b2"].reshape(1, D)
    r["ident"] = np.eye(P, dtype=np.float32)
    r["half_mask"] = np.repeat(np.eye(HALF, dtype=np.float32), HD, axis=0)
    r["rank8"] = np.arange(8, dtype=np.float32).reshape(1, 8)
    angle = (np.pi / 2) * np.arange(1, BATCH + 1) / BATCH
    r["cosines"] = np.cos(angle[:, None] - angle[None, :]).astype(np.float32).reshape(1, -1)
    r["spread"] = np.repeat(np.eye(BLOCKS, dtype=np.float32), BLOCK, axis=1)
    return {k: np.ascontiguousarray(v) for k, v in r.items()}


def kernel(**inputs):
    import concourse.bacc as bacc
    from concourse.bass_utils import run_bass_kernel_spmd

    nc = bacc.Bacc("TRN2", target_bir_lowering=False, num_devices=1)
    arrays = {f"in_{k}": v for k, v in layouts(inputs).items()}
    t = {k[3:]: nc.dram_tensor(k, v.shape, mybir.dt.from_np(v.dtype), kind="ExternalInput").ap() for k, v in arrays.items()}
    out = nc.dram_tensor("out_0", (BATCH, SEQ, D), F32, kind="ExternalOutput").ap()
    lm_tower(nc, t, out)
    r = run_bass_kernel_spmd(nc, [arrays], core_ids=[0])
    return r.results[0]["out_0"]
```
